# Optimizing a Trainium2 kernel written in Bass

```python
import numpy as np
import jax
import jax.numpy as jnp

def _softmax(x, axis=-1):
    return jax.nn.softmax(x, axis=axis)

def _gelu(x):
    return jax.nn.gelu(x, approximate=True)

def _silu(x):
    return jax.nn.silu(x)

def _sigmoid(x):
    return jax.nn.sigmoid(x)

def _layernorm(x, axis=-1, eps=1e-05):
    m = jnp.mean(x, axis=axis, keepdims=True)
    v = jnp.var(x, axis=axis, keepdims=True)
    return (x - m) / jnp.sqrt(v + eps)

def _scatter_add(tgt, idx, src, axis=0):
    return tgt.at[idx].add(src)

def _segment_sum(src, seg, n):
    return jax.ops.segment_sum(src, seg, n)
kernel_name = 'mk_seq_preln_d1_jaxref_r4_2655cb'

def setup_inputs(seed: int=0):
    np.random.seed(seed)
    _w = jnp.asarray

    def _L0_attn_setup():
        import jax, jax.numpy as jnp
        import numpy as np
        B_, L_, D_, N_ = (16, 256, 256, 8)

        def soft_clamp(x, mn, mx, sharp):
            c = (mx + mn) / 2.0
            r = (mx - mn) / 2.0
            xn = (x - c) / (r + 1e-08)
            return jnp.tanh(xn * sharp) / sharp * r + c

        def _forward(x, W_dt, b_dt, W_B, W_C, A_log, D_param):
            Bb, L, D = x.shape
            N = W_B.shape[0]
            dt = soft_clamp(jax.nn.softplus(jnp.einsum('bld,ed->ble', x, W_dt) + b_dt), 0.001, 0.1, 0.5)
            Bp = jnp.einsum('bld,nd->bln', x, W_B)
            Cp = jnp.einsum('bld,nd->bln', x, W_C)
            A = -jnp.exp(soft_clamp(A_log, -5.0, 5.0, 0.5))

            def step(h, inp):
                t, x_t, dt_t, B_t, C_t = inp
                dA = jnp.exp(soft_clamp(dt_t[:, :, None] * A[None], -8.0, 8.0, 0.5))
                h = h * dA + (dt_t * x_t)[:, :, None] * B_t[:, None, :]
                hnorm = jnp.sqrt(jnp.sum(h.astype(jnp.float32) ** 2, axis=(1, 2), keepdims=True))
                scale = jnp.minimum(20.0 / (hnorm + 1e-08), 1.0).astype(h.dtype)
                h = jnp.where(t % 10 == 0, h * scale, h)
                y = jnp.einsum('bdn,bn->bd', h, C_t) + D_param * x_t
                return (h, y)
            h0 = jnp.zeros((Bb, D, N), dtype=x.dtype)
            ts = jnp.arange(L)
            xs = (ts, jnp.swapaxes(x, 0, 1), jnp.swapaxes(dt, 0, 1), jnp.swapaxes(Bp, 0, 1), jnp.swapaxes(Cp, 0, 1))
            _, ys = jax.lax.scan(step, h0, xs)
            return jnp.swapaxes(ys, 0, 1)
        key = jax.random.key(seed)
        ks = jax.random.split(key, 6)
        x = jax.random.normal(ks[0], (B_, L_, D_), dtype=jnp.float32)
        W_dt = jax.random.normal(ks[1], (D_, D_), dtype=jnp.float32) * 0.02
        b_dt = jnp.full((D_,), -2.0, dtype=jnp.float32)
        W_B = jax.random.normal(ks[2], (N_, D_), dtype=jnp.float32) * (1.0 / np.sqrt(D_))
        W_C = jax.random.normal(ks[3], (N_, D_), dtype=jnp.float32) * (1.0 / np.sqrt(D_))
        A_log = jax.random.normal(ks[4], (D_, N_), dtype=jnp.float32) * 0.1
        D_param = jnp.full((D_,), 0.1, dtype=jnp.float32)
        return {'x': x, 'W_dt': W_dt, 'b_dt': b_dt, 'W_B': W_B, 'W_C': W_C, 'A_log': A_log, 'D_param': D_param}
    _L0_attn_in = _L0_attn_setup()

    def _L0_ffn_setup():
        import jax, jax.numpy as jnp
        import numpy as np
        S, B, D = (256, 2, 256)
        E, TOPK = (15, 3)
        F = 256
        FS = 512

        def _uinit(k, shape, out_dim):
            std = out_dim ** (-0.5)
            return jax.random.uniform(k, shape, jnp.float32, -std, std)
        key = jax.random.key(seed)
        ks = jax.random.split(key, 10)
        return {'x': jax.random.normal(ks[0], (S, B, D), jnp.float32), 'gate_w': jax.random.normal(ks[1], (E, D), jnp.float32) * D ** (-0.5), 'fc1_w': _uinit(ks[2], (E, 2 * F, D), 2 * F), 'fc1_b': _uinit(ks[3], (E, 2 * F), 2 * F), 'geglu_mult': jnp.ones((E, F), jnp.float32), 'fc2_w': _uinit(ks[4], (E, D, F), D), 'fc2_b': _uinit(ks[5], (E, D), D), 's_fc1_w': _uinit(ks[6], (2 * FS, D), 2 * FS), 's_fc1_b': _uinit(ks[7], (2 * FS,), 2 * FS), 's_geglu_mult': jnp.ones((FS,), jnp.float32), 's_fc2_w': _uinit(ks[8], (D, FS), D), 's_fc2_b': _uinit(ks[9], (D,), D)}
    _L0_ffn_in = _L0_ffn_setup()
    _d = {'L0_attn_x': _L0_attn_in['x'], 'L0_attn_W_dt': _L0_attn_in['W_dt'], 'L0_attn_b_dt': _L0_attn_in['b_dt'], 'L0_attn_W_B': _L0_attn_in['W_B'], 'L0_attn_W_C': _L0_attn_in['W_C'], 'L0_attn_A_log': _L0_attn_in['A_log'], 'L0_attn_D_param': _L0_attn_in['D_param'], 'L0_ffn_gate_w': _L0_ffn_in['gate_w'], 'L0_ffn_fc1_w': _L0_ffn_in['fc1_w'], 'L0_ffn_fc1_b': _L0_ffn_in['fc1_b'], 'L0_ffn_geglu_mult': _L0_ffn_in['geglu_mult'], 'L0_ffn_fc2_w': _L0_ffn_in['fc2_w'], 'L0_ffn_fc2_b': _L0_ffn_in['fc2_b'], 'L0_ffn_s_fc1_w': _L0_ffn_in['s_fc1_w'], 'L0_ffn_s_fc1_b': _L0_ffn_in['s_fc1_b'], 'L0_ffn_s_geglu_mult': _L0_ffn_in['s_geglu_mult'], 'L0_ffn_s_fc2_w': _L0_ffn_in['s_fc2_w'], 'L0_ffn_s_fc2_b': _L0_ffn_in['s_fc2_b']}
    _x0 = _d['L0_attn_x']
    _d['L0_attn_x'] = jax.random.normal(jax.random.fold_in(jax.random.key(seed), 1), (8, 1024, 256), dtype=_x0.dtype)
    del _x0
    return _d

def reference(L0_attn_x, L0_attn_W_dt, L0_attn_b_dt, L0_attn_W_B, L0_attn_W_C, L0_attn_A_log, L0_attn_D_param, L0_ffn_gate_w, L0_ffn_fc1_w, L0_ffn_fc1_b, L0_ffn_geglu_mult, L0_ffn_fc2_w, L0_ffn_fc2_b, L0_ffn_s_fc1_w, L0_ffn_s_fc1_b, L0_ffn_s_geglu_mult, L0_ffn_s_fc2_w, L0_ffn_s_fc2_b):

    def _L0_attn_ref(x, W_dt, b_dt, W_B, W_C, A_log, D_param):
        import jax, jax.numpy as jnp
        import numpy as np
        B_, L_, D_, N_ = (16, 256, 256, 8)

        def soft_clamp(x, mn, mx, sharp):
            c = (mx + mn) / 2.0
            r = (mx - mn) / 2.0
            xn = (x - c) / (r + 1e-08)
            return jnp.tanh(xn * sharp) / sharp * r + c

        def _forward(x, W_dt, b_dt, W_B, W_C, A_log, D_param):
            Bb, L, D = x.shape
            N = W_B.shape[0]
            dt = soft_clamp(jax.nn.softplus(jnp.einsum('bld,ed->ble', x, W_dt) + b_dt), 0.001, 0.1, 0.5)
            Bp = jnp.einsum('bld,nd->bln', x, W_B)
            Cp = jnp.einsum('bld,nd->bln', x, W_C)
            A = -jnp.exp(soft_clamp(A_log, -5.0, 5.0, 0.5))

            def step(h, inp):
                t, x_t, dt_t, B_t, C_t = inp
                dA = jnp.exp(soft_clamp(dt_t[:, :, None] * A[None], -8.0, 8.0, 0.5))
                h = h * dA + (dt_t * x_t)[:, :, None] * B_t[:, None, :]
                hnorm = jnp.sqrt(jnp.sum(h.astype(jnp.float32) ** 2, axis=(1, 2), keepdims=True))
                scale = jnp.minimum(20.0 / (hnorm + 1e-08), 1.0).astype(h.dtype)
                h = jnp.where(t % 10 == 0, h * scale, h)
                y = jnp.einsum('bdn,bn->bd', h, C_t) + D_param * x_t
                return (h, y)
            h0 = jnp.zeros((Bb, D, N), dtype=x.dtype)
            ts = jnp.arange(L)
            xs = (ts, jnp.swapaxes(x, 0, 1), jnp.swapaxes(dt, 0, 1), jnp.swapaxes(Bp, 0, 1), jnp.swapaxes(Cp, 0, 1))
            _, ys = jax.lax.scan(step, h0, xs)
            return jnp.swapaxes(ys, 0, 1)
        return _forward(x, W_dt, b_dt, W_B, W_C, A_log, D_param)

    def _L0_ffn_ref(x, gate_w, fc1_w, fc1_b, geglu_mult, fc2_w, fc2_b, s_fc1_w, s_fc1_b, s_geglu_mult, s_fc2_w, s_fc2_b):
        import jax, jax.numpy as jnp
        import numpy as np
        S, B, D = (256, 2, 256)
        E, TOPK = (15, 3)
        F = 256
        FS = 512

        def _uinit(k, shape, out_dim):
            std = out_dim ** (-0.5)
            return jax.random.uniform(k, shape, jnp.float32, -std, std)
        s, b, d = x.shape
        xt = x.reshape(-1, d)
        T = xt.shape[0]
        logits = xt @ gate_w.T
        scores = jax.nn.softmax(logits, axis=-1)
        topk_w, topk_idx = jax.lax.top_k(scores, TOPK)
        topk_w = topk_w / (jnp.sum(topk_w, axis=-1, keepdims=True) + 1e-20)
        comb = jnp.zeros((T, E), xt.dtype).at[jnp.arange(T)[:, None], topk_idx].add(topk_w)
        h = jnp.einsum('td,efd->etf', xt, fc1_w) + fc1_b[:, None, :]
        xh, g = (h[..., :F], h[..., F:])
        a = jax.nn.gelu(g, approximate=False) * xh * geglu_mult[:, None, :]
        yexp = jnp.einsum('etf,edf->etd', a, fc2_w) + fc2_b[:, None, :]
        y = jnp.einsum('etd,te->td', yexp, comb)
        hs = xt @ s_fc1_w.T + s_fc1_b
        xs, gs = (hs[..., :FS], hs[..., FS:])
        as_ = jax.nn.gelu(gs, approximate=False) * xs * s_geglu_mult
        ys = as_ @ s_fc2_w.T + s_fc2_b
        return (y + ys).reshape(s, b, d)
    x = L0_attn_x
    x = x + _L0_attn_ref(_layernorm(x, axis=-1), L0_attn_W_dt, L0_attn_b_dt, L0_attn_W_B, L0_attn_W_C, L0_attn_A_log, L0_attn_D_param)
    x = x + _L0_ffn_ref(_layernorm(x, axis=-1), L0_ffn_gate_w, L0_ffn_fc1_w, L0_ffn_fc1_b, L0_ffn_geglu_mult, L0_ffn_fc2_w, L0_ffn_fc2_b, L0_ffn_s_fc1_w, L0_ffn_s_fc1_b, L0_ffn_s_geglu_mult, L0_ffn_s_fc2_w, L0_ffn_s_fc2_b)
    return x

_drawn_inputs = setup_inputs


def setup_inputs(seed=0):
    import zlib

    import numpy as np

    out = dict(_drawn_inputs(seed))
    spreads = {'L0_attn_b_dt': (-2.0, 0.2),
     'L0_attn_D_param': (0.10000000149011612, 0.6),
     'L0_ffn_geglu_mult': (1.0, 0.6),
     'L0_ffn_s_geglu_mult': (1.0, 0.6)}
    factors = {'L0_ffn_fc1_b': 8.0, 'L0_ffn_fc2_b': 3.311, 'L0_ffn_s_fc1_b': 8.0}
    for name, (base, spread) in spreads.items():
        noise = np.random.default_rng([zlib.crc32(name.encode()), seed]).standard_normal(out[name].shape)
        drawn = base * np.exp(spread * noise) if base else spread * noise
        out[name] = jnp.asarray(drawn.astype(out[name].dtype))
    for name, factor in factors.items():
        out[name] = (out[name] * factor).astype(out[name].dtype)
    return out
```

```python
from contextlib import ExitStack

import concourse.bass as bass
from concourse import mybir

F32 = mybir.dt.float32
I32 = mybir.dt.int32
U32 = mybir.dt.uint32
ALU = mybir.AluOpType
ACT = mybir.ActivationFunctionType
AX = mybir.AxisListType
ds = bass.ds

P = 128
EPS = 1e-5
DT_MID, DT_HALF = (0.1 + 0.001) / 2.0, (0.1 - 0.001) / 2.0
SHARP = 0.5
A_HALF = 5.0
DA_HALF = 8.0
NORM_MAX = 20.0
SEG = 10
TOPK = 3


class Memory:
    pass


def model_kernel(nc, x, W_dt_t, b_dt, W_bc_t, A_log, D_param, gate_t, fc1_t, fc1_b, mult_t, fc2_t,
                 fc2_b, s_fc1_t, s_fc1_b, s_mult, s_fc2_t, s_fc2_b, out):
    NB, T, D = x.shape
    N = A_log.shape[1]
    E, F = mult_t.shape[1], mult_t.shape[0]
    FS = s_mult.shape[0]
    TOK = NB * T
    TILES = TOK // P
    KD = D // P
    XT = TOK * TOPK // P + E
    XT += XT % 2
    R = KD * N
    NSEG = T // SEG
    TAIL = T - NSEG * SEG

    x_rows = x.rearrange("b t d -> (b t) d")
    out_rows = out.rearrange("b t d -> (b t) d")
    x_skip = nc.dram_tensor("x_skip", (TOK, D), F32, kind="Internal").ap()
    x_mid = nc.dram_tensor("x_mid", (TOK, D), F32, kind="Internal").ap()
    x_norm = nc.dram_tensor("x_norm", (TOK, D), F32, kind="Internal").ap()
    row_token = nc.dram_tensor("row_token", (XT * P, 1), I32, kind="Internal").ap()
    row_out = nc.dram_tensor("row_out", (XT * P, D), F32, kind="Internal").ap()

    with ExitStack() as ctx:
        def sb(name, shape, dt=F32):
            return ctx.enter_context(nc.sbuf_tensor(name, shape, dt))

        phase_sems = []

        def sem(name):
            phase_sems.append(nc.alloc_semaphore(name))
            return phase_sems[-1]

        passed = ctx.enter_context(nc.semaphore("passed"))

        def settle(eng):
            eng.sem_inc(passed, 1)

        def end_phase():
            nc.clear_and_free_semaphores(list(phase_sems))
            phase_sems.clear()
            nc.all_engine_barrier()

        def sems(name, n=2):
            return [sem(f"{name}{i}") for i in range(n)]

        bank = ctx.enter_context(nc.psum_tensor("bank", [P, 8, 512], F32))

        arena_x = sb("arena_x", [P, KD * TOK])
        arena_dt = sb("arena_dt", [P, KD * TOK])
        xT = arena_x[:, :].rearrange("p (k t) -> p k t", k=KD)
        dtT = arena_dt[:, :].rearrange("p (k t) -> p k t", k=KD)
        w1 = arena_dt[:, 0:KD * E * 2 * F].rearrange("p (k e f) -> p k (e f)", k=KD, e=E)
        w2 = arena_x[:, 0:KD * E * D].rearrange("p (k e f) -> p k (e f)", k=KD, e=E)
        b1 = arena_x[:, KD * E * D:KD * E * D + E * 2 * F]

        ident = sb("ident", [P, P])
        ones = sb("ones", [P, P])
        before = sb("before", [P, P])
        minus_half = sb("minus_half", [P, 1])
        half = sb("half", [P, 8])
        expert_no = sb("expert_no", [P, E])

        with ExitStack() as part:
            def sb(name, shape, dt=F32):
                return part.enter_context(nc.sbuf_tensor(name, shape, dt))

            wdt = sb("wdt", [P, KD, D])
            wbc = sb("wbc", [P, KD, 2 * N])
            dbc = sb("dbc", [P, D])
            bdt = sb("bdt", [P, KD])
            tanh_bias = sb("tanh_bias", [P, 1])
            one_col = sb("one_col", [P, 1])
            a_neg = sb("a_neg", [P, KD, N])
            pick = sb("pick", [2 * N, 2 * N, P])
            bcT = sb("bcT", [2 * N, TOK])
            iota_i = sb("iota_i", [P, E], I32)
            load_part = ExitStack()

            def sb(name, shape, dt=F32):
                return load_part.enter_context(nc.sbuf_tensor(name, shape, dt))

            xin = [sb(f"xin{s}", [P, D]) for s in range(2)]
            xn = [sb(f"xn{s}", [P, D]) for s in range(2)]
            skip = [sb(f"skip{s}", [P, D]) for s in range(2)]
            stats = [sb(f"stats{s}", [P, 6]) for s in range(2)]
            meanvar = [sb(f"meanvar{s}", [P, 2]) for s in range(2)]
            rstd = [sb(f"rstd{s}", [P, 1]) for s in range(2)]

            c_loaded = sem("c_loaded")
            c_made = sem("c_made")
            c_a = sem("c_a")
            x_loaded, stats_made, aggregated = sems("x_loaded"), sems("stats_made"), sems("aggregated")
            eps_added, rstd_made, xn_made = sems("eps_added"), sems("rstd_made"), sems("xn_made")
            xn_turned, xT_written = sems("xn_turned"), sems("xT_written")
            dx_made, skip_made, skip_stored = sems("dx_made"), sems("skip_made"), sems("skip_stored")

            with nc.Block() as block:
                @block.sync
                def _(sp):
                    sp.dma_start(wdt[:], W_dt_t.rearrange("(k p) e -> p k e", p=P)).then_inc(c_loaded, 16)
                    sp.dma_start(wbc[:], W_bc_t.rearrange("(k p) n -> p k n", p=P)).then_inc(c_loaded, 16)
                    sp.dma_start(dbc[:], D_param.partition_broadcast(P)).then_inc(c_loaded, 16)
                    with nc.allow_non_contiguous_dma(reason="small constants, once"):
                        sp.dma_start(bdt[:], b_dt.rearrange("(k p) -> p k", p=P)).then_inc(c_loaded, 16)
                    sp.dma_start(a_neg[:], A_log.rearrange("(k p) n -> p k n", p=P)).then_inc(c_loaded, 16)
                    with sp.Fori(0, TILES // 2) as it:
                        for s in range(2):
                            sp.wait_ge(xn_made[s], it)
                            sp.wait_ge(skip_made[s], it)
                            sp.dma_start(xin[s][:], x_rows[ds((it * 2 + s) * P, P), :]).then_inc(x_loaded[s], 16)

                @block.gpsimd
                def _(pool):
                    pool.memset(ident[:], 0.0).then_inc(c_made, 1)
                    pool.memset(pick[:], 0.0).then_inc(c_made, 1)
                    pool.memset(before[:], 1.0).then_inc(c_made, 1)
                    pool.memset(ones[:], 1.0).then_inc(c_made, 1)
                    pool.memset(minus_half[:], -0.5).then_inc(c_made, 1)
                    pool.memset(half[:], 0.5).then_inc(c_made, 1)
                    pool.memset(tanh_bias[:], -DT_MID * SHARP / (DT_HALF + 1e-8)).then_inc(c_made, 1)
                    pool.memset(one_col[:], 1.0).then_inc(c_made, 1)
                    pool.iota(iota_i[:], pattern=[[1, E]], base=0, channel_multiplier=0).then_inc(c_made, 1)
                    pool.wait_ge(c_made, 9)
                    pool.affine_select(out=ident[:], in_=ident[:], compare_op=ALU.not_equal, fill=1.0,
                                       base=0, pattern=[[-1, P]], channel_multiplier=1).then_inc(c_made, 1)
                    pool.affine_select(out=pick[:], in_=pick[:], compare_op=ALU.not_equal, fill=1.0,
                                       base=0, pattern=[[-1, 2 * N], [0, P]],
                                       channel_multiplier=1).then_inc(c_made, 1)
                    pool.affine_select(out=before[:], in_=before[:], compare_op=ALU.is_gt, fill=0.0,
                                       base=0, pattern=[[1, P]], channel_multiplier=-1).then_inc(c_made, 1)
                    pool.tensor_copy(expert_no[:], iota_i[:]).then_inc(c_made, 1)
                    with pool.Fori(0, TILES // 2) as it:
                        for s in range(2):
                            pool.wait_ge(aggregated[s], it + 1)
                            settle(pool)
                            pool.tensor_scalar(rstd[s][:], meanvar[s][:, 1:2], EPS, None,
                                               ALU.add).then_inc(eps_added[s], 1)
                            pool.wait_ge(eps_added[s], it + 1)
                            pool.tensor_tensor(rstd[s][:], rstd[s][:], minus_half[:],
                                               ALU.pow).then_inc(rstd_made[s], 1)

                @block.vector
                def _(dve):
                    dve.wait_ge(c_loaded, 80)
                    with dve.Fori(0, TILES // 2) as it:
                        for s in range(2):
                            dve.wait_ge(x_loaded[s], 16 * (it + 1))
                            dve.bn_stats(stats[s][:], xin[s][:]).then_inc(stats_made[s], 1)
                            dve.wait_ge(stats_made[s], it + 1)
                            dve.wait_ge(rstd_made[s], it)
                            settle(dve)
                            dve.bn_aggr(meanvar[s][:], stats[s][:]).then_inc(aggregated[s], 1)
                        for s in range(2):
                            dve.wait_ge(rstd_made[s], it + 1)
                            dve.wait_ge(xn_turned[s], it)
                            dve.wait_ge(aggregated[s], it + 1)
                            dve.tensor_scalar(xn[s][:], xin[s][:], meanvar[s][:, 0:1], rstd[s][:, 0:1],
                                              ALU.subtract, ALU.mult).then_inc(xn_made[s], 1)
                        for s in range(2):
                            dve.wait_ge(xn_made[s], it + 1)
                            dve.wait_ge(skip_stored[s], 16 * it)
                            dve.tensor_tensor(skip[s][:], xn[s][:], dbc[:], ALU.mult).then_inc(dx_made[s], 1)
                        for s in range(2):
                            dve.wait_ge(dx_made[s], it + 1)
                            dve.tensor_tensor(skip[s][:], skip[s][:], xin[s][:], ALU.add).then_inc(skip_made[s], 1)

                @block.tensor
                def _(pe):
                    pe.wait_ge(c_made, 13)
                    with pe.Fori(0, TILES // 2) as it:
                        for s in range(2):
                            pe.wait_ge(xn_made[s], it + 1)
                            pe.wait_ge(xT_written[s], it)
                            for k in range(KD):
                                last = pe.transpose(bank[:, s, k * P:(k + 1) * P], xn[s][:, k * P:(k + 1) * P],
                                                    ident[:])
                            last.then_inc(xn_turned[s], 1)

                @block.scalar
                def _(act):
                    act.wait_ge(c_loaded, 80)
                    act.activation(a_neg[:], a_neg[:], ACT.Tanh, scale=SHARP / (A_HALF + 1e-8)).then_inc(c_a, 1)
                    act.wait_ge(c_a, 1)
                    act.activation(a_neg[:], a_neg[:], ACT.Exp, scale=A_HALF / SHARP).then_inc(c_a, 1)
                    act.wait_ge(c_a, 2)
                    act.mul(a_neg[:], a_neg[:], -1.0).then_inc(c_a, 1)
                    act.wait_ge(c_a, 3)
                    with act.Fori(0, TILES // 2) as it:
                        for s in range(2):
                            act.wait_ge(xn_turned[s], it + 1)
                            act.activation(xT[:, :, ds((it * 2 + s) * P, P)],
                                           bank[:, s, 0:D].rearrange("p (k t) -> p k t", k=KD),
                                           ACT.Copy).then_inc(xT_written[s], 1)
                            act.wait_ge(skip_made[s], it + 1)
                            act.dma_start(x_skip[ds((it * 2 + s) * P, P), :], skip[s][:]).then_inc(skip_stored[s], 16)
                    for s in range(2):
                        act.wait_ge(skip_stored[s], 16 * (TILES // 2))
            load_part.close()
            end_phase()

            proj_part = ExitStack()

            def sb(name, shape, dt=F32):
                return proj_part.enter_context(nc.sbuf_tensor(name, shape, dt))

            CH = 512
            mag = [sb(f"mag{s}", [P, KD, CH]) for s in range(2)]
            pos = [sb(f"pos{s}", [P, KD, CH]) for s in range(2)]
            projected, mag_made, e_made, l_made = sems("projected"), sems("mag_made"), sems("e_made"), sems("l_made")
            pos_made, sp_made, bc_copied = sems("pos_made"), sems("sp_made"), sems("bc_copied")
            tanh_made, dt_made, g_made = sem("tanh_made"), sem("dt_made"), sem("g_made")
            NG = 8
            GW = KD * TOK // NG
            with nc.Block() as block:
                @block.tensor
                def _(pe):
                    with pe.Fori(0, TOK // CH // 2) as it:
                        for s in range(2):
                            here = ds((it * 2 + s) * CH, CH)
                            pe.wait_ge(mag_made[s], it)
                            pe.wait_ge(bc_copied[s], it)
                            pe.wait_ge(pos_made[s], it)
                            for e in range(KD):
                                for k in range(KD):
                                    pe.matmul(bank[:, 3 * s + e, :], wdt[:, k, e * P:(e + 1) * P],
                                              xT[:, k, here], start=(k == 0), stop=(k == KD - 1))
                            for k in range(KD):
                                last = pe.matmul(bank[0:2 * N, 3 * s + 2, :], wbc[:, k, :], xT[:, k, here],
                                                 start=(k == 0), stop=(k == KD - 1))
                            last.then_inc(projected[s], 1)

                @block.scalar
                def _(act):
                    act.preload_act_table_set("natural_log_exp_and_others")
                    with act.Fori(0, TOK // CH // 2) as it:
                        for s in range(2):
                            here = ds((it * 2 + s) * CH, CH)
                            act.wait_ge(pos_made[s], it + 1)
                            act.wait_ge(sp_made[s], it)
                            for e in range(KD):
                                last = act.activation(mag[s][:, e, :], bank[:, 3 * s + e, :], ACT.Abs,
                                                      bias=bdt[:, e:e + 1])
                            last.then_inc(mag_made[s], 1)
                            act.activation(bcT[:, here], bank[0:2 * N, 3 * s + 2, :], ACT.Copy).then_inc(bc_copied[s], 1)
                            act.wait_ge(mag_made[s], it + 1)
                            act.activation(mag[s][:], mag[s][:], ACT.Exp, scale=-1.0).then_inc(e_made[s], 1)
                            act.wait_ge(e_made[s], it + 1)
                            act.activation(mag[s][:], mag[s][:], ACT.Ln, bias=one_col[:, 0:1]).then_inc(l_made[s], 1)
                    for s in range(2):
                        act.wait_ge(sp_made[s], TOK // CH // 2)
                    with act.Fori(0, NG) as i:
                        part_i = arena_dt[:, ds(i * GW, GW)]
                        act.activation(part_i, part_i, ACT.Tanh, bias=tanh_bias[:, 0:1],
                                       scale=SHARP / (DT_HALF + 1e-8)).then_inc(tanh_made, 1)

                @block.vector
                def _(dve):
                    with dve.Fori(0, TOK // CH // 2) as it:
                        for s in range(2):
                            here = ds((it * 2 + s) * CH, CH)
                            dve.wait_ge(projected[s], it + 1)
                            dve.wait_ge(sp_made[s], it)
                            for e in range(KD):
                                last = dve.tensor_scalar(pos[s][:, e, :], bank[:, 3 * s + e, :], bdt[:, e:e + 1],
                                                         0.0, ALU.add, ALU.max)
                            last.then_inc(pos_made[s], 1)
                            dve.wait_ge(pos_made[s], it + 1)
                            dve.wait_ge(l_made[s], it + 1)
                            dve.tensor_tensor(dtT[:, :, here], pos[s][:], mag[s][:], ALU.add).then_inc(sp_made[s], 1)
                    with dve.Fori(0, NG) as i:
                        part_i = arena_dt[:, ds(i * GW, GW)]
                        x_i = arena_x[:, ds(i * GW, GW)]
                        dve.wait_ge(tanh_made, i + 1)
                        dve.tensor_scalar(part_i, part_i, DT_HALF / SHARP, DT_MID, ALU.mult,
                                          ALU.add).then_inc(dt_made, 1)
                        dve.wait_ge(dt_made, i + 1)
                        dve.tensor_tensor(x_i, x_i, part_i, ALU.mult).then_inc(g_made, 1)
                    dve.wait_ge(g_made, NG)
            proj_part.close()
            end_phase()

            scan_part = ExitStack()

            def sb(name, shape, dt=F32):
                return scan_part.enter_context(nc.sbuf_tensor(name, shape, dt))

            W = R * NB
            dA = [sb(f"dA{s}", [P, W * SEG]) for s in range(2)]
            u = sb("u", [P, W * SEG])
            h = sb("h", [P, W * SEG])
            hc = sb("hc", [P, W * SEG])
            t1 = sb("t1", [P, W])
            h0 = sb("h0", [P, W])
            sq = sb("sq", [P, W])
            h_last = sb("h_last", [P, W])
            norm2 = sb("norm2", [P, NB])
            norm = sb("norm", [P, NB])
            scale = sb("scale", [P, NB])
            gT = arena_x[:, :].rearrange("p (k b t) -> p k b t", k=KD, b=NB)
            dtT4 = arena_dt[:, :].rearrange("p (k b t) -> p k b t", k=KD, b=NB)
            bcT3 = bcT[:, :].rearrange("r (b t) -> r b t", b=NB)

            z_made, tanh_z, dA_made, scanned = sems("z_made"), sems("tanh_z"), sems("dA_made"), sems("scanned")
            b_spread, c_spread, u_made, hc_made = sem("b_spread"), sem("c_spread"), sem("u_made"), sem("hc_made")
            decayed, h0_made, sq_made, sq_summed = sem("decayed"), sem("h0_made"), sem("sq_made"), sem("sq_summed")
            norm2_made, norm_made, eps_in, inv_made = sem("norm2_made"), sem("norm_made"), sem("eps_in"), sem("inv_made")
            scale_made, h0_in, dA_cut, y_made, last_kept = (sem("scale_made"), sem("h0_in"), sem("dA_cut"),
                                                             sem("y_made"), sem("last_kept"))
            first_state = sem("first_state")

            def rows(buf, L):
                return buf[:, 0:W * L].rearrange("p (k n b t) -> p k n b t", k=KD, n=N, b=NB)

            def flat_rows(buf, L):
                return buf[:, 0:W * L].rearrange("p (r b t) -> p r b t", r=R, b=NB)

            HN = N // 2

            def spread(half_no, first_bank, L):
                return bank[:, first_bank + half_no, 0:HN * NB * L].rearrange("p (n b t) -> p n b t", n=HN, b=NB)

            with nc.Block() as block:
                def segments(eng, body):
                    with eng.Fori(0, NSEG // 2) as it:
                        for s in range(2):
                            body(it, s, it * 2 + s, SEG)
                    body(NSEG // 2, 0, NSEG, TAIL)

                @block.gpsimd
                def _(pool):
                    def body(it, s, seg, L):
                        pool.wait_ge(scanned[s], it)
                        z = rows(dA[s], L)
                        for k in range(KD):
                            last = pool.tensor_tensor(
                                z[:, k], dtT4[:, k, :, ds(seg * SEG, L)].unsqueeze(1).to_broadcast([P, N, NB, L]),
                                a_neg[:, k, :].unsqueeze(2).unsqueeze(3).to_broadcast([P, N, NB, L]), ALU.mult)
                        last.then_inc(z_made[s], 1)
                        pool.wait_ge(norm2_made, seg + 1)
                        pool.tensor_tensor(norm[:], norm2[:], half[:, 0:NB], ALU.pow).then_inc(norm_made, 1)
                    segments(pool, body)

                @block.scalar
                def _(act):
                    act.preload_act_table_set("exp_and_others")

                    def body(it, s, seg, L):
                        z = dA[s][:, 0:W * L]
                        act.wait_ge(z_made[s], it + 1)
                        act.activation(z, z, ACT.Tanh, scale=SHARP / (DA_HALF + 1e-8)).then_inc(tanh_z[s], 1)
                        act.wait_ge(tanh_z[s], it + 1)
                        act.activation(z, z, ACT.Exp, scale=DA_HALF / SHARP).then_inc(dA_made[s], 1)
                    segments(act, body)

                @block.tensor
                def _(pe):
                    def body(it, s, seg, L):
                        for half_no in range(2):
                            if half_no == 0:
                                pe.wait_ge(u_made, seg)
                                settle(pe)
                            for n in range(HN):
                                last = pe.matmul(spread(half_no, 0, L)[:, n], pick[:, half_no * HN + n, :],
                                                 bcT3[:, :, ds(seg * SEG, L)], start=True, stop=True)
                        last.then_inc(b_spread, 1)
                        for half_no in range(2):
                            if half_no == 0:
                                pe.wait_ge(hc_made, seg)
                                settle(pe)
                            for n in range(HN):
                                last = pe.matmul(spread(half_no, 2, L)[:, n], pick[:, N + half_no * HN + n, :],
                                                 bcT3[:, :, ds(seg * SEG, L)], start=True, stop=True)
                        last.then_inc(c_spread, 1)
                        pe.wait_ge(sq_made, seg + 1)
                        pe.wait_ge(norm2_made, seg)
                        pe.matmul(bank[:, 4, 0:W], ones[:], sq[:], start=True, stop=True).then_inc(sq_summed, 1)
                    segments(pe, body)

                @block.vector
                def _(dve):
                    dve.memset(h_last[:], 0.0).then_inc(first_state, 1)
                    dve.wait_ge(first_state, 1)

                    def body(it, s, seg, L):
                        at = ds(seg * SEG, L)
                        uu, cc = rows(u, L), rows(hc, L)
                        dve.wait_ge(b_spread, seg + 1)
                        for k in range(KD):
                            for half_no in range(2):
                                n0 = half_no * HN
                                last = dve.tensor_tensor(
                                    uu[:, k, n0:n0 + HN], gT[:, k, :, at].unsqueeze(1).to_broadcast([P, HN, NB, L]),
                                    spread(half_no, 0, L), ALU.mult)
                        last.then_inc(u_made, 1)
                        dve.wait_ge(dA_made[s], it + 1)
                        dve.wait_ge(last_kept, seg)
                        d3 = flat_rows(dA[s], L)
                        u3 = flat_rows(u, L)
                        h3 = flat_rows(h, L)

                        def grid(buf):
                            return buf[:].rearrange("p (r b) -> p r b", r=R)

                        dve.tensor_tensor(grid(t1), grid(h_last), d3[:, :, :, 0], ALU.mult).then_inc(decayed, 1)
                        dve.wait_ge(decayed, seg + 1)
                        dve.wait_ge(u_made, seg + 1)
                        dve.tensor_tensor(grid(h0), grid(t1), u3[:, :, :, 0], ALU.add).then_inc(h0_made, 1)
                        dve.memset(d3[:, :, :, 0], 0.0).then_inc(dA_cut, 1)
                        dve.wait_ge(h0_made, seg + 1)
                        dve.tensor_tensor(sq[:], h0[:], h0[:], ALU.mult).then_inc(sq_made, 1)
                        dve.wait_ge(sq_summed, seg + 1)
                        dve.tensor_reduce(norm2[:], bank[:, 4, 0:W].rearrange("p (r b) -> p b r", r=R), AX.X,
                                          ALU.add).then_inc(norm2_made, 1)
                        dve.wait_ge(norm_made, seg + 1)
                        dve.tensor_scalar(norm[:], norm[:], 1e-8, None, ALU.add).then_inc(eps_in, 1)
                        dve.wait_ge(eps_in, seg + 1)
                        dve.reciprocal(scale[:], norm[:]).then_inc(inv_made, 1)
                        dve.wait_ge(inv_made, seg + 1)
                        dve.tensor_scalar(scale[:], scale[:], NORM_MAX, 1.0, ALU.mult, ALU.min).then_inc(scale_made, 1)
                        dve.wait_ge(scale_made, seg + 1)
                        dve.tensor_tensor(u3[:, :, :, 0], grid(h0), scale[:].unsqueeze(1).to_broadcast([P, R, NB]),
                                          ALU.mult).then_inc(h0_in, 1)
                        dve.wait_ge(h0_in, seg + 1)
                        dve.wait_ge(dA_cut, seg + 1)
                        dve.tensor_tensor_scan(h[:, 0:W * L], dA[s][:, 0:W * L], u[:, 0:W * L], 0.0, ALU.mult,
                                               ALU.add).then_inc(scanned[s], 1)
                        dve.wait_ge(scanned[s], it + 1)
                        dve.tensor_copy(grid(h_last), h3[:, :, :, L - 1]).then_inc(last_kept, 1)
                        dve.wait_ge(c_spread, seg + 1)
                        for k in range(KD):
                            for half_no in range(2):
                                n0 = half_no * HN
                                last = dve.tensor_tensor(cc[:, k, n0:n0 + HN], rows(h, L)[:, k, n0:n0 + HN],
                                                         spread(half_no, 2, L), ALU.mult)
                        last.then_inc(hc_made, 1)
                        dve.wait_ge(hc_made, seg + 1)
                        settle(dve)
                        for k in range(KD):
                            last = dve.tensor_reduce(gT[:, k, :, at], cc[:, k].rearrange("p n b t -> p b t n"), AX.X,
                                                     ALU.add)
                        last.then_inc(y_made, 1)
                        dve.wait_ge(y_made, seg + 1)
                    segments(dve, body)
            scan_part.close()
            end_phase()

        with ExitStack() as part:
            def sb(name, shape, dt=F32):
                return part.enter_context(nc.sbuf_tensor(name, shape, dt))

            chosen = sb("chosen", [P, TILES, TOPK, E])
            weight = sb("weight", [P, TILES, TOPK])
            row_i = sb("row_i", [P, TILES, TOPK], I32)
            tile_expert = sb("tile_expert", [1, XT], I32)
            tile_no = sb("tile_no", [1, XT])

            route_part = ExitStack()

            def sb(name, shape, dt=F32):
                return route_part.enter_context(nc.sbuf_tensor(name, shape, dt))

            gate = sb("gate", [P, KD, E])
            ycp = [sb(f"ycp{s}", [P, KD, P]) for s in range(2)]
            xs = [sb(f"xs{s}", [P, D]) for s in range(2)]
            x2 = [sb(f"x2{s}", [P, D]) for s in range(2)]
            xn2 = [sb(f"xnb{s}", [P, D]) for s in range(2)]
            xn2T = [sb(f"xnbT{s}", [P, KD, P]) for s in range(2)]
            stats = [sb(f"statsb{s}", [P, 6]) for s in range(2)]
            meanvar = [sb(f"meanvarb{s}", [P, 2]) for s in range(2)]
            rstd = [sb(f"rstdb{s}", [P, 1]) for s in range(2)]
            logit = [sb(f"logit{s}", [P, E + 1]) for s in range(2)]
            best = [sb(f"best{s}", [P, 8]) for s in range(2)]
            best_at = [sb(f"best_at{s}", [P, 8], U32) for s in range(2)]
            best_f = [sb(f"best_f{s}", [P, 8]) for s in range(2)]
            neg_max = [sb(f"neg_max{s}", [P, 1]) for s in range(2)]
            ex = [sb(f"ex{s}", [P, E]) for s in range(2)]
            z_sum = [sb(f"z_sum{s}", [P, 1]) for s in range(2)]
            ek = [sb(f"ek{s}", [P, TOPK]) for s in range(2)]
            s_sum = [sb(f"s_sum{s}", [P, 1]) for s in range(2)]

            gate_loaded, pad_made = sem("gate_loaded"), sem("pad_made")
            names = ["xs_loaded", "y_copied", "y_turned", "x2_made", "x2_stored", "st_made", "ag_made", "ep_made",
                     "rs_made", "xn2_made", "xn2_stored", "xn2_turned", "xn2T_made", "logit_done", "logit_copied",
                     "best_made", "at_made", "neg_made", "ex_made", "ek_made", "zr_made", "sk_made", "sum_made",
                     "sum_eps", "sum_inv", "w_made", "atf_made", "hot_made"]
            q = Memory()
            (q.xs_loaded, q.y_copied, q.y_turned, q.x2_made, q.x2_stored, q.st_made, q.ag_made, q.ep_made,
             q.rs_made, q.xn2_made, q.xn2_stored, q.xn2_turned, q.xn2T_made, q.logit_done, q.logit_copied,
             q.best_made, q.at_made, q.neg_made, q.ex_made, q.ek_made, q.zr_made, q.sk_made, q.sum_made,
             q.sum_eps, q.sum_inv, q.w_made, q.atf_made, q.hot_made) = [sems(n) for n in names]

            with nc.Block() as block:
                @block.sync
                def _(sp):
                    sp.dma_start(gate[:], gate_t.rearrange("(k p) e -> p k e", p=P)).then_inc(gate_loaded, 16)
                    with sp.Fori(0, TILES // 2) as it:
                        for s in range(2):
                            sp.wait_ge(q.x2_made[s], it)
                            sp.dma_start(xs[s][:], x_skip[ds((it * 2 + s) * P, P), :]).then_inc(q.xs_loaded[s], 16)
                        for s in range(2):
                            sp.wait_ge(q.x2_made[s], it + 1)
                            sp.dma_start(x_mid[ds((it * 2 + s) * P, P), :], x2[s][:]).then_inc(q.x2_stored[s], 16)
                        for s in range(2):
                            sp.wait_ge(q.xn2_made[s], it + 1)
                            sp.dma_start(x_norm[ds((it * 2 + s) * P, P), :], xn2[s][:]).then_inc(q.xn2_stored[s], 16)
                    for s in range(2):
                        sp.wait_ge(q.x2_stored[s], 16 * (TILES // 2))
                        sp.wait_ge(q.xn2_stored[s], 16 * (TILES // 2))

                @block.gpsimd
                def _(pool):
                    with pool.Fori(0, TILES // 2) as it:
                        for s in range(2):
                            pool.wait_ge(q.ag_made[s], it + 1)
                            pool.wait_ge(q.xn2_made[s], it)
                            settle(pool)
                            pool.tensor_scalar(rstd[s][:], meanvar[s][:, 1:2], EPS, None,
                                               ALU.add).then_inc(q.ep_made[s], 1)
                            pool.wait_ge(q.ep_made[s], it + 1)
                            pool.tensor_tensor(rstd[s][:], rstd[s][:], minus_half[:],
                                               ALU.pow).then_inc(q.rs_made[s], 1)

                @block.tensor
                def _(pe):
                    pe.wait_ge(gate_loaded, 16)
                    with pe.Fori(0, TILES // 2) as it:
                        for s in range(2):
                            pe.wait_ge(q.y_copied[s], it + 1)
                            pe.wait_ge(q.x2_made[s], it)
                            for k in range(KD):
                                last = pe.transpose(bank[:, s, k * P:(k + 1) * P], ycp[s][:, k, :], ident[:])
                            last.then_inc(q.y_turned[s], 1)
                        for s in range(2):
                            pe.wait_ge(q.xn2_made[s], it + 1)
                            pe.wait_ge(q.xn2T_made[s], it)
                            for k in range(KD):
                                last = pe.transpose(bank[:, 2 + s, k * P:(k + 1) * P], xn2[s][:, k * P:(k + 1) * P],
                                                    ident[:])
                            last.then_inc(q.xn2_turned[s], 1)
                        for s in range(2):
                            pe.wait_ge(q.xn2T_made[s], it + 1)
                            pe.wait_ge(q.logit_copied[s], it)
                            for k in range(KD):
                                last = pe.matmul(bank[:, 4 + s, 0:E], xn2T[s][:, k, :], gate[:, k, :],
                                                 start=(k == 0), stop=(k == KD - 1))
                            last.then_inc(q.logit_done[s], 1)

                @block.scalar
                def _(act):
                    act.preload_act_table_set("exp_and_others")
                    with act.Fori(0, TILES // 2) as it:
                        for s in range(2):
                            act.wait_ge(q.y_turned[s], it)
                            act.activation(ycp[s][:], xT[:, :, ds((it * 2 + s) * P, P)], ACT.Copy)\
                               .then_inc(q.y_copied[s], 1)
                        for s in range(2):
                            act.wait_ge(q.xn2_turned[s], it + 1)
                            act.wait_ge(q.logit_done[s], it)
                            act.activation(xn2T[s][:], bank[:, 2 + s, 0:D].rearrange("p (k t) -> p k t", k=KD),
                                           ACT.Copy).then_inc(q.xn2T_made[s], 1)
                        for s in range(2):
                            act.wait_ge(q.neg_made[s], it + 1)
                            act.wait_ge(q.w_made[s], it)
                            act.activation(ex[s][:], logit[s][:, 0:E], ACT.Exp, bias=neg_max[s][:, 0:1],
                                           accum_out=z_sum[s][:]).then_inc(q.ex_made[s], 1)
                            act.activation(ek[s][:], best[s][:, 0:TOPK], ACT.Exp,
                                           bias=neg_max[s][:, 0:1]).then_inc(q.ek_made[s], 1)

                @block.vector
                def _(dve):
                    for s in range(2):
                        dve.memset(logit[s][:], -3.0e38).then_inc(pad_made, 1)
                    dve.wait_ge(pad_made, 2)
                    with dve.Fori(0, TILES // 2) as it:
                        for s in range(2):
                            dve.wait_ge(q.xs_loaded[s], 16 * (it + 1))
                            dve.wait_ge(q.y_turned[s], it + 1)
                            dve.wait_ge(q.x2_stored[s], 16 * it)
                            dve.tensor_tensor(x2[s][:], xs[s][:], bank[:, s, 0:D], ALU.add).then_inc(q.x2_made[s], 1)
                        for s in range(2):
                            dve.wait_ge(q.x2_made[s], it + 1)
                            dve.bn_stats(stats[s][:], x2[s][:]).then_inc(q.st_made[s], 1)
                        for s in range(2):
                            dve.wait_ge(q.st_made[s], it + 1)
                            settle(dve)
                            dve.bn_aggr(meanvar[s][:], stats[s][:]).then_inc(q.ag_made[s], 1)
                        for s in range(2):
                            dve.wait_ge(q.rs_made[s], it + 1)
                            dve.wait_ge(q.ag_made[s], it + 1)
                            dve.wait_ge(q.xn2_turned[s], it)
                            dve.wait_ge(q.xn2_stored[s], 16 * it)
                            dve.tensor_scalar(xn2[s][:], x2[s][:], meanvar[s][:, 0:1], rstd[s][:, 0:1],
                                              ALU.subtract, ALU.mult).then_inc(q.xn2_made[s], 1)
                        for s in range(2):
                            dve.wait_ge(q.logit_done[s], it + 1)
                            dve.tensor_copy(logit[s][:, 0:E], bank[:, 4 + s, 0:E]).then_inc(q.logit_copied[s], 1)
                        for s in range(2):
                            dve.wait_ge(q.logit_copied[s], it + 1)
                            settle(dve)
                            dve.max(best[s][:], logit[s][:]).then_inc(q.best_made[s], 1)
                        for s in range(2):
                            dve.wait_ge(q.best_made[s], it + 1)
                            dve.tensor_scalar(neg_max[s][:], best[s][:, 0:1], -1.0, None, ALU.mult)\
                               .then_inc(q.neg_made[s], 1)
                            dve.max_index(best_at[s][:], best[s][:], logit[s][:]).then_inc(q.at_made[s], 1)
                        for s in range(2):
                            dve.wait_ge(q.at_made[s], it + 1)
                            dve.tensor_copy(best_f[s][:], best_at[s][:]).then_inc(q.atf_made[s], 1)
                        for s in range(2):
                            dve.wait_ge(q.atf_made[s], it + 1)
                            for k in range(TOPK):
                                last = dve.tensor_scalar(
                                    chosen[:, ds(it * 2 + s, 1), k, :].rearrange("p o e -> p (o e)"), expert_no[:],
                                    best_f[s][:, k:k + 1], None, ALU.is_equal)
                            last.then_inc(q.hot_made[s], 1)
                        for s in range(2):
                            dve.wait_ge(q.ex_made[s], it + 1)
                            dve.reciprocal(z_sum[s][:], z_sum[s][:]).then_inc(q.zr_made[s], 1)
                        for s in range(2):
                            dve.wait_ge(q.zr_made[s], it + 1)
                            dve.wait_ge(q.ek_made[s], it + 1)
                            dve.tensor_scalar(ek[s][:], ek[s][:], z_sum[s][:, 0:1], None, ALU.mult)\
                               .then_inc(q.sk_made[s], 1)
                        for s in range(2):
                            dve.wait_ge(q.sk_made[s], it + 1)
                            dve.tensor_reduce(s_sum[s][:], ek[s][:], AX.X, ALU.add).then_inc(q.sum_made[s], 1)
                        for s in range(2):
                            dve.wait_ge(q.sum_made[s], it + 1)
                            dve.tensor_scalar(s_sum[s][:], s_sum[s][:], 1e-20, None, ALU.add)\
                               .then_inc(q.sum_eps[s], 1)
                        for s in range(2):
                            dve.wait_ge(q.sum_eps[s], it + 1)
                            dve.reciprocal(s_sum[s][:], s_sum[s][:]).then_inc(q.sum_inv[s], 1)
                        for s in range(2):
                            dve.wait_ge(q.sum_inv[s], it + 1)
                            dve.tensor_scalar(weight[:, ds(it * 2 + s, 1), :].rearrange("p o k -> p (o k)"), ek[s][:],
                                              s_sum[s][:, 0:1], None, ALU.mult).then_inc(q.w_made[s], 1)
            route_part.close()
            end_phase()

            rank_part = ExitStack()

            def sb(name, shape, dt=F32):
                return rank_part.enter_context(nc.sbuf_tensor(name, shape, dt))

            taken = sb("taken", [P, TILES, E])
            so_far = sb("so_far", [P, E, TILES])
            row_f = sb("row_f", [P, TILES, E])
            one_row = sb("one_row", [P, TILES, E])
            picked = sb("picked", [P, TILES, TOPK])
            step_i = sb("step_i", [P, TILES], I32)
            step_f = sb("step_f", [P, TILES])
            over = sb("over", [P, E, TILES])
            n_tiles = sb("n_tiles", [P, E])
            tiles_to = sb("tiles_to", [P, E])
            base = sb("base", [P, E])
            tno_i = sb("tno_i", [1, XT], I32)
            past = sb("past", [1, XT, E])
            exp_f = sb("exp_f", [1, XT])
            zero_i = sb("zero_i", [P, XT], I32)
            wmul = sb("wmul", [P, KD, E])
            w_loaded, r_pool, r_dve, r_pe, m_done = (sem("w_loaded"), sem("r_pool"), sem("r_dve"), sem("r_pe"),
                                                     sem("m_done"))
            cleared = sem("cleared")
            HT = TILES // 2
            with nc.Block() as block:
                @block.sync
                def _(sp):
                    sp.dma_start(w2, fc2_t.rearrange("(k p) e d -> p k (e d)", p=P)).then_inc(w_loaded, 16)
                    sp.dma_start(wmul[:], mult_t.rearrange("(k p) e -> p k e", p=P)).then_inc(w_loaded, 16)
                    sp.dma_start(w1, fc1_t.rearrange("(k p) e f -> p k (e f)", p=P)).then_inc(w_loaded, 16)
                    sp.dma_start(b1, fc1_b.rearrange("e f -> (e f)").partition_broadcast(P)).then_inc(w_loaded, 16)
                    sp.wait_ge(r_pool, 3)
                    sp.dma_start(row_token.rearrange("(p j) o -> p (j o)", p=P), zero_i[:]).then_inc(cleared, 16)
                    sp.wait_ge(cleared, 16)
                    sp.wait_ge(w_loaded, 64)

                @block.gpsimd
                def _(pool):
                    pool.iota(step_i[:], pattern=[[P, TILES]], base=0, channel_multiplier=0).then_inc(r_pool, 1)
                    pool.iota(tno_i[:], pattern=[[1, XT]], base=0, channel_multiplier=0).then_inc(r_pool, 1)
                    pool.memset(zero_i[:], 0).then_inc(r_pool, 1)
                    pool.wait_ge(r_pool, 3)
                    pool.tensor_copy(step_f[:], step_i[:]).then_inc(r_pool, 1)
                    pool.tensor_copy(tile_no[:], tno_i[:]).then_inc(r_pool, 1)

                @block.tensor
                def _(pe):
                    pe.wait_ge(r_dve, 2)
                    for hf in range(2):
                        m = taken[:, hf * HT:(hf + 1) * HT, :].rearrange("p i e -> p (i e)")
                        pe.matmul(bank[:, hf, 0:HT * E], before[:], m, start=True, stop=True)
                        last = pe.matmul(bank[:, 2 + hf, 0:HT * E], ones[:], m, start=True, stop=True)
                    last.then_inc(r_pe, 1)

                @block.vector
                def _(dve):
                    n = [0]

                    def chain(ins):
                        ins.then_inc(r_dve, 1)
                        n[0] += 1
                        dve.wait_ge(r_dve, n[0])

                    chain(dve.tensor_tensor(taken[:], chosen[:, :, 0, :], chosen[:, :, 1, :], ALU.add))
                    chain(dve.tensor_tensor(taken[:], taken[:], chosen[:, :, 2, :], ALU.add))
                    dve.wait_ge(r_pe, 1)
                    for e in range(E):
                        for hf in range(2):
                            chain(dve.tensor_tensor_scan(
                                so_far[:, e, hf * HT:(hf + 1) * HT], ones[:, 0:HT],
                                bank[:, 2 + hf, 0:HT * E].rearrange("p (i e) -> p e i", e=E)[:, e, :],
                                0.0 if hf == 0 else so_far[:, e, HT - 1:HT], ALU.mult, ALU.add))
                    dve.wait_ge(r_pool, 5)
                    chain(dve.tensor_tensor(over[:], so_far[:, :, TILES - 1:TILES].to_broadcast([P, E, TILES]),
                                            step_f[:].unsqueeze(1).to_broadcast([P, E, TILES]), ALU.is_gt))
                    chain(dve.tensor_reduce(n_tiles[:], over[:], AX.X, ALU.add))
                    chain(dve.tensor_tensor_scan(tiles_to[:], ones[:, 0:E], n_tiles[:], 0.0, ALU.mult, ALU.add))
                    chain(dve.tensor_tensor(base[:], tiles_to[:], n_tiles[:], ALU.subtract))
                    chain(dve.tensor_scalar(base[:], base[:], float(P), None, ALU.mult))
                    for hf in range(2):
                        i0 = hf * HT
                        r = row_f[:, i0:i0 + HT, :]
                        chain(dve.tensor_tensor(r, so_far[:, :, i0:i0 + HT].rearrange("p e i -> p i e"),
                                                bank[:, 2 + hf, 0:HT * E].rearrange("p (i e) -> p i e", e=E),
                                                ALU.subtract))
                        chain(dve.tensor_tensor(r, r, bank[:, hf, 0:HT * E].rearrange("p (i e) -> p i e", e=E),
                                                ALU.add))
                    chain(dve.tensor_tensor(row_f[:], row_f[:], base[:].unsqueeze(1).to_broadcast([P, TILES, E]),
                                            ALU.add))
                    for k in range(TOPK):
                        chain(dve.tensor_tensor(one_row[:], row_f[:], chosen[:, :, k, :], ALU.mult))
                        chain(dve.tensor_reduce(picked[:, :, k], one_row[:], AX.X, ALU.add))
                    chain(dve.tensor_copy(row_i[:], picked[:]))
                    chain(dve.tensor_tensor(past[:], tile_no[:].unsqueeze(2).to_broadcast([1, XT, E]),
                                            tiles_to[0:1, :].unsqueeze(1).to_broadcast([1, XT, E]), ALU.is_ge))
                    chain(dve.tensor_reduce(exp_f[:], past[:], AX.X, ALU.add))
                    chain(dve.tensor_scalar(exp_f[:], exp_f[:], float(E - 1), None, ALU.min))
                    chain(dve.tensor_copy(tile_expert[:], exp_f[:]))
                    dve.wait_ge(w_loaded, 64)
                    for k in range(KD):
                        v = w2[:, k, :].rearrange("p (e d) -> p e d", e=E)
                        chain(dve.tensor_tensor(v, v, wmul[:, k, :].unsqueeze(2).to_broadcast([P, E, D]), ALU.mult))
            rank_part.close()
            end_phase()

            ids_part = ExitStack()

            def sb(name, shape, dt=F32):
                return ids_part.enter_context(nc.sbuf_tensor(name, shape, dt))

            to_row = [sb(f"to_row{s}", [P, TOPK], I32) for s in range(2)]
            token = [sb(f"token{s}", [P, 1], I32) for s in range(2)]
            token_all = sb("token_all", [P, TILES], I32)
            t_made, t_copied, t_sent = sem("t_made"), sems("t_copied"), sems("t_sent")
            with nc.Block() as block:
                @block.gpsimd
                def _(pool):
                    pool.iota(token_all[:], pattern=[[P, TILES]], base=0, channel_multiplier=1).then_inc(t_made, 1)
                    pool.wait_ge(t_made, 1)
                    with pool.Fori(0, TILES // 2) as it:
                        for s in range(2):
                            pool.wait_ge(t_sent[s], 48 * it)
                            pool.tensor_copy(to_row[s][:], row_i[:, ds(it * 2 + s, 1), :].rearrange("p o k -> p (o k)"))
                            pool.tensor_copy(token[s][:], token_all[:, ds(it * 2 + s, 1)]).then_inc(t_copied[s], 1)
                            pool.wait_ge(t_copied[s], it + 1)
                            settle(pool)
                            for k in range(TOPK):
                                pool.indirect_dma_start(
                                    out=row_token, out_offset=bass.IndirectOffsetOnAxis(ap=to_row[s][:, k:k + 1], axis=0),
                                    in_=token[s][:], in_offset=None).then_inc(t_sent[s], 16)
                    for s in range(2):
                        pool.wait_ge(t_sent[s], 48 * (TILES // 2))
            ids_part.close()
            end_phase()

            exp_part = ExitStack()

            def sb(name, shape, dt=F32):
                return exp_part.enter_context(nc.sbuf_tensor(name, shape, dt))

            rt = [sb(f"rt{s}", [P, 1], I32) for s in range(2)]
            xg = [sb(f"xg{s}", [P, D]) for s in range(2)]
            xgT = [sb(f"xgT{s}", [P, KD, P]) for s in range(2)]
            hid = [sb(f"hid{s}", [P, 2 * F]) for s in range(2)]
            act_g = [sb(f"act_g{s}", [P, F]) for s in range(2)]
            glu = [sb(f"glu{s}", [P, F]) for s in range(2)]
            gluT = [sb(f"gluT{s}", [P, F // P, P]) for s in range(2)]
            ye = [sb(f"ye{s}", [P, D]) for s in range(2)]
            z = Memory()
            (z.rt_loaded, z.xg_loaded, z.xg_turned, z.xgT_made, z.h_done, z.hid_made, z.gelu_made, z.glu_made,
             z.glu_turned, z.gluT_made, z.y_done, z.ye_made, z.ye_stored) = [sems(n) for n in (
                 "rt_loaded", "xg_loaded", "xg_turned", "xgT_made", "h_done", "hid_made", "gelu_made", "glu_made",
                 "glu_turned", "gluT_made", "ye_done", "ye_made", "ye_stored")]
            with nc.Block() as block:
                @block.sync
                def _(sp):
                    with sp.Fori(0, XT // 2) as it:
                        for s in range(2):
                            sp.wait_ge(z.xg_loaded[s], 16 * it)
                            sp.dma_start(rt[s][:], row_token[ds((it * 2 + s) * P, P), :]).then_inc(z.rt_loaded[s], 16)
                        for s in range(2):
                            sp.wait_ge(z.ye_made[s], it + 1)
                            sp.dma_start(row_out[ds((it * 2 + s) * P, P), :], ye[s][:]).then_inc(z.ye_stored[s], 16)
                    for s in range(2):
                        sp.wait_ge(z.ye_stored[s], 16 * (XT // 2))

                @block.gpsimd
                def _(pool):
                    with pool.Fori(0, XT // 2) as it:
                        for s in range(2):
                            pool.wait_ge(z.rt_loaded[s], 16 * (it + 1))
                            pool.wait_ge(z.xg_turned[s], it)
                            settle(pool)
                            pool.indirect_dma_start(
                                out=xg[s][:], out_offset=None, in_=x_norm,
                                in_offset=bass.IndirectOffsetOnAxis(ap=rt[s][:, 0:1], axis=0)).then_inc(z.xg_loaded[s], 16)

                @block.tensor
                def _(pe):
                    with pe.Fori(0, XT // 2) as it:
                        for s in range(2):
                            pe.wait_ge(z.xg_loaded[s], 16 * (it + 1))
                            pe.wait_ge(z.xgT_made[s], it)
                            for k in range(KD):
                                last = pe.transpose(bank[:, s, k * P:(k + 1) * P], xg[s][:, k * P:(k + 1) * P], ident[:])
                            last.then_inc(z.xg_turned[s], 1)
                        e_no = [pe.value_load(tile_expert[0:1, ds(it * 2 + s, 1)], min_val=0, max_val=E - 1)
                                for s in range(2)]
                        for s in range(2):
                            pe.wait_ge(z.xgT_made[s], it + 1)
                            pe.wait_ge(z.hid_made[s], it)
                            for k in range(KD):
                                last = pe.matmul(bank[:, 2 + s, :], xgT[s][:, k, :], w1[:, k, ds(e_no[s] * (2 * F), 2 * F)],
                                                 start=(k == 0), stop=(k == KD - 1))
                            last.then_inc(z.h_done[s], 1)
                        for s in range(2):
                            pe.wait_ge(z.glu_made[s], it + 1)
                            pe.wait_ge(z.gluT_made[s], it)
                            for k in range(F // P):
                                last = pe.transpose(bank[:, 4 + s, k * P:(k + 1) * P], glu[s][:, k * P:(k + 1) * P], ident[:])
                            last.then_inc(z.glu_turned[s], 1)
                            pe.wait_ge(z.gluT_made[s], it + 1)
                            pe.wait_ge(z.ye_made[s], it)
                            for k in range(F // P):
                                last = pe.matmul(bank[:, 6 + s, 0:D], gluT[s][:, k, :], w2[:, k, ds(e_no[s] * D, D)],
                                                 start=(k == 0), stop=(k == F // P - 1))
                            last.then_inc(z.y_done[s], 1)

                @block.scalar
                def _(act):
                    act.preload_act_table_set("gelu_and_others")
                    with act.Fori(0, XT // 2) as it:
                        for s in range(2):
                            act.wait_ge(z.xg_turned[s], it + 1)
                            act.wait_ge(z.h_done[s], it)
                            act.activation(xgT[s][:], bank[:, s, 0:D].rearrange("p (k t) -> p k t", k=KD), ACT.Copy)\
                               .then_inc(z.xgT_made[s], 1)
                        for s in range(2):
                            act.wait_ge(z.hid_made[s], it + 1)
                            act.wait_ge(z.glu_made[s], it)
                            act.activation(act_g[s][:], hid[s][:, F:2 * F], ACT.Gelu).then_inc(z.gelu_made[s], 1)
                        for s in range(2):
                            act.wait_ge(z.glu_turned[s], it + 1)
                            act.wait_ge(z.y_done[s], it)
                            act.activation(gluT[s][:], bank[:, 4 + s, 0:F].rearrange("p (k t) -> p k t", t=P), ACT.Copy)\
                               .then_inc(z.gluT_made[s], 1)

                @block.vector
                def _(dve):
                    with dve.Fori(0, XT // 2) as it:
                        e_no = [dve.value_load(tile_expert[0:1, ds(it * 2 + s, 1)], min_val=0, max_val=E - 1)
                                for s in range(2)]
                        for s in range(2):
                            dve.wait_ge(z.h_done[s], it + 1)
                            dve.wait_ge(z.glu_made[s], it)
                            dve.tensor_tensor(hid[s][:], bank[:, 2 + s, :], b1[:, ds(e_no[s] * (2 * F), 2 * F)],
                                              ALU.add).then_inc(z.hid_made[s], 1)
                        for s in range(2):
                            dve.wait_ge(z.gelu_made[s], it + 1)
                            dve.wait_ge(z.hid_made[s], it + 1)
                            dve.wait_ge(z.glu_turned[s], it)
                            dve.tensor_tensor(glu[s][:], hid[s][:, 0:F], act_g[s][:], ALU.mult).then_inc(z.glu_made[s], 1)
                        for s in range(2):
                            dve.wait_ge(z.y_done[s], it + 1)
                            dve.wait_ge(z.ye_stored[s], 16 * it)
                            dve.tensor_copy(ye[s][:], bank[:, 6 + s, 0:D]).then_inc(z.ye_made[s], 1)
            exp_part.close()
            end_phase()

            def sb(name, shape, dt=F32):
                return part.enter_context(nc.sbuf_tensor(name, shape, dt))

            KS = FS // P
            sw1 = sb("sw1", [P, KD, 2 * FS])
            sb1 = sb("sb1", [P, 2 * FS])
            sw2 = sb("sw2", [P, KS, D])
            smul = sb("smul", [P, KS])
            bias2 = sb("bias2", [E + 1, D])
            xm = [sb(f"xm{s}", [P, D]) for s in range(2)]
            xa = [sb(f"xa{s}", [P, D]) for s in range(2)]
            xaT = [sb(f"xaT{s}", [P, KD, P]) for s in range(2)]
            from_row = [sb(f"from_row{s}", [P, TOPK], I32) for s in range(2)]
            yg = [[sb(f"yg{s}_{k}", [P, D]) for k in range(TOPK)] for s in range(2)]
            shid = sb("shid", [P, 2 * FS])
            sgel = sb("sgel", [P, FS])
            sglu = sb("sglu", [P, FS])
            sgluT = [sb(f"sgluT{s}", [P, KS, P]) for s in range(2)]
            comb = [sb(f"comb{s}", [P, E + 1]) for s in range(2)]
            combT = [sb(f"combT{s}", [E + 1, P]) for s in range(2)]
            acc = [sb(f"acc{s}", [P, D]) for s in range(2)]
            s_loaded, s_scaled, comb_pad = sem("s_loaded"), sem("s_scaled"), sem("comb_pad")
            v = Memory()
            (v.xm_loaded, v.xa_loaded, v.fr_made, v.yg_loaded, v.xa_turned, v.xaT_made, v.h_done, v.hid_made, v.gelu_made,
             v.glu_made, v.glu_turned, v.gluT_made, v.c0, v.c1, v.comb_made, v.comb_turned, v.combT_made, v.o_done,
             v.a0, v.a1, v.a2, v.acc_made, v.stored) = [sems("v_" + n) for n in (
                 "xm", "xa", "fr", "yg", "xat", "xatm", "h", "hid", "gelu", "glu", "glut", "glutm", "c0", "c1", "cm",
                 "ct", "ctm", "od", "a0", "a1", "a2", "am", "st")]
            with nc.Block() as block:
                @block.sync
                def _(sp):
                    sp.dma_start(sw1[:], s_fc1_t.rearrange("(k p) f -> p k f", p=P)).then_inc(s_loaded, 16)
                    sp.dma_start(sb1[:], s_fc1_b.partition_broadcast(P)).then_inc(s_loaded, 16)
                    sp.dma_start(sw2[:], s_fc2_t.rearrange("(k p) f -> p k f", p=P)).then_inc(s_loaded, 16)
                    with nc.allow_non_contiguous_dma(reason="small constants, once"):
                        sp.dma_start(smul[:], s_mult.rearrange("(k p) -> p k", p=P)).then_inc(s_loaded, 16)
                    sp.dma_start(bias2[0:E, :], fc2_b).then_inc(s_loaded, 16)
                    sp.dma_start(bias2[E:E + 1, :], s_fc2_b.rearrange("(o d) -> o d", o=1)).then_inc(s_loaded, 16)
                    with sp.Fori(0, TILES // 2) as it:
                        for s in range(2):
                            here = ds((it * 2 + s) * P, P)
                            sp.wait_ge(v.a0[s], it)
                            sp.dma_start(xm[s][:], x_mid[here, :]).then_inc(v.xm_loaded[s], 16)
                            sp.wait_ge(v.xa_turned[s], it)
                            sp.dma_start(xa[s][:], x_norm[here, :]).then_inc(v.xa_loaded[s], 16)

                @block.gpsimd
                def _(pool):
                    with pool.Fori(0, TILES // 2) as it:
                        for s in range(2):
                            pool.wait_ge(v.yg_loaded[s], 48 * it)
                            pool.tensor_copy(from_row[s][:], row_i[:, ds(it * 2 + s, 1), :].rearrange("p o k -> p (o k)"))\
                                .then_inc(v.fr_made[s], 1)
                            pool.wait_ge(v.fr_made[s], it + 1)
                            pool.wait_ge(v.a2[s], it)
                            settle(pool)
                            for k in range(TOPK):
                                pool.indirect_dma_start(
                                    out=yg[s][k][:], out_offset=None, in_=row_out,
                                    in_offset=bass.IndirectOffsetOnAxis(ap=from_row[s][:, k:k + 1], axis=0))\
                                    .then_inc(v.yg_loaded[s], 16)

                @block.tensor
                def _(pe):
                    pe.wait_ge(s_loaded, 96)
                    pe.wait_ge(s_scaled, 1)
                    with pe.Fori(0, TILES // 2) as it:
                        for s in range(2):
                            pe.wait_ge(v.xa_loaded[s], 16 * (it + 1))
                            pe.wait_ge(v.xaT_made[s], it)
                            for k in range(KD):
                                last = pe.transpose(bank[:, s, k * P:(k + 1) * P], xa[s][:, k * P:(k + 1) * P], ident[:])
                            last.then_inc(v.xa_turned[s], 1)
                        for s in range(2):
                            pe.wait_ge(v.xaT_made[s], it + 1)
                            pe.wait_ge(v.hid_made[1 - s], it + s)
                            for c in range(2):
                                for k in range(KD):
                                    last = pe.matmul(bank[:, 2 + c, :], xaT[s][:, k, :], sw1[:, k, c * FS:(c + 1) * FS],
                                                     start=(k == 0), stop=(k == KD - 1))
                            last.then_inc(v.h_done[s], 1)
                        for s in range(2):
                            pe.wait_ge(v.comb_made[s], it + 1)
                            pe.wait_ge(v.acc_made[s], it)
                            pe.transpose(bank[0:E + 1, 6 + s, D:D + P], comb[s][:], ident[:]).then_inc(v.comb_turned[s], 1)
                            pe.wait_ge(v.glu_made[s], it + 1)
                            pe.wait_ge(v.gluT_made[s], it)
                            for k in range(KS):
                                last = pe.transpose(bank[:, 4 + s, k * P:(k + 1) * P], sglu[:, k * P:(k + 1) * P], ident[:])
                            last.then_inc(v.glu_turned[s], 1)
                            pe.wait_ge(v.combT_made[s], it + 1)
                            pe.wait_ge(v.gluT_made[s], it + 1)
                            pe.matmul(bank[:, 6 + s, 0:D], combT[s][:], bias2[:], start=True, stop=False)
                            for k in range(KS):
                                last = pe.matmul(bank[:, 6 + s, 0:D], sgluT[s][:, k, :], sw2[:, k, :],
                                                 start=False, stop=(k == KS - 1))
                            last.then_inc(v.o_done[s], 1)

                @block.scalar
                def _(act):
                    act.preload_act_table_set("gelu_and_others")
                    with act.Fori(0, TILES // 2) as it:
                        for s in range(2):
                            act.wait_ge(v.xa_turned[s], it + 1)
                            act.wait_ge(v.h_done[s], it)
                            act.activation(xaT[s][:], bank[:, s, 0:D].rearrange("p (k t) -> p k t", k=KD), ACT.Copy)\
                               .then_inc(v.xaT_made[s], 1)
                        for s in range(2):
                            act.wait_ge(v.hid_made[s], it + 1)
                            act.wait_ge(v.glu_made[1 - s], it + s)
                            act.activation(sgel[:], shid[:, FS:2 * FS], ACT.Gelu).then_inc(v.gelu_made[s], 1)
                            act.wait_ge(v.comb_turned[s], it + 1)
                            act.wait_ge(v.o_done[s], it)
                            act.activation(combT[s][:], bank[0:E + 1, 6 + s, D:D + P], ACT.Copy).then_inc(v.combT_made[s], 1)
                            act.wait_ge(v.glu_turned[s], it + 1)
                            act.activation(sgluT[s][:], bank[:, 4 + s, 0:FS].rearrange("p (k t) -> p k t", t=P), ACT.Copy)\
                               .then_inc(v.gluT_made[s], 1)
                        for s in range(2):
                            act.wait_ge(v.acc_made[s], it + 1)
                            act.dma_start(out_rows[ds((it * 2 + s) * P, P), :], acc[s][:]).then_inc(v.stored[s], 16)
                    for s in range(2):
                        act.wait_ge(v.stored[s], 16 * (TILES // 2))

                @block.vector
                def _(dve):
                    dve.wait_ge(s_loaded, 96)
                    dve.tensor_tensor(sw2[:], sw2[:], smul[:].unsqueeze(2).to_broadcast([P, KS, D]), ALU.mult)\
                       .then_inc(s_scaled, 1)
                    for s in range(2):
                        dve.memset(comb[s][:], 1.0).then_inc(comb_pad, 1)
                    dve.wait_ge(comb_pad, 2)
                    with dve.Fori(0, TILES // 2) as it:
                        for s in range(2):
                            hot = chosen[:, ds(it * 2 + s, 1), :, :].rearrange("p o k e -> p (o k) e")
                            wt = weight[:, ds(it * 2 + s, 1), :].rearrange("p o k -> p (o k)")
                            dve.wait_ge(v.comb_turned[s], it)
                            dve.tensor_scalar(comb[s][:, 0:E], hot[:, 0, :], wt[:, 0:1], None, ALU.mult).then_inc(v.c0[s], 1)
                            dve.wait_ge(v.c0[s], it + 1)
                            dve.scalar_tensor_tensor(comb[s][:, 0:E], hot[:, 1, :], wt[:, 1:2], comb[s][:, 0:E], ALU.mult,
                                                     ALU.add).then_inc(v.c1[s], 1)
                            dve.wait_ge(v.c1[s], it + 1)
                            dve.scalar_tensor_tensor(comb[s][:, 0:E], hot[:, 2, :], wt[:, 2:3], comb[s][:, 0:E], ALU.mult,
                                                     ALU.add).then_inc(v.comb_made[s], 1)
                        for s in range(2):
                            dve.wait_ge(v.h_done[s], it + 1)
                            dve.wait_ge(v.glu_made[1 - s], it + s)
                            dve.tensor_tensor(shid[:].rearrange("p (c f) -> p c f", c=2), bank[:, 2:4, :],
                                              sb1[:].rearrange("p (c f) -> p c f", c=2), ALU.add).then_inc(v.hid_made[s], 1)
                            dve.wait_ge(v.hid_made[s], it + 1)
                            dve.wait_ge(v.gelu_made[s], it + 1)
                            dve.wait_ge(v.glu_turned[1 - s], it + s)
                            dve.tensor_tensor(sglu[:], shid[:, 0:FS], sgel[:], ALU.mult).then_inc(v.glu_made[s], 1)
                        for s in range(2):
                            wt = weight[:, ds(it * 2 + s, 1), :].rearrange("p o k -> p (o k)")
                            dve.wait_ge(v.xm_loaded[s], 16 * (it + 1))
                            dve.wait_ge(v.yg_loaded[s], 48 * (it + 1))
                            dve.wait_ge(v.stored[s], 16 * it)
                            dve.scalar_tensor_tensor(acc[s][:], yg[s][0][:], wt[:, 0:1], xm[s][:], ALU.mult, ALU.add)\
                               .then_inc(v.a0[s], 1)
                            dve.wait_ge(v.a0[s], it + 1)
                            dve.scalar_tensor_tensor(acc[s][:], yg[s][1][:], wt[:, 1:2], acc[s][:], ALU.mult, ALU.add)\
                               .then_inc(v.a1[s], 1)
                            dve.wait_ge(v.a1[s], it + 1)
                            dve.scalar_tensor_tensor(acc[s][:], yg[s][2][:], wt[:, 2:3], acc[s][:], ALU.mult, ALU.add)\
                               .then_inc(v.a2[s], 1)
                            dve.wait_ge(v.a2[s], it + 1)
                            dve.wait_ge(v.o_done[s], it + 1)
                            dve.tensor_tensor(acc[s][:], acc[s][:], bank[:, 6 + s, 0:D], ALU.add).then_inc(v.acc_made[s], 1)


def kernel(**inputs):
    import numpy as np
    import concourse.bacc as bacc
    from concourse import mybir as _mybir
    from concourse.bass_utils import run_bass_kernel_spmd

    a = {k: np.asarray(v) for k, v in inputs.items()}
    laid = {
        "x": a["L0_attn_x"],
        "W_dt_t": a["L0_attn_W_dt"].T,
        "b_dt": a["L0_attn_b_dt"],
        "W_bc_t": np.concatenate([a["L0_attn_W_B"], a["L0_attn_W_C"]], axis=0).T,
        "A_log": a["L0_attn_A_log"],
        "D_param": a["L0_attn_D_param"],
        "gate_t": a["L0_ffn_gate_w"].T,
        "fc1_t": a["L0_ffn_fc1_w"].transpose(2, 0, 1),
        "fc1_b": a["L0_ffn_fc1_b"],
        "mult_t": a["L0_ffn_geglu_mult"].T,
        "fc2_t": a["L0_ffn_fc2_w"].transpose(2, 0, 1),
        "fc2_b": a["L0_ffn_fc2_b"],
        "s_fc1_t": a["L0_ffn_s_fc1_w"].T,
        "s_fc1_b": a["L0_ffn_s_fc1_b"],
        "s_mult": a["L0_ffn_s_geglu_mult"],
        "s_fc2_t": a["L0_ffn_s_fc2_w"].T,
        "s_fc2_b": a["L0_ffn_s_fc2_b"],
    }
    nc = bacc.Bacc("TRN2", target_bir_lowering=False, num_devices=1)
    arrays, args = {}, {}
    for name, value in laid.items():
        value = np.ascontiguousarray(value)
        arrays["in_" + name] = value
        args[name] = nc.dram_tensor("in_" + name, value.shape, _mybir.dt.from_np(value.dtype), kind="ExternalInput").ap()
    shape = a["L0_attn_x"].shape
    args["out"] = nc.dram_tensor("out_0", shape, _mybir.dt.float32, kind="ExternalOutput").ap()
    model_kernel(nc, **args)
    r = run_bass_kernel_spmd(nc, [arrays], core_ids=[0])
    return r.results[0]["out_0"]
```

```python
from contextlib import ExitStack

import concourse.bass as bass
from concourse import mybir

F32 = mybir.dt.float32
I32 = mybir.dt.int32
U32 = mybir.dt.uint32
BF16 = mybir.dt.bfloat16
ALU = mybir.AluOpType
ACT = mybir.ActivationFunctionType
AX = mybir.AxisListType
ds = bass.ds

P = 128
EPS = 1e-5
DT_MID, DT_HALF = (0.1 + 0.001) / 2.0, (0.1 - 0.001) / 2.0
SHARP = 0.5
A_HALF = 5.0
DA_HALF = 8.0
NORM_MAX = 20.0
NORM2_SURE = 399.9
SEG = 10
TOPK = 3
SLOTS = 4
SLOTS_LOG = 2


class Memory:
    pass


def model_kernel(nc, x, W_dt_t, b_dt, W_bc_t, A_log, D_param, gate_t, fc1_t, fc1_b, mult_t, fc2_t,
                 fc2_b, s_fc1_t, s_fc1_b, s_mult, s_fc2_t, s_fc2_b, out):
    NB, T, D = x.shape
    N = A_log.shape[1]
    E, F = mult_t.shape[1], mult_t.shape[0]
    FS = s_mult.shape[0]
    TOK = NB * T
    TILES = TOK // P
    KD = D // P
    XT = TOK * TOPK // P + E
    XT += -XT % 8
    R = KD * N
    NSEG = T // SEG
    TAIL = T - NSEG * SEG
    NORMS = -(-T // SEG)
    Q = 32

    GT = 4
    GROUPS = TILES // GT

    def group_rows(t, g):
        return t[ds(g * (GT * P), GT * P), :].rearrange("(i p) d -> p i d", p=P)

    x_rows = x.rearrange("b t d -> (b t) d")
    out_rows = out.rearrange("b t d -> (b t) d")
    x_skip = nc.dram_tensor("x_skip", (TOK, D), F32, kind="Internal").ap()
    x_mid = nc.dram_tensor("x_mid", (TOK, D), F32, kind="Internal").ap()
    x_norm = nc.dram_tensor("x_norm", (TOK, D), F32, kind="Internal").ap()
    row_choice = nc.dram_tensor("row_choice", (XT * P, 1), F32, kind="Internal").ap()
    choice_out = nc.dram_tensor("choice_out", (TOK * SLOTS + XT * P, D), F32, kind="Internal").ap()

    with ExitStack() as ctx:
        def sb(name, shape, dt=F32):
            return ctx.enter_context(nc.sbuf_tensor(name, shape, dt))

        phase_sems = []
        phase_no = [0]

        def sem(name):
            phase_sems.append(nc.alloc_semaphore(f"{name}_of{phase_no[0]}"))
            return phase_sems[-1]

        passed = ctx.enter_context(nc.semaphore("passed"))

        def settle(eng):
            eng.sem_inc(passed, 1)

        def wait(eng, signal, count):
            if not isinstance(count, int) or count > 0:
                eng.wait_ge(signal, count)

        def rounds(eng, n, body):
            body(0)
            with eng.Fori(1, n) as i:
                body(i)

        def steps(eng, n, body, unroll):
            rounds = n // unroll
            for c in range(unroll):
                body(0, c, c)
            with eng.Fori(1, rounds - 1) as it:
                for c in range(unroll):
                    body(it, c, it * unroll + c)
            for c in range(unroll):
                body(rounds - 1, c, (rounds - 1) * unroll + c)

        def end_phase():
            nc.clear_and_free_semaphores(list(phase_sems))
            phase_sems.clear()
            phase_no[0] += 1
            nc.all_engine_barrier()

        def sems(name, n=2):
            return [sem(f"{name}{i}") for i in range(n)]

        bank = ctx.enter_context(nc.psum_tensor("bank", [P, 8, 512], F32))

        arena_x = sb("arena_x", [P, KD * TOK])
        arena_dt = sb("arena_dt", [P, KD * TOK])
        xT = arena_x[:, :].rearrange("p (k t) -> p k t", k=KD)
        dtT = arena_dt[:, :].rearrange("p (k t) -> p k t", k=KD)
        w1 = arena_dt[:, 0:KD * E * 2 * F].rearrange("p (k e f) -> p k (e f)", k=KD, e=E)
        w2 = arena_x[:, 0:KD * E * D].rearrange("p (k e f) -> p k (e f)", k=KD, e=E)
        b1 = arena_x[:, KD * E * D:KD * E * D + E * 2 * F]

        ident = sb("ident", [P, P])
        ones = sb("ones", [P, P])
        minus_half = sb("minus_half", [P, 1])
        half = sb("half", [P, 8])
        expert_no = sb("expert_no", [P, E])
        out_of_bounds = sb("out_of_bounds", [P, 1], I32)

        with ExitStack() as part:
            def sb(name, shape, dt=F32):
                return part.enter_context(nc.sbuf_tensor(name, shape, dt))

            a_neg = sb("a_neg", [P, KD, N])
            pick = sb("pick", [3 * Q, N, P], BF16)
            pick_c = sb("pick_c", [3 * Q, N], BF16)
            bc3 = sb("bc3", [3 * Q, TOK], BF16)
            c_tok = sb("c_tok", [P, TILES, N])
            iota_i = sb("iota_i", [P, E], I32)
            in_bounds = sb("in_bounds", [P, NORMS])
            weights_part = ExitStack()

            def sb(name, shape, dt=F32):
                return weights_part.enter_context(nc.sbuf_tensor(name, shape, dt))

            wdt = sb("wdt", [P, KD, D])
            wbc = sb("wbc", [P, KD, 3 * Q])
            dbc = sb("dbc", [P, D])
            bdt = sb("bdt", [P, KD])
            tanh_bias = sb("tanh_bias", [P, 1])
            one_col = sb("one_col", [P, 1])
            pick_f = sb("pick_f", [3 * Q, Q])
            load_part = ExitStack()

            def sb(name, shape, dt=F32):
                return load_part.enter_context(nc.sbuf_tensor(name, shape, dt))

            xin = [sb(f"xin{c}", [P, GT, D]) for c in range(4)]
            xn = [sb(f"xn{s}", [P, GT, D]) for s in range(2)]
            skip = [sb(f"skip{s}", [P, GT, D]) for s in range(2)]
            stats = [sb(f"stats{s}", [P, GT, 6]) for s in range(2)]
            meanvar = [sb(f"meanvar{s}", [P, GT, 2]) for s in range(2)]
            rstd = [sb(f"rstd{s}", [P, GT]) for s in range(2)]

            c_loaded = sem("c_loaded")
            c_made = sem("c_made")
            c_a = sem("c_a")
            x_loaded, skip_stored = sems("x_loaded", 4), sems("skip_stored")
            (stats_made, aggregated, eps_added, rstd_made, xn_made, xn_turned, xT_written, dx_made,
             skip_made) = [sem(n) for n in (
                 "stats_made", "aggregated", "eps_added", "rstd_made", "xn_made", "xn_turned", "xT_written", "dx_made",
                 "skip_made")]

            with nc.Block() as block:
                @block.sync
                def _(sp):
                    sp.dma_start(wdt[:], W_dt_t.rearrange("(k p) e -> p k e", p=P)).then_inc(c_loaded, 16)
                    sp.wait_ge(c_made, 1)
                    for q in range(3):
                        for k in range(KD):
                            sp.dma_start(wbc[:, k, q * Q:q * Q + 2 * N], W_bc_t[k * P:(k + 1) * P, :])\
                              .then_inc(c_loaded, 16)
                    sp.dma_start(dbc[:], D_param.partition_broadcast(P)).then_inc(c_loaded, 16)
                    with nc.allow_non_contiguous_dma(reason="small constants, once"):
                        sp.dma_start(bdt[:], b_dt.rearrange("(k p) -> p k", p=P)).then_inc(c_loaded, 16)
                    sp.dma_start(a_neg[:], A_log.rearrange("(k p) n -> p k n", p=P)).then_inc(c_loaded, 16)

                    def load(it, c, g):
                        wait(sp, xn_made, g - 3)
                        wait(sp, skip_made, g - 3)
                        sp.dma_start(xin[c][:], group_rows(x_rows, g)).then_inc(x_loaded[c], 16)
                    steps(sp, GROUPS, load, 4)

                @block.gpsimd
                def _(pool):
                    pool.memset(wbc[:], 0.0).then_inc(c_made, 1)
                    pool.memset(ident[:], 0.0).then_inc(c_made, 1)
                    pool.memset(pick_f[:], 0.0).then_inc(c_made, 1)
                    pool.memset(ones[:], 1.0).then_inc(c_made, 1)
                    pool.memset(minus_half[:], -0.5).then_inc(c_made, 1)
                    pool.memset(half[:], 0.5).then_inc(c_made, 1)
                    pool.memset(tanh_bias[:], -DT_MID * SHARP / (DT_HALF + 1e-8)).then_inc(c_made, 1)
                    pool.memset(one_col[:], 1.0).then_inc(c_made, 1)
                    pool.iota(iota_i[:], pattern=[[1, E]], base=0, channel_multiplier=0).then_inc(c_made, 1)
                    pool.wait_ge(c_made, 9)
                    pool.affine_select(out=ident[:], in_=ident[:], compare_op=ALU.not_equal, fill=1.0,
                                       base=0, pattern=[[-1, P]], channel_multiplier=1).then_inc(c_made, 1)
                    for q in range(3):
                        pool.affine_select(out=pick_f[:], in_=pick_f[:], compare_op=ALU.not_equal, fill=1.0,
                                           base=-q * Q, pattern=[[-1, Q]], channel_multiplier=1).then_inc(c_made, 1)
                        pool.wait_ge(c_made, 11 + q)
                    pool.tensor_copy(expert_no[:], iota_i[:]).then_inc(c_made, 1)
                    pool.tensor_copy(pick[:], pick_f[:, 0:N].unsqueeze(2).to_broadcast([3 * Q, N, P]))\
                        .then_inc(c_made, 1)
                    pool.tensor_copy(pick_c[:], pick_f[:, N:2 * N]).then_inc(c_made, 1)

                    def skip_rows(g, c):
                        s = c % 2
                        pool.wait_ge(xn_made, g + 1)
                        if not isinstance(g, int) or g > 1:
                            pool.wait_ge(skip_stored[s], (g - s) * 8)
                        pool.tensor_tensor(skip[s][:], xn[s][:], dbc[:].unsqueeze(1).to_broadcast([P, GT, D]), ALU.mult)\
                            .then_inc(dx_made, 1)
                        pool.wait_ge(dx_made, g + 1)
                        pool.tensor_tensor(skip[s][:], skip[s][:], xin[c][:], ALU.add).then_inc(skip_made, 1)

                    pool.wait_ge(c_loaded, 160)

                    def step(it, c, g):
                        s = c % 2
                        pool.wait_ge(aggregated, g + 1)
                        wait(pool, xn_made, g - 1)
                        settle(pool)
                        pool.tensor_scalar(rstd[s][:], meanvar[s][:, :, 1], EPS, None, ALU.add).then_inc(eps_added, 1)
                        pool.wait_ge(eps_added, g + 1)
                        pool.tensor_tensor(rstd[s][:], rstd[s][:], minus_half[:].to_broadcast([P, GT]), ALU.pow)\
                            .then_inc(rstd_made, 1)
                        if not isinstance(g, int) or g > 0:
                            skip_rows(g - 1, (c - 1) % 4)
                    steps(pool, GROUPS, step, 4)
                    skip_rows(GROUPS - 1, 3)

                @block.vector
                def _(dve):
                    def measure(g, c):
                        s = c % 2
                        dve.wait_ge(x_loaded[c], (g - c) * 4 + 16)
                        wait(dve, aggregated, g - 1)
                        settle(dve)
                        for i in range(GT):
                            dve.bn_stats(stats[s][:, i, :], xin[c][:, i, :]).then_inc(stats_made, 1)
                        dve.wait_ge(stats_made, GT * (g + 1))
                        wait(dve, rstd_made, g - 1)
                        settle(dve)
                        for i in range(GT):
                            last = dve.bn_aggr(meanvar[s][:, i, :], stats[s][:, i, :])
                        last.then_inc(aggregated, 1)

                    measure(0, 0)

                    def step(it, c, g):
                        s = c % 2
                        if not isinstance(g, int) or g + 1 < GROUPS:
                            measure(g + 1, (c + 1) % 4)
                        dve.wait_ge(rstd_made, g + 1)
                        dve.wait_ge(aggregated, g + 1)
                        wait(dve, xn_turned, g - 1)
                        wait(dve, skip_made, g - 1)
                        settle(dve)
                        for i in range(GT):
                            last = dve.tensor_scalar(xn[s][:, i, :], xin[c][:, i, :], meanvar[s][:, i, 0:1],
                                                     rstd[s][:, i:i + 1], ALU.subtract, ALU.mult)
                        last.then_inc(xn_made, 1)
                    steps(dve, GROUPS, step, 4)

                @block.tensor
                def _(pe):
                    pe.wait_ge(c_made, 16)

                    def pair(it):
                        for s in range(2):
                            g = it * 2 + s
                            pe.wait_ge(xn_made, g + 1)
                            wait(pe, xT_written, g - 1)
                            for k in range(KD):
                                for i in range(GT):
                                    last = pe.transpose(bank[:, 2 * s + k, i * P:(i + 1) * P],
                                                        xn[s][:, i, k * P:(k + 1) * P], ident[:])
                            last.then_inc(xn_turned, 1)
                    rounds(pe, GROUPS // 2, pair)

                @block.scalar
                def _(act):
                    act.wait_ge(c_loaded, 160)
                    act.activation(a_neg[:], a_neg[:], ACT.Tanh, scale=SHARP / (A_HALF + 1e-8)).then_inc(c_a, 1)
                    act.wait_ge(c_a, 1)
                    act.activation(a_neg[:], a_neg[:], ACT.Exp, scale=A_HALF / SHARP).then_inc(c_a, 1)
                    act.wait_ge(c_a, 2)
                    act.mul(a_neg[:], a_neg[:], -SHARP / (DA_HALF + 1e-8)).then_inc(c_a, 1)
                    act.wait_ge(c_a, 3)

                    def store(g, s):
                        act.wait_ge(skip_made, g + 1)
                        act.dma_start(group_rows(x_skip, g), skip[s][:]).then_inc(skip_stored[s], 16)

                    def pair(it):
                        for s in range(2):
                            g = it * 2 + s
                            act.wait_ge(xn_turned, g + 1)
                            act.activation(xT[:, :, ds(g * (GT * P), GT * P)], bank[:, 2 * s:2 * s + 2, :],
                                           ACT.Copy).then_inc(xT_written, 1)
                            if not isinstance(g, int) or g > 0:
                                store(g - 1, 1 - s)
                    rounds(act, GROUPS // 2, pair)
                    store(GROUPS - 1, 1)
                    for s in range(2):
                        act.wait_ge(skip_stored[s], 8 * GROUPS)
            load_part.close()
            end_phase()

            proj_part = ExitStack()

            def sb(name, shape, dt=F32):
                return proj_part.enter_context(nc.sbuf_tensor(name, shape, dt))

            CH = 512
            NCH = TOK // CH
            mag = [sb(f"mag{s}", [P, KD, CH]) for s in range(2)]
            pos = [sb(f"pos{s}", [P, KD, CH]) for s in range(2)]
            top = [sb(f"top{s}", [3 * Q, CH], BF16) for s in range(2)]
            rest = [sb(f"rest{s}", [3 * Q, CH]) for s in range(2)]
            mid = [sb(f"mid{s}", [3 * Q, CH], BF16) for s in range(2)]
            (projected, mag_made, e_made, l_made, pos_made, sp_made, top_made, rest_made, mid_made,
             parts_made, c_turned, c_made2) = [sem(n) for n in (
                 "projected", "mag_made", "e_made", "l_made", "pos_made", "sp_made", "top_made", "rest_made",
                 "mid_made", "parts_made", "c_turned", "c_made2")]
            tanh_made, dt_made, g_made = sem("tanh_made"), sem("dt_made"), sem("g_made")
            NG = 8
            GW = KD * TOK // NG
            with nc.Block() as block:
                @block.tensor
                def _(pe):
                    def project(it):
                        for s in range(2):
                            j = it * 2 + s
                            here = ds(j * CH, CH)
                            wait(pe, mag_made, j - 1)
                            wait(pe, rest_made, j - 1)
                            for e in range(KD):
                                for k in range(KD):
                                    pe.matmul(bank[:, 3 * s + e, :], wdt[:, k, e * P:(e + 1) * P],
                                              xT[:, k, here], start=(k == 0), stop=(k == KD - 1))
                            for k in range(KD):
                                last = pe.matmul(bank[0:3 * Q, 3 * s + 2, :], wbc[:, k, :], xT[:, k, here],
                                                 start=(k == 0), stop=(k == KD - 1))
                            last.then_inc(projected, 1)

                    def turn_c(j, s):
                        pe.wait_ge(parts_made, 3 * (j + 1))
                        wait(pe, c_made2, j - 1)
                        for i in range(CH // P):
                            last = pe.matmul(bank[:, 6 + s, i * N:(i + 1) * N], bc3[:, ds(j * CH + i * P, P)],
                                             pick_c[:], start=True, stop=True)
                        last.then_inc(c_turned, 1)

                    project(0)
                    project(1)
                    for s in range(2):
                        turn_c(s, s)
                    with pe.Fori(2, NCH // 2) as it:
                        project(it)
                        for s in range(2):
                            turn_c(it * 2 - 2 + s, s)
                    for s in range(2):
                        turn_c(NCH - 2 + s, s)

                @block.scalar
                def _(act):
                    act.preload_act_table_set("natural_log_exp_and_others")

                    def body(it):
                        for s in range(2):
                            j = it * 2 + s
                            act.wait_ge(pos_made, j + 1)
                            wait(act, sp_made, j - 1)
                            for e in range(KD):
                                last = act.activation(mag[s][:, e, :], bank[:, 3 * s + e, :], ACT.Abs,
                                                      bias=bdt[:, e:e + 1])
                            last.then_inc(mag_made, 1)
                            wait(act, parts_made, 3 * (j - 1))
                            act.activation(top[s][:], bank[0:3 * Q, 3 * s + 2, :], ACT.Copy).then_inc(top_made, 1)
                            act.wait_ge(mag_made, j + 1)
                            act.activation(mag[s][:], mag[s][:], ACT.Exp, scale=-1.0).then_inc(e_made, 1)
                            act.wait_ge(e_made, j + 1)
                            act.activation(mag[s][:], mag[s][:], ACT.Ln, bias=one_col[:, 0:1]).then_inc(l_made, 1)
                            act.wait_ge(rest_made, j + 1)
                            act.activation(mid[s][:], rest[s][:], ACT.Copy).then_inc(mid_made, 1)
                    rounds(act, NCH // 2, body)
                    act.wait_ge(sp_made, NCH)

                    def tanh_part(i):
                        part_i = arena_dt[:, ds(i * GW, GW)]
                        act.activation(part_i, part_i, ACT.Tanh, bias=tanh_bias[:, 0:1],
                                       scale=SHARP / (DT_HALF + 1e-8)).then_inc(tanh_made, 1)
                    with act.Fori(0, NG) as i:
                        tanh_part(i)

                @block.vector
                def _(dve):
                    def body(it):
                        for s in range(2):
                            j = it * 2 + s
                            dve.wait_ge(projected, j + 1)
                            wait(dve, sp_made, j - 1)
                            for e in range(KD):
                                last = dve.tensor_scalar(pos[s][:, e, :], bank[:, 3 * s + e, :], bdt[:, e:e + 1],
                                                         0.0, ALU.add, ALU.max)
                            last.then_inc(pos_made, 1)
                            dve.wait_ge(top_made, j + 1)
                            dve.tensor_tensor(rest[s][:], bank[0:3 * Q, 3 * s + 2, :], top[s][:],
                                              ALU.subtract).then_inc(rest_made, 1)
                        for s in range(2):
                            j = it * 2 + s
                            dve.wait_ge(mid_made, j + 1)
                            dve.wait_ge(rest_made, j + 1)
                            dve.tensor_copy(bc3[0:Q, ds(j * CH, CH)], top[s][0:Q, :]).then_inc(parts_made, 1)
                            dve.tensor_copy(bc3[Q:2 * Q, ds(j * CH, CH)], mid[s][Q:2 * Q, :]).then_inc(parts_made, 1)
                            dve.tensor_tensor(bc3[2 * Q:3 * Q, ds(j * CH, CH)], rest[s][2 * Q:3 * Q, :],
                                              mid[s][2 * Q:3 * Q, :], ALU.subtract).then_inc(parts_made, 1)
                            wait(dve, c_turned, j - 1)
                            if not isinstance(j, int) or j >= 2:
                                dve.tensor_copy(c_tok[:, ds((j - 2) * (CH // P), CH // P), :],
                                                bank[:, 6 + s, 0:CH // P * N].rearrange("p (i n) -> p i n", n=N))\
                                   .then_inc(c_made2, 1)
                    rounds(dve, NCH // 2, body)
                    for s in range(2):
                        j = NCH - 2 + s
                        dve.wait_ge(c_turned, j + 1)
                        dve.tensor_copy(c_tok[:, j * (CH // P):(j + 1) * (CH // P), :],
                                        bank[:, 6 + s, 0:CH // P * N].rearrange("p (i n) -> p i n", n=N))\
                           .then_inc(c_made2, 1)
                    with dve.Fori(0, NG) as i:
                        part_i = arena_dt[:, ds(i * GW, GW)]
                        x_i = arena_x[:, ds(i * GW, GW)]
                        dve.wait_ge(tanh_made, i + 1)
                        dve.tensor_scalar(part_i, part_i, DT_HALF / SHARP, DT_MID, ALU.mult,
                                          ALU.add).then_inc(dt_made, 1)
                        dve.wait_ge(dt_made, i + 1)
                        dve.tensor_tensor(x_i, x_i, part_i, ALU.mult).then_inc(g_made, 1)

                @block.gpsimd
                def _(pool):
                    def body(it):
                        for s in range(2):
                            j = it * 2 + s
                            pool.wait_ge(pos_made, j + 1)
                            pool.wait_ge(l_made, j + 1)
                            pool.tensor_tensor(dtT[:, :, ds(j * CH, CH)], pos[s][:], mag[s][:], ALU.add)\
                                .then_inc(sp_made, 1)
                    rounds(pool, NCH // 2, body)
            proj_part.close()
            end_phase()

            weights_part.close()
            gT = arena_x[:, :].rearrange("p (k b t) -> p k b t", k=KD, b=NB)
            dtT4 = arena_dt[:, :].rearrange("p (k b t) -> p k b t", k=KD, b=NB)
            bc3v = bc3[:, :].rearrange("r (b t) -> r b t", b=NB)

            fast_part = ExitStack()

            def sb(name, shape, dt=F32):
                return fast_part.enter_context(nc.sbuf_tensor(name, shape, dt))

            TB = T // P
            PAIRS = TB // 2
            TH = T // 2
            decay = [sb(f"decay{s}", [P, KD, T]) for s in range(2)]
            state = [sb(f"state{s}", [P, KD, T]) for s in range(2)]
            b_all = [[sb(f"b_all{s}_{hf}", [P, TH]) for hf in range(2)] for s in range(2)]
            sq = [sb(f"state_sq{s}", [P, KD, NORMS]) for s in range(2)]
            y_acc = [sb(f"y_acc{s}", [P, TB, D]) for s in range(2)]
            all_in = sb("all_in", [P, 1])
            tanh_made, decay_made, b_spread, b_copied, u_made = (
                sem("z_tanh"), sem("decay_made"), sem("b_spread"), sem("b_copied"), sem("u_made"))
            scanned, turned, y_added, sq_made, sq_summed = (
                sem("scanned"), sem("turned"), sem("y_added"), sem("sq_made"), sem("sq_summed"))
            norms_checked, bounds_clear, checked = sem("norms_checked"), sem("bounds_clear"), sem("checked")
            acc_loaded, acc_stored = sems("acc_loaded"), sems("acc_stored")
            UNITS = NB * N

            with nc.Block() as block:
                def units(eng, body):
                    def pair(it):
                        for bs in range(2):
                            for n in range(N):
                                body(it * 2 + bs, bs, n, it * (2 * N) + bs * N + n)
                    rounds(eng, NB // 2, pair)

                @block.scalar
                def _(act):
                    act.preload_act_table_set("exp_and_others")

                    def body(b, bs, n, j):
                        s = n % 2
                        for hf in range(2):
                            act.wait_ge(b_spread, 2 * j + hf + 1)
                            wait(act, u_made, 2 * (j - 2) + hf + 1)
                            act.activation(b_all[s][hf][:], bank[:, hf, :], ACT.Copy).then_inc(b_copied, 1)
                        wait(act, scanned, j - 1)
                        settle(act)
                        for k in range(KD):
                            last = act.activation(decay[s][:, k, :],
                                                  dtT4[:, k, ds(b, 1), :].rearrange("p o t -> p (o t)"),
                                                  ACT.Tanh, scale=a_neg[:, k, n:n + 1])
                        last.then_inc(tanh_made, 1)
                        act.wait_ge(tanh_made, j + 1)
                        act.activation(decay[s][:], decay[s][:], ACT.Exp, scale=DA_HALF / SHARP)\
                           .then_inc(decay_made, 1)
                    units(act, body)

                @block.gpsimd
                def _(pool):
                    def square(n, j):
                        s = n % 2
                        pool.wait_ge(scanned, j + 1)
                        wait(pool, sq_summed, j - 1)
                        at_norms = state[s][:, :, 0:T:SEG]
                        pool.tensor_tensor(sq[s][:], at_norms, at_norms, ALU.mult).then_inc(sq_made, 1)

                    def body(b, bs, n, j):
                        s = n % 2
                        for hf in range(2):
                            pool.wait_ge(b_copied, 2 * j + hf + 1)
                            if hf == 0:
                                wait(pool, turned, PAIRS * (j - 1))
                                wait(pool, sq_made, j - 1)
                            settle(pool)
                            pool.tensor_tensor(
                                state[s][:, :, hf * TH:(hf + 1) * TH],
                                gT[:, :, ds(b, 1), hf * TH:(hf + 1) * TH].rearrange("p k o t -> p k (o t)"),
                                b_all[s][hf][:].unsqueeze(1).to_broadcast([P, KD, TH]), ALU.mult).then_inc(u_made, 1)
                        if not isinstance(j, int) or j > 0:
                            square(n + N - 1, j - 1)
                    units(pool, body)
                    square(N - 1, UNITS - 1)

                @block.tensor
                def _(pe):
                    def spread(b, n, j):
                        for hf in range(2):
                            wait(pe, b_copied, 2 * (j - 1) + hf + 1)
                            pe.matmul(bank[:, hf, :], pick[:, n, :],
                                      bc3v[:, ds(b, 1), hf * TH:(hf + 1) * TH].rearrange("r o t -> r (o t)"),
                                      start=True, stop=True).then_inc(b_spread, 1)

                    def turn(n, j):
                        s = n % 2
                        pe.wait_ge(scanned, j + 1)
                        for p in range(PAIRS):
                            wait(pe, y_added, PAIRS * (j - 1) + p + 1)
                            settle(pe)
                            for i in range(2):
                                for k in range(KD):
                                    t0 = (2 * p + i) * P
                                    last = pe.transpose(bank[:, 2 + p, i * D + k * P:i * D + (k + 1) * P],
                                                        state[s][:, k, t0:t0 + P], ident[:])
                            last.then_inc(turned, 1)

                    def add_squares(b, bs, n, j):
                        pe.wait_ge(sq_made, j + 1)
                        if n == 0:
                            wait(pe, norms_checked, b - 1)
                            settle(pe)
                        for k in range(KD):
                            last = pe.matmul(bank[:, 6 + bs, 0:NORMS], ones[:], sq[n % 2][:, k, :],
                                             start=(n == 0 and k == 0), stop=(n == N - 1 and k == KD - 1))
                        last.then_inc(sq_summed, 1)

                    spread(0, 0, 0)
                    spread(0, 1, 1)

                    def body(b, bs, n, j):
                        if not isinstance(j, int) or j + 2 < UNITS:
                            spread(b + (n + 2) // N, (n + 2) % N, j + 2)
                        turn(n, j)
                        if not isinstance(j, int) or j > 0:
                            if n == 0:
                                add_squares(b - 1, 1 - bs, N - 1, j - 1)
                            else:
                                add_squares(b, bs, n - 1, j - 1)

                    for j in range(2 * N):
                        body(j // N, j // N, j % N, j)
                    with pe.Fori(1, NB // 2 - 1) as it:
                        for i in range(2 * N):
                            body(it * 2 + i // N, i // N, i % N, it * (2 * N) + i)
                    for j in range(UNITS - 2 * N, UNITS):
                        body(j // N, j // N % 2, j % N, j)
                    add_squares(NB - 1, 1, N - 1, UNITS - 1)

                @block.vector
                def _(dve):
                    dve.memset(in_bounds[:], 1.0).then_inc(bounds_clear, 1)
                    dve.wait_ge(bounds_clear, 1)

                    def check(b, bs):
                        dve.wait_ge(sq_summed, (b + 1) * N)
                        settle(dve)
                        dve.scalar_tensor_tensor(in_bounds[:], bank[:, 6 + bs, 0:NORMS], NORM2_SURE, in_bounds[:],
                                                 ALU.is_le, ALU.min).then_inc(norms_checked, 1)
                        dve.wait_ge(norms_checked, b + 1)

                    def add_y(b, bs, n, j):
                        s = n % 2
                        if n == 0:
                            dve.wait_ge(acc_loaded[bs], (b - bs) * 8 + 16)
                        for p in range(PAIRS):
                            dve.wait_ge(turned, PAIRS * j + p + 1)
                            wait(dve, y_added, PAIRS * (j - 1) + p + 1)
                            for i in range(2):
                                block_no = 2 * p + i
                                last = dve.scalar_tensor_tensor(
                                    y_acc[bs][:, block_no, :], bank[:, 2 + p, i * D:(i + 1) * D],
                                    c_tok[:, ds(b * TB + block_no, 1), n:n + 1].rearrange("p o n -> p (o n)"),
                                    y_acc[bs][:, block_no, :], ALU.mult, ALU.add)
                            last.then_inc(y_added, 1)

                    def body(b, bs, n, j):
                        s = n % 2
                        dve.wait_ge(decay_made, j + 1)
                        dve.wait_ge(u_made, 2 * j + 2)
                        for k in range(KD):
                            last = dve.tensor_tensor_scan(state[s][:, k, :], decay[s][:, k, :], state[s][:, k, :],
                                                          0.0, ALU.mult, ALU.add)
                        last.then_inc(scanned, 1)
                        if n == 2 and (not isinstance(j, int) or b > 0):
                            check(b - 1, 1 - bs)
                        if not isinstance(j, int) or j > 0:
                            if n == 0:
                                add_y(b - 1, 1 - bs, N - 1, j - 1)
                            else:
                                add_y(b, bs, n - 1, j - 1)
                    units(dve, body)
                    add_y(NB - 1, 1, N - 1, UNITS - 1)
                    check(NB - 1, 1)
                    dve.tensor_reduce(all_in[:], in_bounds[:], AX.X, ALU.min).then_inc(checked, 1)
                    dve.wait_ge(checked, 1)
                    dve.tensor_scalar(out_of_bounds[:], all_in[:], 0.5, None, ALU.is_lt).then_inc(checked, 1)
                    dve.wait_ge(checked, 2)

                @block.sync
                def _(sp):
                    def rows_of(t, b):
                        return t[ds(b * T, T), :].rearrange("(i p) d -> p i d", p=P)

                    def load(b, bs, earlier):
                        if earlier:
                            sp.wait_ge(acc_stored[bs], (b - bs) * 8)
                        sp.dma_start(y_acc[bs][:], rows_of(x_skip, b)).then_inc(acc_loaded[bs], 16)

                    def store(b, bs):
                        sp.wait_ge(y_added, (b + 1) * (N * PAIRS))
                        sp.dma_start(rows_of(x_mid, b), y_acc[bs][:]).then_inc(acc_stored[bs], 16)

                    load(0, 0, False)
                    load(1, 1, False)
                    store(0, 0)
                    with sp.Fori(1, NB // 2) as it:
                        load(it * 2, 0, True)
                        store(it * 2 - 1, 1)
                        load(it * 2 + 1, 1, True)
                        store(it * 2, 0)
                    store(NB - 1, 1)
                    for bs in range(2):
                        sp.wait_ge(acc_stored[bs], 16 * (NB // 2))
            fast_part.close()
            end_phase()

            rescaled = nc.values_load(out_of_bounds[0:1, 0:1], min_val=0, max_val=1)
            with nc.If(rescaled > 0):
                nc.all_engine_barrier()
                scan_part = ExitStack()

                def sb(name, shape, dt=F32):
                    return scan_part.enter_context(nc.sbuf_tensor(name, shape, dt))

                W = R * NB
                dA = [sb(f"dA{s}", [P, W * SEG]) for s in range(2)]
                u = sb("u", [P, W * SEG])
                h = sb("h", [P, W * SEG])
                hc = sb("hc", [P, W * SEG])
                t1 = sb("t1", [P, W])
                h0 = sb("h0", [P, W])
                sq = sb("sq", [P, W])
                h_last = sb("h_last", [P, W])
                norm2 = sb("norm2", [P, NB])
                norm = sb("norm", [P, NB])
                scale = sb("scale", [P, NB])

                z_made, tanh_z, dA_made, scanned = sems("z_made"), sems("tanh_z"), sems("dA_made"), sems("scanned")
                b_spread, c_spread, u_made, hc_made = sem("b_spread"), sem("c_spread"), sem("u_made"), sem("hc_made")
                decayed, h0_made, sq_made, sq_summed = sem("decayed"), sem("h0_made"), sem("sq_made"), sem("sq_summed")
                norm2_made, norm_made, eps_in, inv_made = sem("norm2_made"), sem("norm_made"), sem("eps_in"), sem("inv_made")
                scale_made, h0_in, dA_cut, y_made, last_kept = (sem("scale_made"), sem("h0_in"), sem("dA_cut"),
                                                                 sem("y_made"), sem("last_kept"))
                first_state, pick_made = sem("first_state"), sem("pick_made")
                pick_c_all = sb("pick_c_all", [3 * Q, N, P], BF16)

                def rows(buf, L):
                    return buf[:, 0:W * L].rearrange("p (k n b t) -> p k n b t", k=KD, n=N, b=NB)

                def flat_rows(buf, L):
                    return buf[:, 0:W * L].rearrange("p (r b t) -> p r b t", r=R, b=NB)

                HN = N // 2

                def spread(half_no, first_bank, L):
                    return bank[:, first_bank + half_no, 0:HN * NB * L].rearrange("p (n b t) -> p n b t", n=HN, b=NB)

                with nc.Block() as block:
                    def segments(eng, body):
                        def pair(it):
                            for s in range(2):
                                body(it, s, it * 2 + s, SEG)
                        rounds(eng, NSEG // 2, pair)
                        body(NSEG // 2, 0, NSEG, TAIL)

                    @block.gpsimd
                    def _(pool):
                        def body(it, s, seg, L):
                            wait(pool, scanned[s], it)
                            z = rows(dA[s], L)
                            for k in range(KD):
                                last = pool.tensor_tensor(
                                    z[:, k], dtT4[:, k, :, ds(seg * SEG, L)].unsqueeze(1).to_broadcast([P, N, NB, L]),
                                    a_neg[:, k, :].unsqueeze(2).unsqueeze(3).to_broadcast([P, N, NB, L]), ALU.mult)
                            last.then_inc(z_made[s], 1)
                            pool.wait_ge(norm2_made, seg + 1)
                            pool.tensor_tensor(norm[:], norm2[:], half[:, 0:NB], ALU.pow).then_inc(norm_made, 1)
                        segments(pool, body)

                    @block.scalar
                    def _(act):
                        act.preload_act_table_set("exp_and_others")

                        def body(it, s, seg, L):
                            z = dA[s][:, 0:W * L]
                            act.wait_ge(z_made[s], it + 1)
                            act.activation(z, z, ACT.Tanh).then_inc(tanh_z[s], 1)
                            act.wait_ge(tanh_z[s], it + 1)
                            act.activation(z, z, ACT.Exp, scale=DA_HALF / SHARP).then_inc(dA_made[s], 1)
                        segments(act, body)

                    @block.tensor
                    def _(pe):
                        def body(it, s, seg, L):
                            for half_no in range(2):
                                if half_no == 0:
                                    wait(pe, u_made, seg)
                                    settle(pe)
                                for n in range(HN):
                                    last = pe.matmul(spread(half_no, 0, L)[:, n], pick[:, half_no * HN + n, :],
                                                     bc3v[:, :, ds(seg * SEG, L)], start=True, stop=True)
                            last.then_inc(b_spread, 1)
                            for half_no in range(2):
                                if half_no == 0:
                                    wait(pe, hc_made, seg)
                                    settle(pe)
                                for n in range(HN):
                                    last = pe.matmul(spread(half_no, 2, L)[:, n], pick_c_all[:, half_no * HN + n, :],
                                                     bc3v[:, :, ds(seg * SEG, L)], start=True, stop=True)
                            last.then_inc(c_spread, 1)
                            pe.wait_ge(sq_made, seg + 1)
                            wait(pe, norm2_made, seg)
                            pe.matmul(bank[:, 4, 0:W], ones[:], sq[:], start=True, stop=True).then_inc(sq_summed, 1)
                        pe.wait_ge(pick_made, 1)
                        segments(pe, body)

                    @block.vector
                    def _(dve):
                        dve.tensor_copy(pick_c_all[:], pick_c[:].unsqueeze(2).to_broadcast([3 * Q, N, P]))\
                           .then_inc(pick_made, 1)
                        dve.memset(h_last[:], 0.0).then_inc(first_state, 1)
                        dve.wait_ge(first_state, 1)

                        def body(it, s, seg, L):
                            at = ds(seg * SEG, L)
                            uu, cc = rows(u, L), rows(hc, L)
                            dve.wait_ge(b_spread, seg + 1)
                            for k in range(KD):
                                for half_no in range(2):
                                    n0 = half_no * HN
                                    last = dve.tensor_tensor(
                                        uu[:, k, n0:n0 + HN], gT[:, k, :, at].unsqueeze(1).to_broadcast([P, HN, NB, L]),
                                        spread(half_no, 0, L), ALU.mult)
                            last.then_inc(u_made, 1)
                            dve.wait_ge(dA_made[s], it + 1)
                            wait(dve, last_kept, seg)
                            d3 = flat_rows(dA[s], L)
                            u3 = flat_rows(u, L)
                            h3 = flat_rows(h, L)

                            def grid(buf):
                                return buf[:].rearrange("p (r b) -> p r b", r=R)

                            dve.tensor_tensor(grid(t1), grid(h_last), d3[:, :, :, 0], ALU.mult).then_inc(decayed, 1)
                            dve.wait_ge(decayed, seg + 1)
                            dve.wait_ge(u_made, seg + 1)
                            dve.tensor_tensor(grid(h0), grid(t1), u3[:, :, :, 0], ALU.add).then_inc(h0_made, 1)
                            dve.memset(d3[:, :, :, 0], 0.0).then_inc(dA_cut, 1)
                            dve.wait_ge(h0_made, seg + 1)
                            dve.tensor_tensor(sq[:], h0[:], h0[:], ALU.mult).then_inc(sq_made, 1)
                            dve.wait_ge(sq_summed, seg + 1)
                            dve.tensor_reduce(norm2[:], bank[:, 4, 0:W].rearrange("p (r b) -> p b r", r=R), AX.X,
                                              ALU.add).then_inc(norm2_made, 1)
                            dve.wait_ge(norm_made, seg + 1)
                            dve.tensor_scalar(norm[:], norm[:], 1e-8, None, ALU.add).then_inc(eps_in, 1)
                            dve.wait_ge(eps_in, seg + 1)
                            dve.reciprocal(scale[:], norm[:]).then_inc(inv_made, 1)
                            dve.wait_ge(inv_made, seg + 1)
                            dve.tensor_scalar(scale[:], scale[:], NORM_MAX, 1.0, ALU.mult, ALU.min).then_inc(scale_made, 1)
                            dve.wait_ge(scale_made, seg + 1)
                            dve.tensor_tensor(u3[:, :, :, 0], grid(h0), scale[:].unsqueeze(1).to_broadcast([P, R, NB]),
                                              ALU.mult).then_inc(h0_in, 1)
                            dve.wait_ge(h0_in, seg + 1)
                            dve.wait_ge(dA_cut, seg + 1)
                            dve.tensor_tensor_scan(h[:, 0:W * L], dA[s][:, 0:W * L], u[:, 0:W * L], 0.0, ALU.mult,
                                                   ALU.add).then_inc(scanned[s], 1)
                            dve.wait_ge(scanned[s], it + 1)
                            dve.tensor_copy(grid(h_last), h3[:, :, :, L - 1]).then_inc(last_kept, 1)
                            dve.wait_ge(c_spread, seg + 1)
                            for k in range(KD):
                                for half_no in range(2):
                                    n0 = half_no * HN
                                    last = dve.tensor_tensor(cc[:, k, n0:n0 + HN], rows(h, L)[:, k, n0:n0 + HN],
                                                             spread(half_no, 2, L), ALU.mult)
                            last.then_inc(hc_made, 1)
                            dve.wait_ge(hc_made, seg + 1)
                            settle(dve)
                            for k in range(KD):
                                last = dve.tensor_reduce(gT[:, k, :, at], cc[:, k].rearrange("p n b t -> p b t n"), AX.X,
                                                         ALU.add)
                            last.then_inc(y_made, 1)
                            dve.wait_ge(y_made, seg + 1)
                        segments(dve, body)
                scan_part.close()
                end_phase()

                turn_part = ExitStack()

                def sb(name, shape, dt=F32):
                    return turn_part.enter_context(nc.sbuf_tensor(name, shape, dt))

                ycp = sb("ycp", [P, KD, P])
                xs = sb("xs", [P, D])
                x2 = sb("x2", [P, D])
                y_copied, y_turned, xs_loaded, x2_made, x2_stored = (
                    sem("y_copied"), sem("y_turned"), sem("xs_loaded"), sem("x2_made"), sem("x2_stored"))
                with nc.Block() as block:
                    @block.sync
                    def _(sp):
                        def body(i):
                            wait(sp, x2_made, i)
                            sp.dma_start(xs[:], x_skip[ds(i * P, P), :]).then_inc(xs_loaded, 16)
                            sp.wait_ge(x2_made, i + 1)
                            sp.dma_start(x_mid[ds(i * P, P), :], x2[:]).then_inc(x2_stored, 16)
                        rounds(sp, TILES, body)
                        sp.wait_ge(x2_stored, 16 * TILES)

                    @block.scalar
                    def _(act):
                        def body(i):
                            wait(act, y_turned, i)
                            act.activation(ycp[:], xT[:, :, ds(i * P, P)], ACT.Copy).then_inc(y_copied, 1)
                        rounds(act, TILES, body)

                    @block.tensor
                    def _(pe):
                        def body(i):
                            pe.wait_ge(y_copied, i + 1)
                            wait(pe, x2_made, i)
                            for k in range(KD):
                                last = pe.transpose(bank[:, 0, k * P:(k + 1) * P], ycp[:, k, :], ident[:])
                            last.then_inc(y_turned, 1)
                        rounds(pe, TILES, body)

                    @block.vector
                    def _(dve):
                        def body(i):
                            dve.wait_ge(xs_loaded, 16 * (i + 1))
                            dve.wait_ge(y_turned, i + 1)
                            wait(dve, x2_stored, 16 * i)
                            dve.tensor_tensor(x2[:], xs[:], bank[:, 0, 0:D], ALU.add).then_inc(x2_made, 1)
                        rounds(dve, TILES, body)
                turn_part.close()
                end_phase()

        with ExitStack() as part:
            def sb(name, shape, dt=F32):
                return part.enter_context(nc.sbuf_tensor(name, shape, dt))

            weight = sb("weight", [P, TILES, TOPK])
            row_i = sb("row_i", [P, TILES, TOPK], I32)
            tile_expert = sb("tile_expert", [1, XT], I32)
            tile_no = sb("tile_no", [1, XT])
            b2 = sb("b2", [P, E * D])

            choice_part = ExitStack()
            chosen = choice_part.enter_context(
                nc.sbuf_tensor("chosen", [P, TILES, TOPK, E], F32))
            route_part = ExitStack()

            def sb(name, shape, dt=F32):
                return route_part.enter_context(nc.sbuf_tensor(name, shape, dt))

            gate = sb("gate", [P, KD, E])
            x2 = [sb(f"x2{c}", [P, GT, D]) for c in range(4)]
            xn2 = [sb(f"xnb{s}", [P, GT, D]) for s in range(2)]
            xn2T = [sb(f"xnbT{s}", [P, GT, D]) for s in range(2)]
            stats = [sb(f"statsb{s}", [P, GT, 6]) for s in range(2)]
            meanvar = [sb(f"meanvarb{s}", [P, GT, 2]) for s in range(2)]
            rstd = [sb(f"rstdb{s}", [P, GT]) for s in range(2)]
            logit = [sb(f"logit{s}", [P, GT, E + 1]) for s in range(2)]
            best = [sb(f"best{s}", [P, GT, 8]) for s in range(2)]
            best_at = [sb(f"best_at{s}", [P, GT, 8], U32) for s in range(2)]
            all_logits = sb("all_logits", [P, TILES, E])
            all_best = sb("all_best", [P, TILES, TOPK])
            best_f = sb("best_f", [P, TILES, TOPK])
            shifted = sb("shifted", [P, TILES, E])
            ek = sb("ek", [P, TILES, TOPK])
            z_sum = sb("z_sum", [P, TILES])
            s_sum = sb("s_sum", [P, TILES])

            gate_loaded, pad_made = sem("gate_loaded"), sem("pad_made")
            (st_made, ag_made, ep_made, rs_made, xn2_made, xn2_turned, xn2T_made, logit_done,
             logit_copied, best_made, at_made) = [sem(n) for n in (
                 "st_made", "ag_made", "ep_made", "rs_made", "xn2_made", "xn2_turned", "xn2T_made",
                 "logit_done", "logit_copied", "best_made", "at_made")]
            x2_loaded, xn2_stored = sems("x2_loaded", 4), sems("xn2_stored")
            kept, r_step, shift_made, exp_made = sem("kept"), sem("r_step"), sem("shift_made"), sem("exp_made")

            with nc.Block() as block:
                @block.sync
                def _(sp):
                    sp.dma_start(gate[:], gate_t.rearrange("(k p) e -> p k e", p=P)).then_inc(gate_loaded, 16)

                    def body(it, c, g):
                        wait(sp, xn2_made, g - 3)
                        sp.dma_start(x2[c][:], group_rows(x_mid, g)).then_inc(x2_loaded[c], 16)
                    steps(sp, GROUPS, body, 4)

                @block.gpsimd
                def _(pool):
                    def pair(it):
                        for s in range(2):
                            g = it * 2 + s
                            pool.wait_ge(ag_made, g + 1)
                            wait(pool, xn2_made, g - 1)
                            settle(pool)
                            pool.tensor_scalar(rstd[s][:], meanvar[s][:, :, 1], EPS, None, ALU.add)\
                                .then_inc(ep_made, 1)
                            pool.wait_ge(ep_made, g + 1)
                            pool.tensor_tensor(rstd[s][:], rstd[s][:], minus_half[:].to_broadcast([P, GT]),
                                               ALU.pow).then_inc(rs_made, 1)
                            pool.wait_ge(xn2_made, g + 1)
                            pool.dma_start(group_rows(x_norm, g), xn2[s][:]).then_inc(xn2_stored[s], 16)
                    rounds(pool, GROUPS // 2, pair)
                    for s in range(2):
                        pool.wait_ge(xn2_stored[s], 16 * (GROUPS // 2))

                @block.tensor
                def _(pe):
                    pe.wait_ge(gate_loaded, 16)

                    def logits(g, s):
                        pe.wait_ge(xn2T_made, g + 1)
                        wait(pe, logit_copied, g - 1)
                        for i in range(GT):
                            for k in range(KD):
                                last = pe.matmul(bank[:, 4 + s, i * E:(i + 1) * E],
                                                 xn2T[s][:, i, k * P:(k + 1) * P], gate[:, k, :],
                                                 start=(k == 0), stop=(k == KD - 1))
                        last.then_inc(logit_done, 1)

                    def pair(it):
                        for s in range(2):
                            g = it * 2 + s
                            pe.wait_ge(xn2_made, g + 1)
                            wait(pe, xn2T_made, g - 1)
                            for i in range(GT):
                                for k in range(KD):
                                    at = (i % 2) * D + k * P
                                    last = pe.transpose(bank[:, 2 * s + i // 2, at:at + P],
                                                        xn2[s][:, i, k * P:(k + 1) * P], ident[:])
                            last.then_inc(xn2_turned, 1)
                            if not isinstance(g, int) or g > 0:
                                logits(g - 1, 1 - s)
                    rounds(pe, GROUPS // 2, pair)
                    logits(GROUPS - 1, 1)

                @block.scalar
                def _(act):
                    act.preload_act_table_set("exp_and_others")

                    def pair(it):
                        for s in range(2):
                            g = it * 2 + s
                            act.wait_ge(xn2_turned, g + 1)
                            wait(act, logit_done, g - 1)
                            act.activation(xn2T[s][:], bank[:, 2 * s:2 * s + 2, :].rearrange("p b (i t) -> p (b i) t", t=D),
                                           ACT.Copy).then_inc(xn2T_made, 1)
                    rounds(act, GROUPS // 2, pair)
                    act.wait_ge(shift_made, 2)
                    act.activation(shifted[:], shifted[:], ACT.Exp).then_inc(exp_made, 1)
                    act.activation(ek[:], ek[:], ACT.Exp).then_inc(exp_made, 1)

                @block.vector
                def _(dve):
                    for s in range(2):
                        dve.memset(logit[s][:], -3.0e38).then_inc(pad_made, 1)
                    dve.wait_ge(pad_made, 2)

                    def measure(g, c):
                        s = c % 2
                        dve.wait_ge(x2_loaded[c], (g - c) * 4 + 16)
                        wait(dve, ag_made, g - 1)
                        settle(dve)
                        for i in range(GT):
                            dve.bn_stats(stats[s][:, i, :], x2[c][:, i, :]).then_inc(st_made, 1)
                        dve.wait_ge(st_made, GT * (g + 1))
                        wait(dve, rs_made, g - 1)
                        settle(dve)
                        for i in range(GT):
                            last = dve.bn_aggr(meanvar[s][:, i, :], stats[s][:, i, :])
                        last.then_inc(ag_made, 1)

                    def normalise(g, c):
                        s = c % 2
                        dve.wait_ge(rs_made, g + 1)
                        dve.wait_ge(ag_made, g + 1)
                        wait(dve, xn2_turned, g - 1)
                        if not isinstance(g, int) or g > 1:
                            dve.wait_ge(xn2_stored[s], (g - s) * 8)
                        for i in range(GT):
                            last = dve.tensor_scalar(xn2[s][:, i, :], x2[c][:, i, :], meanvar[s][:, i, 0:1],
                                                     rstd[s][:, i:i + 1], ALU.subtract, ALU.mult)
                        last.then_inc(xn2_made, 1)

                    def copy_logits(g, s):
                        dve.wait_ge(logit_done, g + 1)
                        wait(dve, at_made, g - 1)
                        dve.tensor_copy(logit[s][:, :, 0:E],
                                        bank[:, 4 + s, 0:GT * E].rearrange("p (i e) -> p i e", e=E))\
                           .then_inc(logit_copied, 1)

                    def three_best(g, s):
                        dve.wait_ge(logit_copied, g + 1)
                        wait(dve, kept, g - 1)
                        settle(dve)
                        for i in range(GT):
                            dve.max(best[s][:, i, :], logit[s][:, i, :]).then_inc(best_made, 1)
                        dve.tensor_copy(all_logits[:, ds(g * GT, GT), :], logit[s][:, :, 0:E])
                        dve.wait_ge(best_made, GT * (g + 1))
                        settle(dve)
                        for i in range(GT):
                            last = dve.max_index(best_at[s][:, i, :], best[s][:, i, :], logit[s][:, i, :])
                        last.then_inc(at_made, 1)

                    def keep(g, s):
                        dve.wait_ge(at_made, g + 1)
                        dve.tensor_copy(all_best[:, ds(g * GT, GT), :], best[s][:, :, 0:TOPK])
                        dve.tensor_copy(best_f[:, ds(g * GT, GT), :], best_at[s][:, :, 0:TOPK]).then_inc(kept, 1)

                    measure(0, 0)

                    def step(it, c, g):
                        s = c % 2
                        if not isinstance(g, int) or g + 1 < GROUPS:
                            measure(g + 1, (c + 1) % 4)
                        normalise(g, c)
                        if not isinstance(g, int) or g > 0:
                            copy_logits(g - 1, 1 - s)
                            three_best(g - 1, 1 - s)
                            keep(g - 1, 1 - s)
                    steps(dve, GROUPS, step, 4)
                    copy_logits(GROUPS - 1, 1)
                    three_best(GROUPS - 1, 1)
                    keep(GROUPS - 1, 1)

                    n = [0]

                    def chain(ins):
                        ins.then_inc(r_step, 1)
                        n[0] += 1
                        dve.wait_ge(r_step, n[0])

                    dve.wait_ge(kept, GROUPS)
                    dve.tensor_tensor(shifted[:], all_logits[:], all_best[:, :, 0:1].to_broadcast([P, TILES, E]),
                                      ALU.subtract).then_inc(shift_made, 1)
                    dve.tensor_tensor(ek[:], all_best[:], all_best[:, :, 0:1].to_broadcast([P, TILES, TOPK]),
                                      ALU.subtract).then_inc(shift_made, 1)
                    chain(dve.tensor_tensor(
                        chosen[:], expert_no[:].unsqueeze(1).unsqueeze(2).to_broadcast([P, TILES, TOPK, E]),
                        best_f[:].unsqueeze(3).to_broadcast([P, TILES, TOPK, E]), ALU.is_equal))
                    dve.wait_ge(exp_made, 2)
                    chain(dve.tensor_reduce(z_sum[:], shifted[:], AX.X, ALU.add))
                    chain(dve.reciprocal(z_sum[:], z_sum[:]))
                    chain(dve.tensor_tensor(ek[:], ek[:], z_sum[:].unsqueeze(2).to_broadcast([P, TILES, TOPK]),
                                            ALU.mult))
                    chain(dve.tensor_reduce(s_sum[:], ek[:], AX.X, ALU.add))
                    chain(dve.tensor_scalar(s_sum[:], s_sum[:], 1e-20, None, ALU.add))
                    chain(dve.reciprocal(s_sum[:], s_sum[:]))
                    chain(dve.tensor_tensor(weight[:], ek[:], s_sum[:].unsqueeze(2).to_broadcast([P, TILES, TOPK]),
                                            ALU.mult))
            route_part.close()
            end_phase()

            rank_part = ExitStack()

            def sb(name, shape, dt=F32):
                return rank_part.enter_context(nc.sbuf_tensor(name, shape, dt))

            taken = sb("taken", [P, TILES, E])
            so_far = sb("so_far", [P, E, TILES])
            row_f = sb("row_f", [P, TILES, E])
            one_row = sb("one_row", [P, TILES, E])
            picked = sb("picked", [P, TILES, TOPK])
            step_i = sb("step_i", [P, TILES], I32)
            step_f = sb("step_f", [P, TILES])
            over = sb("over", [P, E, TILES])
            n_tiles = sb("n_tiles", [P, E])
            tiles_to = sb("tiles_to", [P, E])
            base = sb("base", [P, E])
            tno_i = sb("tno_i", [1, XT], I32)
            past = sb("past", [1, XT, E])
            exp_f = sb("exp_f", [1, XT])
            unused_i = sb("unused_i", [P, XT], I32)
            unused = sb("unused", [P, XT])
            before = sb("before", [P, P])
            before_clear, before_made = sem("before_clear"), sem("before_made")
            r_pool, r_dve, r_pe, cleared = sem("r_pool"), sem("r_dve"), sem("r_pe"), sem("cleared")
            HT = TILES // 2
            with nc.Block() as block:
                @block.sync
                def _(sp):
                    sp.wait_ge(r_pool, 6)
                    sp.dma_start(row_choice.rearrange("(p j) o -> p (j o)", p=P), unused[:]).then_inc(cleared, 16)
                    sp.wait_ge(cleared, 16)

                @block.gpsimd
                def _(pool):
                    pool.memset(before[:], 1.0).then_inc(before_clear, 1)
                    pool.wait_ge(before_clear, 1)
                    pool.affine_select(out=before[:], in_=before[:], compare_op=ALU.is_gt, fill=0.0,
                                       base=0, pattern=[[1, P]], channel_multiplier=-1).then_inc(before_made, 1)
                    pool.iota(step_i[:], pattern=[[P, TILES]], base=0, channel_multiplier=0).then_inc(r_pool, 1)
                    pool.iota(tno_i[:], pattern=[[1, XT]], base=0, channel_multiplier=0).then_inc(r_pool, 1)
                    pool.iota(unused_i[:], pattern=[[1, XT]], base=SLOTS * TOK, channel_multiplier=XT).then_inc(r_pool, 1)
                    pool.wait_ge(r_pool, 3)
                    pool.tensor_copy(step_f[:], step_i[:]).then_inc(r_pool, 1)
                    pool.tensor_copy(tile_no[:], tno_i[:]).then_inc(r_pool, 1)
                    pool.tensor_copy(unused[:], unused_i[:]).then_inc(r_pool, 1)

                @block.tensor
                def _(pe):
                    pe.wait_ge(before_made, 1)
                    pe.wait_ge(r_dve, 2)
                    for hf in range(2):
                        m = taken[:, hf * HT:(hf + 1) * HT, :].rearrange("p i e -> p (i e)")
                        pe.matmul(bank[:, hf, 0:HT * E], before[:], m, start=True, stop=True)
                        last = pe.matmul(bank[:, 2 + hf, 0:HT * E], ones[:], m, start=True, stop=True)
                    last.then_inc(r_pe, 1)

                @block.vector
                def _(dve):
                    n = [0]

                    def chain(ins):
                        ins.then_inc(r_dve, 1)
                        n[0] += 1
                        dve.wait_ge(r_dve, n[0])

                    chain(dve.tensor_tensor(taken[:], chosen[:, :, 0, :], chosen[:, :, 1, :], ALU.add))
                    chain(dve.tensor_tensor(taken[:], taken[:], chosen[:, :, 2, :], ALU.add))
                    dve.wait_ge(r_pe, 1)
                    for e in range(E):
                        for hf in range(2):
                            chain(dve.tensor_tensor_scan(
                                so_far[:, e, hf * HT:(hf + 1) * HT], ones[:, 0:HT],
                                bank[:, 2 + hf, 0:HT * E].rearrange("p (i e) -> p e i", e=E)[:, e, :],
                                0.0 if hf == 0 else so_far[:, e, HT - 1:HT], ALU.mult, ALU.add))
                    dve.wait_ge(r_pool, 5)
                    chain(dve.tensor_tensor(over[:], so_far[:, :, TILES - 1:TILES].to_broadcast([P, E, TILES]),
                                            step_f[:].unsqueeze(1).to_broadcast([P, E, TILES]), ALU.is_gt))
                    chain(dve.tensor_reduce(n_tiles[:], over[:], AX.X, ALU.add))
                    chain(dve.tensor_tensor_scan(tiles_to[:], ones[:, 0:E], n_tiles[:], 0.0, ALU.mult, ALU.add))
                    chain(dve.tensor_tensor(base[:], tiles_to[:], n_tiles[:], ALU.subtract))
                    chain(dve.tensor_scalar(base[:], base[:], float(P), None, ALU.mult))
                    for hf in range(2):
                        i0 = hf * HT
                        r = row_f[:, i0:i0 + HT, :]
                        chain(dve.tensor_tensor(r, so_far[:, :, i0:i0 + HT].rearrange("p e i -> p i e"),
                                                bank[:, 2 + hf, 0:HT * E].rearrange("p (i e) -> p i e", e=E),
                                                ALU.subtract))
                        chain(dve.tensor_tensor(r, r, bank[:, hf, 0:HT * E].rearrange("p (i e) -> p i e", e=E),
                                                ALU.add))
                    chain(dve.tensor_tensor(row_f[:], row_f[:], base[:].unsqueeze(1).to_broadcast([P, TILES, E]),
                                            ALU.add))
                    for k in range(TOPK):
                        chain(dve.tensor_tensor(one_row[:], row_f[:], chosen[:, :, k, :], ALU.mult))
                        chain(dve.tensor_reduce(picked[:, :, k], one_row[:], AX.X, ALU.add))
                    chain(dve.tensor_copy(row_i[:], picked[:]))
                    chain(dve.tensor_tensor(past[:], tile_no[:].unsqueeze(2).to_broadcast([1, XT, E]),
                                            tiles_to[0:1, :].unsqueeze(1).to_broadcast([1, XT, E]), ALU.is_ge))
                    chain(dve.tensor_reduce(exp_f[:], past[:], AX.X, ALU.add))
                    chain(dve.tensor_scalar(exp_f[:], exp_f[:], float(E - 1), None, ALU.min))
                    chain(dve.tensor_copy(tile_expert[:], exp_f[:]))
            rank_part.close()
            choice_part.close()
            end_phase()

            shared_part = ExitStack()

            def sb(name, shape, dt=F32):
                return shared_part.enter_context(nc.sbuf_tensor(name, shape, dt))

            KS = FS // P
            GN = GT * P
            W_LOADS = 4 * E + 1
            assert E == GROUPS - 1
            sw1 = sb("sw1", [P, KD, 2 * FS])
            sb1 = sb("sb1", [P, 2 * KS])
            sw2 = sb("sw2", [P, KS, D])
            sb2 = sb("sb2", [P, D])
            smul = sb("smul", [P, KS])
            wmul = sb("wmul", [P, KD, E])
            xm = [sb(f"xm{s}", [P, GT, D]) for s in range(2)]
            xa = [sb(f"xa{s}", [P, GT, D]) for s in range(2)]
            xaT = [sb(f"xaT{s}", [P, KD, GN]) for s in range(2)]
            sgel = [sb(f"sgel{c}", [P, GN]) for c in range(2)]
            sglu = [sb(f"sglu{s}", [P, KS, GN]) for s in range(2)]
            to_row = [sb(f"to_row{s}", [P, TOPK], I32) for s in range(2)]
            choice = [sb(f"choice{s}", [P, TOPK]) for s in range(2)]
            choice_i = sb("choice_i", [P, TILES, TOPK], I32)
            choice_all = sb("choice_all", [P, TILES, TOPK])
            c_made, c_copied, c_sent = sem("c_made"), sems("c_copied"), sems("c_sent")
            s_loaded, s_scaled, w_loaded, w_scaled = sem("s_loaded"), sem("s_scaled"), sem("w_loaded"), sem("w_scaled")
            (xa_turned, xaT_made, gate_done, x_done, gelu_made, glu_made, o_done, bias_in, acc_made) = [sem(n) for n in (
                "xa_turned", "xaT_made", "gate_done", "x_done", "gelu_made", "glu_made", "o_done", "bias_in",
                "acc_made")]
            xa_loaded, xm_loaded, stored = sems("xa_loaded"), sems("xm_loaded"), sems("stored")
            with nc.Block() as block:
                def pairs(eng, body):
                    def pair(it):
                        for s in range(2):
                            body(it * 2 + s, s)
                    rounds(eng, GROUPS // 2, pair)

                @block.sync
                def _(sp):
                    def load_xa(g, s):
                        wait(sp, xa_turned, g - 1)
                        sp.dma_start(xa[s][:], group_rows(x_norm, g)).then_inc(xa_loaded[s], 16)

                    def load_xm(g, s):
                        if not isinstance(g, int) or g > 1:
                            sp.wait_ge(stored[s], (g - s) * 8)
                        sp.dma_start(xm[s][:], group_rows(x_mid, g)).then_inc(xm_loaded[s], 16)

                    def store(g, s):
                        sp.wait_ge(acc_made, 2 * (g + 1))
                        sp.dma_start(group_rows(x_mid, g), xm[s][:]).then_inc(stored[s], 16)

                    load_xa(0, 0)
                    sp.dma_start(sw1[:], s_fc1_t.rearrange("(k p) f -> p k f", p=P)).then_inc(s_loaded, 16)
                    with nc.allow_non_contiguous_dma(reason="small constants, once"):
                        sp.dma_start(sb1[:], s_fc1_b.rearrange("(k p) -> p k", p=P)).then_inc(s_loaded, 16)
                        sp.dma_start(smul[:], s_mult.rearrange("(k p) -> p k", p=P)).then_inc(s_loaded, 16)
                    sp.dma_start(sw2[:], s_fc2_t.rearrange("(k p) f -> p k f", p=P)).then_inc(s_loaded, 16)
                    sp.dma_start(sb2[:], s_fc2_b.partition_broadcast(P)).then_inc(s_loaded, 16)
                    load_xm(0, 0)
                    load_xa(1, 1)
                    load_xm(1, 1)
                    load_xa(2, 0)

                    def body(g, s, last=False):
                        if not last:
                            load_xa(g + 1, 1 - s)
                        store(g - 2, s)
                        load_xm(g, s)
                    with sp.Fori(1, GROUPS // 2 - 1) as it:
                        for s in range(2):
                            body(it * 2 + s, s)
                    body(GROUPS - 2, 0)
                    body(GROUPS - 1, 1, last=True)
                    store(GROUPS - 2, 0)
                    store(GROUPS - 1, 1)
                    for s in range(2):
                        sp.wait_ge(stored[s], 8 * GROUPS)

                @block.gpsimd
                def _(pool):
                    pool.iota(choice_i[:], pattern=[[SLOTS * P, TILES], [1, TOPK]], base=0, channel_multiplier=SLOTS)\
                        .then_inc(c_made, 1)
                    pool.wait_ge(c_made, 1)
                    pool.tensor_copy(choice_all[:], choice_i[:]).then_inc(c_made, 1)
                    pool.wait_ge(c_made, 2)

                    def pair(it):
                        for s in range(2):
                            wait(pool, c_sent[s], 48 * it)
                            pool.tensor_copy(to_row[s][:], row_i[:, ds(it * 2 + s, 1), :].rearrange("p o k -> p (o k)"))
                            pool.tensor_copy(choice[s][:], choice_all[:, ds(it * 2 + s, 1), :].rearrange("p o k -> p (o k)"))\
                                .then_inc(c_copied[s], 1)
                            pool.wait_ge(c_copied[s], it + 1)
                            settle(pool)
                            for k in range(TOPK):
                                pool.indirect_dma_start(
                                    out=row_choice, out_offset=bass.IndirectOffsetOnAxis(ap=to_row[s][:, k:k + 1], axis=0),
                                    in_=choice[s][:, k:k + 1], in_offset=None).then_inc(c_sent[s], 16)
                    rounds(pool, TILES // 2, pair)
                    pool.wait_ge(w_loaded, W_LOADS * 16)
                    for k in range(KD):
                        rows_k = w2[:, k, :].rearrange("p (e d) -> p e d", e=E)
                        pool.tensor_tensor(rows_k, rows_k, wmul[:, k, :].unsqueeze(2).to_broadcast([P, E, D]),
                                           ALU.mult).then_inc(w_scaled, 1)
                    for s in range(2):
                        pool.wait_ge(c_sent[s], 48 * (TILES // 2))

                @block.tensor
                def _(pe):
                    def turn(g, s):
                        pe.wait_ge(xa_loaded[s], (g - s) * 8 + 16)
                        wait(pe, xaT_made, g)
                        for k in range(KD):
                            for i in range(GT):
                                last = pe.transpose(bank[:, 4 + k, i * P:(i + 1) * P], xa[s][:, i, k * P:(k + 1) * P],
                                                    ident[:])
                        last.then_inc(xa_turned, 1)

                    def fc1(g, s):
                        pe.wait_ge(xaT_made, g + 1)
                        for i in range(KS):
                            c, two = g * KS + i, 2 * (i % 2)
                            wait(pe, gelu_made, c - 1)
                            for k in range(KD):
                                last = pe.matmul(bank[:, two, :], sw1[:, k, FS + i * P:FS + (i + 1) * P],
                                                 xaT[s][:, k, :], start=(k == 0), stop=(k == KD - 1))
                            last.then_inc(gate_done, 1)
                            wait(pe, glu_made, c - 1)
                            for k in range(KD):
                                last = pe.matmul(bank[:, two + 1, :], sw1[:, k, i * P:(i + 1) * P],
                                                 xaT[s][:, k, :], start=(k == 0), stop=(k == KD - 1))
                            last.then_inc(x_done, 1)

                    def fc2(g, s):
                        pe.wait_ge(glu_made, KS * (g + 1))
                        for p in range(2):
                            wait(pe, acc_made, 2 * (g - 1) + p + 1)
                            for i in range(2):
                                for k in range(KS):
                                    last = pe.matmul(bank[:, 6 + p, i * D:(i + 1) * D],
                                                     sglu[s][:, k, (2 * p + i) * P:(2 * p + i + 1) * P], sw2[:, k, :],
                                                     start=(k == 0), stop=(k == KS - 1))
                            last.then_inc(o_done, 1)

                    turn(0, 0)
                    pe.wait_ge(s_loaded, 80)

                    def body(g, s, last=False):
                        if not last:
                            turn(g + 1, 1 - s)
                        fc1(g, s)
                        if isinstance(g, int) and g == 0:
                            pe.wait_ge(s_scaled, 1)
                        else:
                            fc2(g - 1, 1 - s)
                    body(0, 0)
                    body(1, 1)
                    with pe.Fori(1, GROUPS // 2 - 1) as it:
                        for s in range(2):
                            body(it * 2 + s, s)
                    body(GROUPS - 2, 0)
                    body(GROUPS - 1, 1, last=True)
                    fc2(GROUPS - 1, 1)

                @block.scalar
                def _(act):
                    act.preload_act_table_set("gelu_and_others")
                    def load_weights(e):
                        act.dma_start(w1[:, :, ds(e * (2 * F), 2 * F)],
                                      fc1_t[:, ds(e, 1), :].rearrange("(k p) o f -> p k (o f)", p=P)).then_inc(w_loaded, 16)
                        act.dma_start(w2[:, :, ds(e * D, D)],
                                      fc2_t[:, ds(e, 1), :].rearrange("(k p) o d -> p k (o d)", p=P)).then_inc(w_loaded, 16)
                        act.dma_start(b1[:, ds(e * (2 * F), 2 * F)],
                                      fc1_b[ds(e, 1), :].rearrange("o f -> (o f)").partition_broadcast(P))\
                           .then_inc(w_loaded, 16)
                        act.dma_start(b2[:, ds(e * D, D)],
                                      fc2_b[ds(e, 1), :].rearrange("o d -> (o d)").partition_broadcast(P))\
                           .then_inc(w_loaded, 16)

                    def copy_xT(g, s):
                        act.wait_ge(xa_turned, g + 1)
                        wait(act, x_done, KS * (g - 1))
                        act.activation(xaT[s][:], bank[:, 4:6, :], ACT.Copy).then_inc(xaT_made, 1)

                    copy_xT(0, 0)
                    act.wait_ge(s_loaded, 80)
                    act.dma_start(wmul[:], mult_t.rearrange("(k p) e -> p k e", p=P)).then_inc(w_loaded, 16)

                    def body(g, s, last=False):
                        if not last:
                            copy_xT(g + 1, 1 - s)
                            load_weights(g)
                        for i in range(KS):
                            c = g * KS + i
                            act.wait_ge(gate_done, c + 1)
                            wait(act, glu_made, c - 1)
                            settle(act)
                            act.activation(sgel[i % 2][:], bank[:, 2 * (i % 2), :], ACT.Gelu,
                                           bias=sb1[:, KS + i:KS + i + 1]).then_inc(gelu_made, 1)
                    body(0, 0)
                    body(1, 1)
                    with act.Fori(1, GROUPS // 2 - 1) as it:
                        for s in range(2):
                            body(it * 2 + s, s)
                    body(GROUPS - 2, 0)
                    body(GROUPS - 1, 1, last=True)
                    act.wait_ge(w_loaded, W_LOADS * 16)

                @block.vector
                def _(dve):
                    dve.wait_ge(s_loaded, 80)
                    dve.tensor_tensor(sw2[:], sw2[:], smul[:].unsqueeze(2).to_broadcast([P, KS, D]), ALU.mult)\
                       .then_inc(s_scaled, 1)

                    def add_out(g, s):
                        dve.wait_ge(xm_loaded[s], (g - s) * 8 + 16)
                        dve.tensor_tensor(xm[s][:], xm[s][:], sb2[:].unsqueeze(1).to_broadcast([P, GT, D]), ALU.add)\
                           .then_inc(bias_in, 1)
                        dve.wait_ge(bias_in, g + 1)
                        for p in range(2):
                            dve.wait_ge(o_done, 2 * g + p + 1)
                            dve.tensor_tensor(xm[s][:, 2 * p:2 * p + 2, :], xm[s][:, 2 * p:2 * p + 2, :],
                                              bank[:, 6 + p, :].rearrange("p (i d) -> p i d", i=2), ALU.add)\
                               .then_inc(acc_made, 1)

                    def body(g, s):
                        for i in range(KS):
                            c = g * KS + i
                            dve.wait_ge(x_done, c + 1)
                            dve.wait_ge(gelu_made, c + 1)
                            wait(dve, o_done, 2 * (g - 1))
                            settle(dve)
                            dve.scalar_tensor_tensor(sglu[s][:, i, :], bank[:, 2 * (i % 2) + 1, :], sb1[:, i:i + 1],
                                                     sgel[i % 2][:], ALU.add, ALU.mult).then_inc(glu_made, 1)
                        if not isinstance(g, int) or g > 0:
                            add_out(g - 1, 1 - s)
                    pairs(dve, body)
                    add_out(GROUPS - 1, 1)
            shared_part.close()
            end_phase()

            exp_part = ExitStack()

            def sb(name, shape, dt=F32):
                return exp_part.enter_context(nc.sbuf_tensor(name, shape, dt))

            NB4 = 8
            TR = NB4 // 2
            row_ids = sb("row_ids", [XT // 2, 2, P])
            ids = sb("ids", [P, 2, XT // 2], I32)
            tokens = sb("tokens", [P, 2, XT // 2], I32)
            rt = [sb(f"rt{c}", [P, 1], I32) for c in range(NB4)]
            to_slot = [sb(f"to_slot{c}", [P, 1], I32) for c in range(NB4)]
            xg = [sb(f"xg{c}", [P, D]) for c in range(NB4)]
            xgT = [sb(f"xgT{s}", [P, KD, P]) for s in range(2)]
            hid = [sb(f"hid{s}", [P, 2 * F]) for s in range(2)]
            act_g = [sb(f"act_g{s}", [P, F]) for s in range(2)]
            glu = [sb(f"glu{s}", [P, F]) for s in range(2)]
            gluT = [sb(f"gluT{s}", [P, F // P, P]) for s in range(2)]
            ye = [sb(f"ye{c}", [P, D]) for c in range(NB4)]
            ids_loaded, ids_turned, ids_made = sem("ids_loaded"), sem("ids_turned"), sem("ids_made")
            rt_made, slot_made = sem("rt_made"), sem("slot_made")
            xg_loaded, ye_stored = sems("xg_loaded", NB4), sems("ye_stored", NB4)
            (xg_turned, xgT_made, h_done, hid_made, gelu_made, glu_made, glu_turned, gluT_made, y_done,
             ye_made) = [sem(n) for n in ("xg_turned", "xgT_made", "h_done", "hid_made", "gelu_made", "glu_made",
                                          "glu_turned", "gluT_made", "ye_done", "ye_made")]
            with nc.Block() as block:
                @block.sync
                def _(sp):
                    sp.dma_start(row_ids[:], row_choice.rearrange("(q s p) o -> q s (p o)", s=2, p=P)).then_inc(ids_loaded, 16)
                    sp.wait_ge(ids_loaded, 16)

                @block.gpsimd
                def _(pool):
                    pool.wait_ge(ids_made, 3)

                    def gather(it, c, j):
                        wait(pool, xg_loaded[c], 16 * it)
                        pool.tensor_copy(rt[c][:], tokens[:, c % 2, ds(it * TR + c // 2, 1)]).then_inc(rt_made, 1)
                        pool.wait_ge(rt_made, j + 1)
                        wait(pool, xg_turned, j - NB4 + 1)
                        settle(pool)
                        pool.indirect_dma_start(
                            out=xg[c][:], out_offset=None, in_=x_norm,
                            in_offset=bass.IndirectOffsetOnAxis(ap=rt[c][:, 0:1], axis=0)).then_inc(xg_loaded[c], 16)

                    def scatter(it, c, j):
                        wait(pool, ye_stored[c], 16 * it)
                        pool.tensor_copy(to_slot[c][:], ids[:, c % 2, ds(it * TR + c // 2, 1)]).then_inc(slot_made, 1)
                        pool.wait_ge(slot_made, j + 1)
                        pool.wait_ge(ye_made, j + 1)
                        settle(pool)
                        pool.indirect_dma_start(
                            out=choice_out, out_offset=bass.IndirectOffsetOnAxis(ap=to_slot[c][:, 0:1], axis=0),
                            in_=ye[c][:], in_offset=None).then_inc(ye_stored[c], 16)

                    AHEAD = NB4 - 2
                    for c in range(AHEAD):
                        gather(0, c, c)

                    def step(it, c, j):
                        if not isinstance(j, int) or j + AHEAD < XT:
                            gather(it + (c + AHEAD) // NB4, (c + AHEAD) % NB4, j + AHEAD)
                        if not isinstance(j, int) or j > 0:
                            scatter(it if c else it - 1, (c - 1) % NB4, j - 1)
                    steps(pool, XT, step, NB4)
                    scatter(XT // NB4 - 1, NB4 - 1, XT - 1)
                    for c in range(NB4):
                        pool.wait_ge(ye_stored[c], 16 * (XT // NB4))

                @block.tensor
                def _(pe):
                    pe.wait_ge(ids_loaded, 16)
                    for s in range(2):
                        last = pe.transpose(bank[:, s, 0:XT // 2], row_ids[:, s, :], ident[0:XT // 2, 0:XT // 2])
                    last.then_inc(ids_turned, 1)
                    pe.wait_ge(ids_made, 1)

                    def turn_x(c, it, j):
                        s = c % 2
                        pe.wait_ge(xg_loaded[c % NB4], 16 * (it + 1))
                        wait(pe, xgT_made, j - 1)
                        for k in range(KD):
                            last = pe.transpose(bank[:, s, k * P:(k + 1) * P], xg[c % NB4][:, k * P:(k + 1) * P], ident[:])
                        last.then_inc(xg_turned, 1)

                    def fc1(c, j):
                        s = c % 2
                        e_no = pe.value_load(tile_expert[0:1, ds(j, 1)], min_val=0, max_val=E - 1)
                        pe.wait_ge(xgT_made, j + 1)
                        wait(pe, hid_made, j - 1)
                        for k in range(KD):
                            last = pe.matmul(bank[:, 2 + s, :], xgT[s][:, k, :], w1[:, k, ds(e_no * (2 * F), 2 * F)],
                                             start=(k == 0), stop=(k == KD - 1))
                        last.then_inc(h_done, 1)

                    def turn_glu(c, j):
                        s = c % 2
                        pe.wait_ge(glu_made, j + 1)
                        wait(pe, gluT_made, j - 1)
                        for k in range(F // P):
                            last = pe.transpose(bank[:, 4 + s, k * P:(k + 1) * P], glu[s][:, k * P:(k + 1) * P], ident[:])
                        last.then_inc(glu_turned, 1)

                    def fc2(c, j):
                        s = c % 2
                        e_no = pe.value_load(tile_expert[0:1, ds(j, 1)], min_val=0, max_val=E - 1)
                        pe.wait_ge(gluT_made, j + 1)
                        wait(pe, ye_made, j - 1)
                        for k in range(F // P):
                            last = pe.matmul(bank[:, 6 + s, 0:D], gluT[s][:, k, :], w2[:, k, ds(e_no * D, D)],
                                             start=(k == 0), stop=(k == F // P - 1))
                        last.then_inc(y_done, 1)

                    turn_x(0, 0, 0)
                    turn_x(1, 0, 1)
                    fc1(0, 0)

                    def step(it, c, j):
                        if not isinstance(j, int) or j + 2 < XT:
                            turn_x(c + 2, it + (c + 2) // NB4, j + 2)
                        if not isinstance(j, int) or j + 1 < XT:
                            fc1(c + 1, j + 1)
                        turn_glu(c, j)
                        if not isinstance(j, int) or j > 0:
                            fc2(c + 1, j - 1)
                    steps(pe, XT, step, NB4)
                    fc2(1, XT - 1)

                @block.scalar
                def _(act):
                    act.preload_act_table_set("gelu_and_others")

                    def xT_copy(c, j):
                        s = c % 2
                        act.wait_ge(xg_turned, j + 1)
                        wait(act, h_done, j - 1)
                        act.activation(xgT[s][:], bank[:, s, 0:D].rearrange("p (k t) -> p k t", k=KD), ACT.Copy)\
                           .then_inc(xgT_made, 1)

                    def gelu(c, j):
                        s = c % 2
                        act.wait_ge(hid_made, j + 1)
                        wait(act, glu_made, j - 1)
                        act.activation(act_g[s][:], hid[s][:, F:2 * F], ACT.Gelu).then_inc(gelu_made, 1)

                    xT_copy(0, 0)
                    xT_copy(1, 1)
                    gelu(0, 0)

                    def step(it, c, j):
                        s = c % 2
                        if not isinstance(j, int) or j + 2 < XT:
                            xT_copy(c, j + 2)
                        act.wait_ge(glu_turned, j + 1)
                        wait(act, y_done, j - 1)
                        act.activation(gluT[s][:], bank[:, 4 + s, 0:F].rearrange("p (k t) -> p k t", t=P), ACT.Copy)\
                           .then_inc(gluT_made, 1)
                        if not isinstance(j, int) or j + 1 < XT:
                            gelu(c + 1, j + 1)
                    steps(act, XT, step, NB4)

                @block.vector
                def _(dve):
                    dve.wait_ge(ids_turned, 1)
                    dve.tensor_copy(ids[:], bank[:, 0:2, 0:XT // 2]).then_inc(ids_made, 1)
                    dve.wait_ge(ids_made, 1)
                    dve.tensor_scalar(tokens[:], ids[:], SLOTS_LOG, None, ALU.logical_shift_right).then_inc(ids_made, 1)
                    dve.wait_ge(ids_made, 2)
                    dve.tensor_scalar(tokens[:], tokens[:], TOK - 1, None, ALU.min).then_inc(ids_made, 1)

                    def add_bias(c, j):
                        s = c % 2
                        e_no = dve.value_load(tile_expert[0:1, ds(j, 1)], min_val=0, max_val=E - 1)
                        dve.wait_ge(h_done, j + 1)
                        wait(dve, glu_made, j - 1)
                        dve.tensor_tensor(hid[s][:], bank[:, 2 + s, :], b1[:, ds(e_no * (2 * F), 2 * F)],
                                          ALU.add).then_inc(hid_made, 1)

                    def gate_glu(c, j):
                        s = c % 2
                        dve.wait_ge(gelu_made, j + 1)
                        dve.wait_ge(hid_made, j + 1)
                        wait(dve, glu_turned, j - 1)
                        dve.tensor_tensor(glu[s][:], hid[s][:, 0:F], act_g[s][:], ALU.mult).then_inc(glu_made, 1)

                    def take_y(c, it, j):
                        e_no = dve.value_load(tile_expert[0:1, ds(j, 1)], min_val=0, max_val=E - 1)
                        dve.wait_ge(y_done, j + 1)
                        wait(dve, ye_stored[c % NB4], 16 * it)
                        dve.tensor_tensor(ye[c % NB4][:], bank[:, 6 + c % 2, 0:D], b2[:, ds(e_no * D, D)], ALU.add)\
                           .then_inc(ye_made, 1)

                    add_bias(0, 0)
                    gate_glu(0, 0)

                    def step(it, c, j):
                        if not isinstance(j, int) or j + 1 < XT:
                            add_bias(c + 1, j + 1)
                        if not isinstance(j, int) or j > 0:
                            take_y(c + NB4 - 1, it if c else it - 1, j - 1)
                        if not isinstance(j, int) or j + 1 < XT:
                            gate_glu(c + 1, j + 1)
                    steps(dve, XT, step, NB4)
                    take_y(NB4 - 1, XT // NB4 - 1, XT - 1)
            exp_part.close()
            end_phase()

            y3 = [part.enter_context(nc.sbuf_tensor(f"y3_{s}", [P, GT, TOPK * D], F32)) for s in range(2)]
            total = [part.enter_context(nc.sbuf_tensor(f"total{s}", [P, GT, D], F32)) for s in range(2)]
            y3_loaded, total_loaded, stored = sems("y3_loaded"), sems("total_loaded"), sems("stored")
            summed = [sem(f"summed{k}") for k in range(TOPK)]
            with nc.Block() as block:
                def pairs(eng, body):
                    def pair(it):
                        for s in range(2):
                            body(it * 2 + s, s)
                    rounds(eng, GROUPS // 2, pair)

                @block.sync
                def _(sp):
                    def body(g, s):
                        wait(sp, summed[TOPK - 1], GT * (g - 1))
                        for i in range(GT):
                            choices = choice_out[ds((g * GT + i) * (P * SLOTS), P * SLOTS), :]
                            sp.dma_start(y3[s][:, i, :],
                                         choices.rearrange("(p k) d -> p (k d)", k=SLOTS)[:, 0:TOPK * D])\
                              .then_inc(y3_loaded[s], 16)
                    pairs(sp, body)

                @block.scalar
                def _(act):
                    def load(g, s):
                        if not isinstance(g, int) or g > 1:
                            act.wait_ge(stored[s], (g - s) * 8)
                        act.dma_start(total[s][:], group_rows(x_mid, g)).then_inc(total_loaded[s], 16)

                    def store(g, s):
                        act.wait_ge(summed[TOPK - 1], GT * (g + 1))
                        act.dma_start(group_rows(out_rows, g), total[s][:]).then_inc(stored[s], 16)

                    load(0, 0)
                    load(1, 1)

                    def body(g, s):
                        if isinstance(g, int) and g < 2:
                            return
                        store(g - 2, s)
                        load(g, s)
                    pairs(act, body)
                    for s in range(2):
                        store(GROUPS - 2 + s, s)
                        act.wait_ge(stored[s], 8 * GROUPS)

                @block.vector
                def _(dve):
                    def body(g, s):
                        dve.wait_ge(total_loaded[s], (g - s) * 8 + 16)
                        dve.wait_ge(y3_loaded[s], (g - s) * (8 * GT) + 16 * GT)
                        for k in range(TOPK):
                            if k:
                                dve.wait_ge(summed[k - 1], GT * (g + 1))
                            for i in range(GT):
                                dve.scalar_tensor_tensor(
                                    total[s][:, i, :], y3[s][:, i, k * D:(k + 1) * D],
                                    weight[:, ds(g * GT + i, 1), k:k + 1].rearrange("p o k -> p (o k)"),
                                    total[s][:, i, :], ALU.mult, ALU.add).then_inc(summed[k], 1)
                    pairs(dve, body)


def kernel(**inputs):
    import numpy as np
    import concourse.bacc as bacc
    from concourse import mybir as _mybir
    from concourse.bass_utils import run_bass_kernel_spmd

    a = {k: np.asarray(v) for k, v in inputs.items()}
    laid = {
        "x": a["L0_attn_x"],
        "W_dt_t": a["L0_attn_W_dt"].T,
        "b_dt": a["L0_attn_b_dt"],
        "W_bc_t": np.concatenate([a["L0_attn_W_B"], a["L0_attn_W_C"]], axis=0).T,
        "A_log": a["L0_attn_A_log"],
        "D_param": a["L0_attn_D_param"],
        "gate_t": a["L0_ffn_gate_w"].T,
        "fc1_t": a["L0_ffn_fc1_w"].transpose(2, 0, 1),
        "fc1_b": a["L0_ffn_fc1_b"],
        "mult_t": a["L0_ffn_geglu_mult"].T,
        "fc2_t": a["L0_ffn_fc2_w"].transpose(2, 0, 1),
        "fc2_b": a["L0_ffn_fc2_b"],
        "s_fc1_t": a["L0_ffn_s_fc1_w"].T,
        "s_fc1_b": a["L0_ffn_s_fc1_b"],
        "s_mult": a["L0_ffn_s_geglu_mult"],
        "s_fc2_t": a["L0_ffn_s_fc2_w"].T,
        "s_fc2_b": a["L0_ffn_s_fc2_b"],
    }
    nc = bacc.Bacc("TRN2", target_bir_lowering=False, num_devices=1)
    arrays, args = {}, {}
    for name, value in laid.items():
        value = np.ascontiguousarray(value)
        arrays["in_" + name] = value
        args[name] = nc.dram_tensor("in_" + name, value.shape, _mybir.dt.from_np(value.dtype), kind="ExternalInput").ap()
    shape = a["L0_attn_x"].shape
    args["out"] = nc.dram_tensor("out_0", shape, _mybir.dt.float32, kind="ExternalOutput").ap()
    model_kernel(nc, **args)
    r = run_bass_kernel_spmd(nc, [arrays], core_ids=[0])
    return r.results[0]["out_0"]
```

```python
from contextlib import ExitStack

import concourse.bass as bass
from concourse import mybir

F32 = mybir.dt.float32
I32 = mybir.dt.int32
U32 = mybir.dt.uint32
BF16 = mybir.dt.bfloat16
ALU = mybir.AluOpType
ACT = mybir.ActivationFunctionType
AX = mybir.AxisListType
ds = bass.ds

P = 128
EPS = 1e-5
DT_MID, DT_HALF = (0.1 + 0.001) / 2.0, (0.1 - 0.001) / 2.0
SHARP = 0.5
A_HALF = 5.0
DA_HALF = 8.0
NORM_MAX = 20.0
NORM2_SURE = 399.9
SEG = 10
TOPK = 3
SLOTS = 4
SLOTS_LOG = 2


class Memory:
    pass


def model_kernel(nc, x, W_dt_t, b_dt, W_bc_t, A_log, D_param, gate_t, fc1_t, fc1_b, mult_t, fc2_t,
                 fc2_b, s_fc1_t, s_fc1_b, s_mult, s_fc2_t, s_fc2_b, out):
    NB, T, D = x.shape
    N = A_log.shape[1]
    E, F = mult_t.shape[1], mult_t.shape[0]
    FS = s_mult.shape[0]
    TOK = NB * T
    TILES = TOK // P
    KD = D // P
    XT = TOK * TOPK // P + E
    XT += -XT % 8
    R = KD * N
    NSEG = T // SEG
    TAIL = T - NSEG * SEG
    NORMS = -(-T // SEG)
    Q = 32

    GT = 4
    GROUPS = TILES // GT

    def group_rows(t, g):
        return t[ds(g * (GT * P), GT * P), :].rearrange("(i p) d -> p i d", p=P)

    x_rows = x.rearrange("b t d -> (b t) d")
    out_rows = out.rearrange("b t d -> (b t) d")
    x_skip = nc.dram_tensor("x_skip", (TOK, D), F32, kind="Internal").ap()
    x_mid = nc.dram_tensor("x_mid", (TOK, D), F32, kind="Internal").ap()
    x_norm = nc.dram_tensor("x_norm", (TOK, D), F32, kind="Internal").ap()
    row_choice = nc.dram_tensor("row_choice", (XT * P, 1), F32, kind="Internal").ap()
    choice_out = nc.dram_tensor("choice_out", (TOK * SLOTS + XT * P, D), F32, kind="Internal").ap()

    with ExitStack() as ctx:
        def sb(name, shape, dt=F32):
            return ctx.enter_context(nc.sbuf_tensor(name, shape, dt))

        phase_sems = []
        phase_no = [0]

        def sem(name):
            phase_sems.append(nc.alloc_semaphore(f"{name}_of{phase_no[0]}"))
            return phase_sems[-1]

        passed = ctx.enter_context(nc.semaphore("passed"))

        def settle(eng):
            eng.sem_inc(passed, 1)

        def wait(eng, signal, count):
            if not isinstance(count, int) or count > 0:
                eng.wait_ge(signal, count)

        def rounds(eng, n, body):
            body(0)
            with eng.Fori(1, n) as i:
                body(i)

        def steps(eng, n, body, unroll):
            rounds = n // unroll
            for c in range(unroll):
                body(0, c, c)
            with eng.Fori(1, rounds - 1) as it:
                for c in range(unroll):
                    body(it, c, it * unroll + c)
            for c in range(unroll):
                body(rounds - 1, c, (rounds - 1) * unroll + c)

        def pairwise(eng, n, body):
            for j in range(2):
                body(j, j)
            with eng.Fori(1, (n - 1) // 2) as it:
                for s in range(2):
                    body(it * 2 + s, s)
            for j in range((n - 1) // 2 * 2, n):
                body(j, j % 2)

        def end_phase():
            nc.clear_and_free_semaphores(list(phase_sems))
            phase_sems.clear()
            phase_no[0] += 1
            nc.all_engine_barrier()

        def sems(name, n=2):
            return [sem(f"{name}{i}") for i in range(n)]

        bank = ctx.enter_context(nc.psum_tensor("bank", [P, 8, 512], F32))

        arena_x = sb("arena_x", [P, KD * TOK])
        arena_dt = sb("arena_dt", [P, KD * TOK])
        xT = arena_x[:, :].rearrange("p (k t) -> p k t", k=KD)
        dtT = arena_dt[:, :].rearrange("p (k t) -> p k t", k=KD)
        w1 = arena_dt[:, 0:KD * E * 2 * F].rearrange("p (k e f) -> p k (e f)", k=KD, e=E)
        w2 = arena_x[:, 0:KD * E * D].rearrange("p (k e f) -> p k (e f)", k=KD, e=E)
        b1 = arena_x[:, KD * E * D:KD * E * D + E * 2 * F]

        ident = sb("ident", [P, P])
        ones = sb("ones", [P, P])
        minus_half = sb("minus_half", [P, 1])
        half = sb("half", [P, 8])
        expert_no = sb("expert_no", [P, E])
        out_of_bounds = sb("out_of_bounds", [P, 1], I32)

        KS = FS // P
        GN = GT * P
        G1 = 10

        def shared_expert(phase_sb, weights, g0, n, to, summed_up=None):
            sh = Memory()

            def sb(name, shape):
                return phase_sb(f"{name}_from{g0}", shape)

            sw1, sb1, sw2, sb2 = weights
            xm = [sb(f"xm{s}", [P, GT, D]) for s in range(2)]
            xa = [sb(f"xa{s}", [P, GT, D]) for s in range(2)]
            xaT = [sb(f"xaT{s}", [P, KD, GN]) for s in range(2)]
            sgel = [sb(f"sgel{c}", [P, GN]) for c in range(2)]
            sglu = [sb(f"sglu{s}", [P, KS, GN]) for s in range(2)]
            (xa_turned, xaT_made, gate_done, x_done, gelu_made, glu_made, o_done, bias_in,
             acc_made) = [sem(name) for name in (
                "xa_turned", "xaT_made", "gate_done", "x_done", "gelu_made", "glu_made", "o_done", "bias_in",
                "acc_made")]
            xa_loaded, xm_loaded, stored = sems("xa_loaded"), sems("xm_loaded"), sems("sh_stored")
            sh.stored = stored

            def load_xa(sp, j, s):
                wait(sp, xa_turned, j - 1)
                sp.dma_start(xa[s][:], group_rows(x_norm, j + g0)).then_inc(xa_loaded[s], 16)

            def load_xm(sp, j, s):
                if not isinstance(j, int) or j > 1:
                    sp.wait_ge(stored[s], (j - s) * 8)
                sp.dma_start(xm[s][:], group_rows(x_mid, j + g0)).then_inc(xm_loaded[s], 16)

            def store(sp, j, s):
                if summed_up is None:
                    sp.wait_ge(acc_made, 2 * (j + 1))
                else:
                    summed_up(sp, j)
                sp.dma_start(group_rows(to, j + g0), xm[s][:]).then_inc(stored[s], 16)

            def move(sp, j, s):
                if not isinstance(j, int) or j + 1 < n:
                    load_xa(sp, j + 1, 1 - s)
                if not isinstance(j, int) or j > 1:
                    store(sp, j - 2, s)
                load_xm(sp, j, s)

            def move_last(sp):
                for j in (n - 2, n - 1):
                    store(sp, j, j % 2)
                for s in range(2):
                    sp.wait_ge(stored[s], 16 * len(range(s, n, 2)))

            def products(pe, weights_ready):
                def turn(j, s):
                    pe.wait_ge(xa_loaded[s], (j - s) * 8 + 16)
                    wait(pe, xaT_made, j)
                    for k in range(KD):
                        for i in range(GT):
                            last = pe.transpose(bank[:, 4 + k, i * P:(i + 1) * P], xa[s][:, i, k * P:(k + 1) * P],
                                                ident[:])
                    last.then_inc(xa_turned, 1)

                def fc1(j, s):
                    pe.wait_ge(xaT_made, j + 1)
                    for i in range(KS):
                        c, two = j * KS + i, 2 * (i % 2)
                        wait(pe, gelu_made, c - 1)
                        for k in range(KD):
                            last = pe.matmul(bank[:, two, :], sw1[:, k, FS + i * P:FS + (i + 1) * P],
                                             xaT[s][:, k, :], start=(k == 0), stop=(k == KD - 1))
                        last.then_inc(gate_done, 1)
                        wait(pe, glu_made, c - 1)
                        for k in range(KD):
                            last = pe.matmul(bank[:, two + 1, :], sw1[:, k, i * P:(i + 1) * P],
                                             xaT[s][:, k, :], start=(k == 0), stop=(k == KD - 1))
                        last.then_inc(x_done, 1)

                def fc2(j, s):
                    pe.wait_ge(glu_made, KS * (j + 1))
                    for p in range(2):
                        wait(pe, acc_made, 2 * (j - 1) + p + 1)
                        for i in range(2):
                            for k in range(KS):
                                last = pe.matmul(bank[:, 6 + p, i * D:(i + 1) * D],
                                                 sglu[s][:, k, (2 * p + i) * P:(2 * p + i + 1) * P], sw2[:, k, :],
                                                 start=(k == 0), stop=(k == KS - 1))
                        last.then_inc(o_done, 1)

                turn(0, 0)
                weights_ready()

                def body(j, s):
                    if not isinstance(j, int) or j + 1 < n:
                        turn(j + 1, 1 - s)
                    fc1(j, s)
                    if not isinstance(j, int) or j > 0:
                        fc2(j - 1, 1 - s)
                pairwise(pe, n, body)
                fc2(n - 1, (n - 1) % 2)

            def copy_xT(act, j, s):
                act.wait_ge(xa_turned, j + 1)
                wait(act, x_done, KS * (j - 1))
                act.activation(xaT[s][:], bank[:, 4:6, :], ACT.Copy).then_inc(xaT_made, 1)

            def gelus(act, j, s):
                for i in range(KS):
                    c = j * KS + i
                    act.wait_ge(gate_done, c + 1)
                    wait(act, glu_made, c - 1)
                    settle(act)
                    act.activation(sgel[i % 2][:], bank[:, 2 * (i % 2), :], ACT.Gelu,
                                   bias=sb1[:, KS + i:KS + i + 1]).then_inc(gelu_made, 1)

            def glu_part(dve, j, s, i):
                c = j * KS + i
                dve.wait_ge(x_done, c + 1)
                dve.wait_ge(gelu_made, c + 1)
                wait(dve, o_done, 2 * (j - 1))
                settle(dve)
                dve.scalar_tensor_tensor(sglu[s][:, i, :], bank[:, 2 * (i % 2) + 1, :], sb1[:, i:i + 1],
                                         sgel[i % 2][:], ALU.add, ALU.mult).then_inc(glu_made, 1)

            def glus(dve, j, s):
                for i in range(KS):
                    glu_part(dve, j, s, i)

            def add_out(dve, j, s):
                dve.wait_ge(xm_loaded[s], (j - s) * 8 + 16)
                dve.tensor_tensor(xm[s][:], xm[s][:], sb2[:].unsqueeze(1).to_broadcast([P, GT, D]), ALU.add)\
                   .then_inc(bias_in, 1)
                dve.wait_ge(bias_in, j + 1)
                for p in range(2):
                    dve.wait_ge(o_done, 2 * j + p + 1)
                    dve.tensor_tensor(xm[s][:, 2 * p:2 * p + 2, :], xm[s][:, 2 * p:2 * p + 2, :],
                                      bank[:, 6 + p, :].rearrange("p (i d) -> p i d", i=2), ALU.add)\
                       .then_inc(acc_made, 1)

            sh.load_xm, sh.store, sh.xm, sh.acc_made = load_xm, store, xm, acc_made
            (sh.load_xa, sh.move, sh.move_last, sh.products, sh.copy_xT, sh.gelus, sh.glu_part, sh.glus, sh.add_out) = (
                load_xa, move, move_last, products, copy_xT, gelus, glu_part, glus, add_out)
            return sh

        with ExitStack() as part:
            def sb(name, shape, dt=F32):
                return part.enter_context(nc.sbuf_tensor(name, shape, dt))

            a_neg = sb("a_neg", [P, KD, N])
            pick = sb("pick", [3 * Q, N, P], BF16)
            pick_c = sb("pick_c", [3 * Q, N], BF16)
            bc3 = sb("bc3", [3 * Q, TOK], BF16)
            c_tok = sb("c_tok", [P, TILES, N])
            iota_i = sb("iota_i", [P, E], I32)
            in_bounds = sb("in_bounds", [P, NORMS])
            tanh_bias = sb("tanh_bias", [P, 1])
            weights_part = ExitStack()

            def sb(name, shape, dt=F32):
                return weights_part.enter_context(nc.sbuf_tensor(name, shape, dt))

            wdt = sb("wdt", [P, KD, D])
            wbc = sb("wbc", [P, KD, 3 * Q])
            dbc = sb("dbc", [P, D])
            bdt = sb("bdt", [P, KD])
            one_col = sb("one_col", [P, 1])
            pick_f = sb("pick_f", [3 * Q, Q])
            load_part = ExitStack()

            def sb(name, shape, dt=F32):
                return load_part.enter_context(nc.sbuf_tensor(name, shape, dt))

            CH = GT * P
            xin = [sb(f"xin{c}", [P, GT, D]) for c in range(4)]
            xn = [sb(f"xn{s}", [P, GT, D]) for s in range(2)]
            dx = [sb(f"dx{s}", [P, GT, D]) for s in range(2)]
            stats = [sb(f"stats{s}", [P, GT, 6]) for s in range(2)]
            meanvar = [sb(f"meanvar{s}", [P, GT, 2]) for s in range(2)]
            rstd = [sb(f"rstd{s}", [P, GT]) for s in range(2)]
            mag = [sb(f"mag{s}", [P, KD, CH]) for s in range(2)]
            top = [sb(f"top{s}", [3 * Q, CH], BF16) for s in range(2)]
            rest = [sb(f"rest{s}", [3 * Q, CH]) for s in range(2)]
            mid = [sb(f"mid{s}", [3 * Q, CH], BF16) for s in range(2)]

            c_loaded = sem("c_loaded")
            c_made = sem("c_made")
            c_a = sem("c_a")
            x_loaded, skip_stored = sems("x_loaded", 4), sems("skip_stored", 4)
            (projected, mag_made, e_made, l_made, pos_made, sp_made, top_made, rest_made, mid_made,
             parts_made, c_turned, c_kept) = [sem(n) for n in (
                 "projected", "mag_made", "e_made", "l_made", "pos_made", "sp_made", "top_made", "rest_made",
                 "mid_made", "parts_made", "c_turned", "c_kept")]
            (stats_made, aggregated, eps_added, rstd_made, xn_made, xn_turned, xT_written, dx_made,
             skip_made) = [sem(n) for n in (
                 "stats_made", "aggregated", "eps_added", "rstd_made", "xn_made", "xn_turned", "xT_written", "dx_made",
                 "skip_made")]

            with nc.Block() as block:
                @block.sync
                def _(sp):
                    sp.dma_start(wdt[:], W_dt_t.rearrange("(k p) e -> p k e", p=P)).then_inc(c_loaded, 16)
                    sp.wait_ge(c_made, 1)
                    for q in range(3):
                        for k in range(KD):
                            sp.dma_start(wbc[:, k, q * Q:q * Q + 2 * N], W_bc_t[k * P:(k + 1) * P, :])\
                              .then_inc(c_loaded, 16)
                    sp.dma_start(dbc[:], D_param.partition_broadcast(P)).then_inc(c_loaded, 16)
                    with nc.allow_non_contiguous_dma(reason="small constants, once"):
                        sp.dma_start(bdt[:], b_dt.rearrange("(k p) -> p k", p=P)).then_inc(c_loaded, 16)
                    sp.dma_start(a_neg[:], A_log.rearrange("(k p) n -> p k n", p=P)).then_inc(c_loaded, 16)

                    def load(g, c):
                        sp.dma_start(xin[c][:], group_rows(x_rows, g)).then_inc(x_loaded[c], 16)

                    for c in range(4):
                        load(c, c)

                    def step(it, c, g):
                        sp.wait_ge(skip_made, g + 1)
                        sp.dma_start(group_rows(x_skip, g), xin[c][:]).then_inc(skip_stored[c], 16)
                        sp.wait_ge(skip_stored[c], (g - c) * 4 + 16)
                        if not isinstance(g, int) or g + 4 < GROUPS:
                            load(g + 4, c)
                    steps(sp, GROUPS, step, 4)

                @block.gpsimd
                def _(pool):
                    pool.memset(wbc[:], 0.0).then_inc(c_made, 1)
                    pool.memset(ident[:], 0.0).then_inc(c_made, 1)
                    pool.memset(pick_f[:], 0.0).then_inc(c_made, 1)
                    pool.memset(ones[:], 1.0).then_inc(c_made, 1)
                    pool.memset(minus_half[:], -0.5).then_inc(c_made, 1)
                    pool.memset(half[:], 0.5).then_inc(c_made, 1)
                    pool.memset(tanh_bias[:], -DT_MID * SHARP / (DT_HALF + 1e-8)).then_inc(c_made, 1)
                    pool.memset(one_col[:], 1.0).then_inc(c_made, 1)
                    pool.iota(iota_i[:], pattern=[[1, E]], base=0, channel_multiplier=0).then_inc(c_made, 1)
                    pool.wait_ge(c_made, 9)
                    pool.affine_select(out=ident[:], in_=ident[:], compare_op=ALU.not_equal, fill=1.0,
                                       base=0, pattern=[[-1, P]], channel_multiplier=1).then_inc(c_made, 1)
                    for q in range(3):
                        pool.affine_select(out=pick_f[:], in_=pick_f[:], compare_op=ALU.not_equal, fill=1.0,
                                           base=-q * Q, pattern=[[-1, Q]], channel_multiplier=1).then_inc(c_made, 1)
                        pool.wait_ge(c_made, 11 + q)
                    pool.tensor_copy(expert_no[:], iota_i[:]).then_inc(c_made, 1)
                    pool.tensor_copy(pick[:], pick_f[:, 0:N].unsqueeze(2).to_broadcast([3 * Q, N, P]))\
                        .then_inc(c_made, 1)
                    pool.tensor_copy(pick_c[:], pick_f[:, N:2 * N]).then_inc(c_made, 1)

                    def rstds(g, s):
                        pool.wait_ge(aggregated, g + 1)
                        wait(pool, xn_made, g - 1)
                        settle(pool)
                        pool.tensor_scalar(rstd[s][:], meanvar[s][:, :, 1], EPS, None, ALU.add).then_inc(eps_added, 1)
                        pool.wait_ge(eps_added, g + 1)
                        pool.tensor_tensor(rstd[s][:], rstd[s][:], minus_half[:].to_broadcast([P, GT]), ALU.pow)\
                            .then_inc(rstd_made, 1)

                    def add_skip(g, c):
                        pool.wait_ge(dx_made, g + 1)
                        pool.tensor_tensor(xin[c][:], xin[c][:], dx[c % 2][:], ALU.add).then_inc(skip_made, 1)

                    def add_log(j, s):
                        pool.wait_ge(pos_made, j + 1)
                        pool.wait_ge(l_made, j + 1)
                        settle(pool)
                        dt_j = dtT[:, :, ds(j * CH, CH)]
                        pool.tensor_tensor(dt_j, dt_j, mag[s][:], ALU.add).then_inc(sp_made, 1)

                    def step(it, c, g):
                        rstds(g, c % 2)
                        if not isinstance(g, int) or g > 0:
                            add_skip(g - 1, (c - 1) % 4)
                        if not isinstance(g, int) or g > 2:
                            add_log(g - 3, 1 - c % 2)
                    steps(pool, GROUPS, step, 4)
                    add_skip(GROUPS - 1, 3)
                    add_log(GROUPS - 3, 1)
                    add_log(GROUPS - 2, 0)
                    add_log(GROUPS - 1, 1)

                @block.vector
                def _(dve):
                    def measure(g, c):
                        s = c % 2
                        dve.wait_ge(x_loaded[c], (g - c) * 4 + 16)
                        wait(dve, aggregated, g - 1)
                        settle(dve)
                        for i in range(GT):
                            dve.bn_stats(stats[s][:, i, :], xin[c][:, i, :]).then_inc(stats_made, 1)
                        dve.wait_ge(stats_made, GT * (g + 1))
                        wait(dve, rstd_made, g - 1)
                        settle(dve)
                        for i in range(GT):
                            last = dve.bn_aggr(meanvar[s][:, i, :], stats[s][:, i, :])
                        last.then_inc(aggregated, 1)

                    def normalise(g, c):
                        s = c % 2
                        dve.wait_ge(rstd_made, g + 1)
                        dve.wait_ge(aggregated, g + 1)
                        wait(dve, xn_turned, g - 1)
                        wait(dve, dx_made, g - 1)
                        settle(dve)
                        for i in range(GT):
                            last = dve.tensor_scalar(xn[s][:, i, :], xin[c][:, i, :], meanvar[s][:, i, 0:1],
                                                     rstd[s][:, i:i + 1], ALU.subtract, ALU.mult)
                        last.then_inc(xn_made, 1)

                    def times_d(g, s):
                        dve.wait_ge(xn_made, g + 1)
                        wait(dve, skip_made, g - 1)
                        dve.tensor_tensor(dx[s][:], xn[s][:], dbc[:].unsqueeze(1).to_broadcast([P, GT, D]), ALU.mult)\
                           .then_inc(dx_made, 1)

                    def positive(j, s):
                        dve.wait_ge(projected, j + 1)
                        settle(dve)
                        for e in range(KD):
                            last = dve.tensor_scalar(dtT[:, e, ds(j * CH, CH)], bank[:, 2 * s + e, :], bdt[:, e:e + 1],
                                                     0.0, ALU.add, ALU.max)
                        last.then_inc(pos_made, 1)
                        dve.wait_ge(top_made, j + 1)
                        dve.tensor_tensor(rest[s][:], bank[0:3 * Q, 4, :], top[s][:], ALU.subtract)\
                           .then_inc(rest_made, 1)

                    def parts(j, s):
                        dve.wait_ge(mid_made, j + 1)
                        dve.wait_ge(rest_made, j + 1)
                        here = ds(j * CH, CH)
                        dve.tensor_copy(bc3[0:Q, here], top[s][0:Q, :]).then_inc(parts_made, 1)
                        dve.tensor_copy(bc3[Q:2 * Q, here], mid[s][Q:2 * Q, :]).then_inc(parts_made, 1)
                        dve.tensor_tensor(bc3[2 * Q:3 * Q, here], rest[s][2 * Q:3 * Q, :], mid[s][2 * Q:3 * Q, :],
                                          ALU.subtract).then_inc(parts_made, 1)

                    def keep_c(j):
                        dve.wait_ge(c_turned, j + 1)
                        dve.tensor_copy(c_tok[:, ds(j * GT, GT), :],
                                        bank[:, 7, 0:GT * N].rearrange("p (i n) -> p i n", n=N))\
                           .then_inc(c_kept, 1)

                    dve.sem_inc(c_kept, 1)
                    measure(0, 0)
                    dve.wait_ge(c_loaded, 160)

                    def step(it, c, g):
                        s = c % 2
                        if not isinstance(g, int) or g + 1 < GROUPS:
                            measure(g + 1, (c + 1) % 4)
                        normalise(g, c)
                        times_d(g, s)
                        if not isinstance(g, int) or g > 1:
                            positive(g - 2, s)
                        if not isinstance(g, int) or g > 2:
                            parts(g - 3, 1 - s)
                        if not isinstance(g, int) or g > 3:
                            keep_c(g - 4)
                    steps(dve, GROUPS, step, 4)
                    for j in (GROUPS - 2, GROUPS - 1):
                        positive(j, j % 2)
                        parts(j - 1, 1 - j % 2)
                        keep_c(j - 2)
                    parts(GROUPS - 1, 1)
                    keep_c(GROUPS - 2)
                    keep_c(GROUPS - 1)

                @block.tensor
                def _(pe):
                    pe.wait_ge(c_made, 16)
                    pe.wait_ge(c_loaded, 160)

                    def turn(g, s):
                        pe.wait_ge(xn_made, g + 1)
                        wait(pe, xT_written, g)
                        for k in range(KD):
                            for i in range(GT):
                                last = pe.transpose(bank[:, 5 + k, i * P:(i + 1) * P], xn[s][:, i, k * P:(k + 1) * P],
                                                    ident[:])
                        last.then_inc(xn_turned, 1)

                    def project(j, s):
                        here = ds(j * CH, CH)
                        pe.wait_ge(xT_written, j + 1)
                        wait(pe, mag_made, j - 1)
                        for e in range(KD):
                            for k in range(KD):
                                pe.matmul(bank[:, 2 * s + e, :], wdt[:, k, e * P:(e + 1) * P],
                                          xT[:, k, here], start=(k == 0), stop=(k == KD - 1))
                        wait(pe, rest_made, j)
                        for k in range(KD):
                            last = pe.matmul(bank[0:3 * Q, 4, :], wbc[:, k, :], xT[:, k, here],
                                             start=(k == 0), stop=(k == KD - 1))
                        last.then_inc(projected, 1)

                    def turn_c(j):
                        pe.wait_ge(parts_made, 3 * (j + 1))
                        pe.wait_ge(c_kept, j + 1)
                        for i in range(GT):
                            last = pe.matmul(bank[:, 7, i * N:(i + 1) * N], bc3[:, ds(j * CH + i * P, P)],
                                             pick_c[:], start=True, stop=True)
                        last.then_inc(c_turned, 1)

                    def step(it, c, g):
                        s = c % 2
                        turn(g, s)
                        if not isinstance(g, int) or g > 3:
                            turn_c(g - 4)
                        if not isinstance(g, int) or g > 0:
                            project(g - 1, 1 - s)
                    steps(pe, GROUPS, step, 4)
                    project(GROUPS - 1, 1)
                    for j in range(GROUPS - 4, GROUPS):
                        turn_c(j)

                @block.scalar
                def _(act):
                    act.wait_ge(c_loaded, 160)
                    act.activation(a_neg[:], a_neg[:], ACT.Tanh, scale=SHARP / (A_HALF + 1e-8)).then_inc(c_a, 1)
                    act.wait_ge(c_a, 1)
                    act.activation(a_neg[:], a_neg[:], ACT.Exp, scale=A_HALF / SHARP).then_inc(c_a, 1)
                    act.wait_ge(c_a, 2)
                    act.mul(a_neg[:], a_neg[:], -SHARP / (DA_HALF + 1e-8)).then_inc(c_a, 1)
                    act.wait_ge(c_a, 3)
                    act.preload_act_table_set("natural_log_exp_and_others")

                    def copy_xT(g):
                        act.wait_ge(xn_turned, g + 1)
                        act.activation(xT[:, :, ds(g * CH, CH)], bank[:, 5:7, :], ACT.Copy).then_inc(xT_written, 1)

                    def logs(j, s):
                        act.wait_ge(projected, j + 1)
                        wait(act, parts_made, 3 * (j - 1))
                        act.activation(top[s][:], bank[0:3 * Q, 4, :], ACT.Copy).then_inc(top_made, 1)
                        act.wait_ge(pos_made, j + 1)
                        wait(act, sp_made, j - 1)
                        settle(act)
                        for e in range(KD):
                            last = act.activation(mag[s][:, e, :], bank[:, 2 * s + e, :], ACT.Abs, bias=bdt[:, e:e + 1])
                        last.then_inc(mag_made, 1)
                        act.wait_ge(mag_made, j + 1)
                        act.activation(mag[s][:], mag[s][:], ACT.Exp, scale=-1.0).then_inc(e_made, 1)
                        act.wait_ge(e_made, j + 1)
                        act.activation(mag[s][:], mag[s][:], ACT.Ln, bias=one_col[:, 0:1]).then_inc(l_made, 1)
                        act.wait_ge(rest_made, j + 1)
                        act.activation(mid[s][:], rest[s][:], ACT.Copy).then_inc(mid_made, 1)

                    def step(it, c, g):
                        copy_xT(g)
                        if not isinstance(g, int) or g > 1:
                            logs(g - 2, c % 2)
                    steps(act, GROUPS, step, 4)
                    logs(GROUPS - 2, 0)
                    logs(GROUPS - 1, 1)
            load_part.close()
            end_phase()
            weights_part.close()
            gT = arena_x[:, :].rearrange("p (k b t) -> p k b t", k=KD, b=NB)
            dtT4 = arena_dt[:, :].rearrange("p (k b t) -> p k b t", k=KD, b=NB)
            bc3v = bc3[:, :].rearrange("r (b t) -> r b t", b=NB)

            fast_part = ExitStack()

            def sb(name, shape, dt=F32):
                return fast_part.enter_context(nc.sbuf_tensor(name, shape, dt))

            TB = T // P
            PAIRS = TB // 2
            TH = T // 2
            decay = [sb(f"decay{s}", [P, KD, T]) for s in range(2)]
            state = [sb(f"state{s}", [P, KD, T]) for s in range(2)]
            b_all = [[sb(f"b_all{s}_{hf}", [P, TH]) for hf in range(2)] for s in range(2)]
            sq = [sb(f"state_sq{s}", [P, KD, NORMS]) for s in range(2)]
            y_acc = [sb(f"y_acc{s}", [P, TB, D]) for s in range(2)]
            all_in = sb("all_in", [P, 1])
            tanh_made, decay_made, b_spread, b_copied, u_made = (
                sem("z_tanh"), sem("decay_made"), sem("b_spread"), sem("b_copied"), sem("u_made"))
            scanned, turned, y_added, sq_made, sq_summed = (
                sem("scanned"), sem("turned"), sem("y_added"), sem("sq_made"), sem("sq_summed"))
            norms_checked, bounds_clear, checked = sem("norms_checked"), sem("bounds_clear"), sem("checked")
            acc_loaded, acc_stored = sems("acc_loaded"), sems("acc_stored")
            dt_tanh, dt_made, g_made = sem("dt_tanh"), sem("dt_made"), sem("g_made")
            UNITS = NB * N

            def batch_of(buf, b):
                return buf[:, :, ds(b, 1), :].rearrange("p k o t -> p k (o t)")

            with nc.Block() as block:
                def units(eng, body):
                    def pair(it):
                        for bs in range(2):
                            for n in range(N):
                                body(it * 2 + bs, bs, n, it * (2 * N) + bs * N + n)
                    pair(0)
                    with eng.Fori(1, NB // 2 - 1) as it:
                        pair(it)
                    pair(NB // 2 - 1)

                def more(b):
                    return not isinstance(b, int) or b + 1 < NB

                @block.scalar
                def _(act):
                    act.preload_act_table_set("exp_and_others")

                    def clamp_dt(b):
                        act.activation(batch_of(dtT4, b), batch_of(dtT4, b), ACT.Tanh, bias=tanh_bias[:, 0:1],
                                       scale=SHARP / (DT_HALF + 1e-8)).then_inc(dt_tanh, 1)

                    clamp_dt(0)

                    def square(n, j):
                        s = n % 2
                        act.wait_ge(scanned, j + 1)
                        wait(act, sq_summed, j - 1)
                        act.activation(sq[s][:], state[s][:, :, 0:T:SEG], ACT.Square).then_inc(sq_made, 1)

                    def body(b, bs, n, j):
                        s = n % 2
                        for hf in range(2):
                            act.wait_ge(b_spread, 2 * j + hf + 1)
                            wait(act, u_made, 2 * (j - 2) + hf + 1)
                            act.activation(b_all[s][hf][:], bank[:, hf, :], ACT.Copy).then_inc(b_copied, 1)
                        if n == 0:
                            act.wait_ge(dt_made, b + 1)
                        wait(act, scanned, j - 1)
                        settle(act)
                        for k in range(KD):
                            last = act.activation(decay[s][:, k, :],
                                                  dtT4[:, k, ds(b, 1), :].rearrange("p o t -> p (o t)"),
                                                  ACT.Tanh, scale=a_neg[:, k, n:n + 1])
                        last.then_inc(tanh_made, 1)
                        act.wait_ge(tanh_made, j + 1)
                        act.activation(decay[s][:], decay[s][:], ACT.Exp, scale=DA_HALF / SHARP)\
                           .then_inc(decay_made, 1)
                        if not isinstance(j, int) or j > 0:
                            square(n + N - 1, j - 1)
                        if n == 1 and more(b):
                            clamp_dt(b + 1)
                    units(act, body)
                    square(N - 1, UNITS - 1)

                @block.gpsimd
                def _(pool):
                    def times_dt(b, k):
                        pool.wait_ge(dt_made, b + 1)
                        settle(pool)
                        g_k = gT[:, k, ds(b, 1), :].rearrange("p o t -> p (o t)")
                        pool.tensor_tensor(g_k, g_k, dtT4[:, k, ds(b, 1), :].rearrange("p o t -> p (o t)"), ALU.mult)\
                            .then_inc(g_made, 1)

                    for k in range(KD):
                        times_dt(0, k)

                    def body(b, bs, n, j):
                        s = n % 2
                        for hf in range(2):
                            pool.wait_ge(b_copied, 2 * j + hf + 1)
                            wait(pool, turned, PAIRS * (j - 2) + (hf + 1) * (PAIRS // 2))
                            wait(pool, sq_made, j - 1)
                            if n == 0 and hf == 0:
                                pool.wait_ge(g_made, KD * (b + 1))
                            settle(pool)
                            pool.tensor_tensor(
                                state[s][:, :, hf * TH:(hf + 1) * TH],
                                gT[:, :, ds(b, 1), hf * TH:(hf + 1) * TH].rearrange("p k o t -> p k (o t)"),
                                b_all[s][hf][:].unsqueeze(1).to_broadcast([P, KD, TH]), ALU.mult).then_inc(u_made, 1)
                        if n in (4, 6) and more(b):
                            times_dt(b + 1, (n - 4) // 2)
                    units(pool, body)

                @block.tensor
                def _(pe):
                    def spread(b, n, j):
                        for hf in range(2):
                            wait(pe, b_copied, 2 * (j - 1) + hf + 1)
                            pe.matmul(bank[:, hf, :], pick[:, n, :],
                                      bc3v[:, ds(b, 1), hf * TH:(hf + 1) * TH].rearrange("r o t -> r (o t)"),
                                      start=True, stop=True).then_inc(b_spread, 1)

                    def turn(n, j):
                        s = n % 2
                        pe.wait_ge(scanned, j + 1)
                        for p in range(PAIRS):
                            wait(pe, y_added, PAIRS * (j - 1) + p + 1)
                            settle(pe)
                            for i in range(2):
                                for k in range(KD):
                                    t0 = (2 * p + i) * P
                                    last = pe.transpose(bank[:, 2 + p, i * D + k * P:i * D + (k + 1) * P],
                                                        state[s][:, k, t0:t0 + P], ident[:])
                            last.then_inc(turned, 1)

                    def add_squares(b, bs, n, j):
                        pe.wait_ge(sq_made, j + 1)
                        if n == 0:
                            wait(pe, norms_checked, b - 1)
                            settle(pe)
                        for k in range(KD):
                            last = pe.matmul(bank[:, 6 + bs, 0:NORMS], ones[:], sq[n % 2][:, k, :],
                                             start=(n == 0 and k == 0), stop=(n == N - 1 and k == KD - 1))
                        last.then_inc(sq_summed, 1)

                    spread(0, 0, 0)
                    spread(0, 1, 1)

                    def body(b, bs, n, j):
                        if not isinstance(j, int) or j + 2 < UNITS:
                            spread(b + (n + 2) // N, (n + 2) % N, j + 2)
                        turn(n, j)
                        if not isinstance(j, int) or j > 0:
                            if n == 0:
                                add_squares(b - 1, 1 - bs, N - 1, j - 1)
                            else:
                                add_squares(b, bs, n - 1, j - 1)

                    for j in range(2 * N):
                        body(j // N, j // N, j % N, j)
                    with pe.Fori(1, NB // 2 - 1) as it:
                        for i in range(2 * N):
                            body(it * 2 + i // N, i // N, i % N, it * (2 * N) + i)
                    for j in range(UNITS - 2 * N, UNITS):
                        body(j // N, j // N % 2, j % N, j)
                    add_squares(NB - 1, 1, N - 1, UNITS - 1)

                @block.vector
                def _(dve):
                    dve.memset(in_bounds[:], 1.0).then_inc(bounds_clear, 1)
                    dve.wait_ge(bounds_clear, 1)

                    def check(b, bs):
                        dve.wait_ge(sq_summed, (b + 1) * N)
                        settle(dve)
                        dve.scalar_tensor_tensor(in_bounds[:], bank[:, 6 + bs, 0:NORMS], NORM2_SURE, in_bounds[:],
                                                 ALU.is_le, ALU.min).then_inc(norms_checked, 1)
                        dve.wait_ge(norms_checked, b + 1)

                    def make_dt(b):
                        dve.wait_ge(dt_tanh, b + 1)
                        settle(dve)
                        dve.tensor_scalar(batch_of(dtT4, b), batch_of(dtT4, b), DT_HALF / SHARP, DT_MID, ALU.mult,
                                          ALU.add).then_inc(dt_made, 1)

                    make_dt(0)

                    def add_y(b, bs, n, j):
                        s = n % 2
                        if n == 0:
                            dve.wait_ge(acc_loaded[bs], (b - bs) * 8 + 16)
                        for p in range(PAIRS):
                            dve.wait_ge(turned, PAIRS * j + p + 1)
                            wait(dve, y_added, PAIRS * (j - 1) + p + 1)
                            for i in range(2):
                                block_no = 2 * p + i
                                last = dve.scalar_tensor_tensor(
                                    y_acc[bs][:, block_no, :], bank[:, 2 + p, i * D:(i + 1) * D],
                                    c_tok[:, ds(b * TB + block_no, 1), n:n + 1].rearrange("p o n -> p (o n)"),
                                    y_acc[bs][:, block_no, :], ALU.mult, ALU.add)
                            last.then_inc(y_added, 1)

                    def body(b, bs, n, j):
                        s = n % 2
                        dve.wait_ge(decay_made, j + 1)
                        dve.wait_ge(u_made, 2 * j + 2)
                        for k in range(KD):
                            last = dve.tensor_tensor_scan(state[s][:, k, :], decay[s][:, k, :], state[s][:, k, :],
                                                          0.0, ALU.mult, ALU.add)
                        last.then_inc(scanned, 1)
                        if n == 2 and (not isinstance(j, int) or b > 0):
                            check(b - 1, 1 - bs)
                        if not isinstance(j, int) or j > 0:
                            if n == 0:
                                add_y(b - 1, 1 - bs, N - 1, j - 1)
                            else:
                                add_y(b, bs, n - 1, j - 1)
                        if n == 2 and more(b):
                            make_dt(b + 1)
                    units(dve, body)
                    add_y(NB - 1, 1, N - 1, UNITS - 1)
                    check(NB - 1, 1)
                    dve.tensor_reduce(all_in[:], in_bounds[:], AX.X, ALU.min).then_inc(checked, 1)
                    dve.wait_ge(checked, 1)
                    dve.tensor_scalar(out_of_bounds[:], all_in[:], 0.5, None, ALU.is_lt).then_inc(checked, 1)
                    dve.wait_ge(checked, 2)

                @block.sync
                def _(sp):
                    def rows_of(t, b):
                        return t[ds(b * T, T), :].rearrange("(i p) d -> p i d", p=P)

                    def load(b, bs, earlier):
                        if earlier:
                            sp.wait_ge(acc_stored[bs], (b - bs) * 8)
                        sp.dma_start(y_acc[bs][:], rows_of(x_skip, b)).then_inc(acc_loaded[bs], 16)

                    def store(b, bs):
                        sp.wait_ge(y_added, (b + 1) * (N * PAIRS))
                        sp.dma_start(rows_of(x_mid, b), y_acc[bs][:]).then_inc(acc_stored[bs], 16)

                    load(0, 0, False)
                    load(1, 1, False)
                    store(0, 0)
                    with sp.Fori(1, NB // 2) as it:
                        load(it * 2, 0, True)
                        store(it * 2 - 1, 1)
                        load(it * 2 + 1, 1, True)
                        store(it * 2, 0)
                    store(NB - 1, 1)
                    for bs in range(2):
                        sp.wait_ge(acc_stored[bs], 16 * (NB // 2))
            fast_part.close()
            end_phase()

            rescaled = nc.values_load(out_of_bounds[0:1, 0:1], min_val=0, max_val=1)
            with nc.If(rescaled > 0):
                nc.all_engine_barrier()
                scan_part = ExitStack()

                def sb(name, shape, dt=F32):
                    return scan_part.enter_context(nc.sbuf_tensor(name, shape, dt))

                W = R * NB
                dA = [sb(f"dA{s}", [P, W * SEG]) for s in range(2)]
                u = sb("u", [P, W * SEG])
                h = sb("h", [P, W * SEG])
                hc = sb("hc", [P, W * SEG])
                t1 = sb("t1", [P, W])
                h0 = sb("h0", [P, W])
                sq = sb("sq", [P, W])
                h_last = sb("h_last", [P, W])
                norm2 = sb("norm2", [P, NB])
                norm = sb("norm", [P, NB])
                scale = sb("scale", [P, NB])

                z_made, tanh_z, dA_made, scanned = sems("z_made"), sems("tanh_z"), sems("dA_made"), sems("scanned")
                b_spread, c_spread, u_made, hc_made = sem("b_spread"), sem("c_spread"), sem("u_made"), sem("hc_made")
                decayed, h0_made, sq_made, sq_summed = sem("decayed"), sem("h0_made"), sem("sq_made"), sem("sq_summed")
                norm2_made, norm_made, eps_in, inv_made = sem("norm2_made"), sem("norm_made"), sem("eps_in"), sem("inv_made")
                scale_made, h0_in, dA_cut, y_made, last_kept = (sem("scale_made"), sem("h0_in"), sem("dA_cut"),
                                                                 sem("y_made"), sem("last_kept"))
                first_state, pick_made = sem("first_state"), sem("pick_made")
                pick_c_all = sb("pick_c_all", [3 * Q, N, P], BF16)

                def rows(buf, L):
                    return buf[:, 0:W * L].rearrange("p (k n b t) -> p k n b t", k=KD, n=N, b=NB)

                def flat_rows(buf, L):
                    return buf[:, 0:W * L].rearrange("p (r b t) -> p r b t", r=R, b=NB)

                HN = N // 2

                def spread(half_no, first_bank, L):
                    return bank[:, first_bank + half_no, 0:HN * NB * L].rearrange("p (n b t) -> p n b t", n=HN, b=NB)

                with nc.Block() as block:
                    def segments(eng, body):
                        def pair(it):
                            for s in range(2):
                                body(it, s, it * 2 + s, SEG)
                        rounds(eng, NSEG // 2, pair)
                        body(NSEG // 2, 0, NSEG, TAIL)

                    @block.gpsimd
                    def _(pool):
                        def body(it, s, seg, L):
                            wait(pool, scanned[s], it)
                            z = rows(dA[s], L)
                            for k in range(KD):
                                last = pool.tensor_tensor(
                                    z[:, k], dtT4[:, k, :, ds(seg * SEG, L)].unsqueeze(1).to_broadcast([P, N, NB, L]),
                                    a_neg[:, k, :].unsqueeze(2).unsqueeze(3).to_broadcast([P, N, NB, L]), ALU.mult)
                            last.then_inc(z_made[s], 1)
                            pool.wait_ge(norm2_made, seg + 1)
                            pool.tensor_tensor(norm[:], norm2[:], half[:, 0:NB], ALU.pow).then_inc(norm_made, 1)
                        segments(pool, body)

                    @block.scalar
                    def _(act):
                        act.preload_act_table_set("exp_and_others")

                        def body(it, s, seg, L):
                            z = dA[s][:, 0:W * L]
                            act.wait_ge(z_made[s], it + 1)
                            act.activation(z, z, ACT.Tanh).then_inc(tanh_z[s], 1)
                            act.wait_ge(tanh_z[s], it + 1)
                            act.activation(z, z, ACT.Exp, scale=DA_HALF / SHARP).then_inc(dA_made[s], 1)
                        segments(act, body)

                    @block.tensor
                    def _(pe):
                        def body(it, s, seg, L):
                            for half_no in range(2):
                                if half_no == 0:
                                    wait(pe, u_made, seg)
                                    settle(pe)
                                for n in range(HN):
                                    last = pe.matmul(spread(half_no, 0, L)[:, n], pick[:, half_no * HN + n, :],
                                                     bc3v[:, :, ds(seg * SEG, L)], start=True, stop=True)
                            last.then_inc(b_spread, 1)
                            for half_no in range(2):
                                if half_no == 0:
                                    wait(pe, hc_made, seg)
                                    settle(pe)
                                for n in range(HN):
                                    last = pe.matmul(spread(half_no, 2, L)[:, n], pick_c_all[:, half_no * HN + n, :],
                                                     bc3v[:, :, ds(seg * SEG, L)], start=True, stop=True)
                            last.then_inc(c_spread, 1)
                            pe.wait_ge(sq_made, seg + 1)
                            wait(pe, norm2_made, seg)
                            pe.matmul(bank[:, 4, 0:W], ones[:], sq[:], start=True, stop=True).then_inc(sq_summed, 1)
                        pe.wait_ge(pick_made, 1)
                        segments(pe, body)

                    @block.vector
                    def _(dve):
                        dve.tensor_copy(pick_c_all[:], pick_c[:].unsqueeze(2).to_broadcast([3 * Q, N, P]))\
                           .then_inc(pick_made, 1)
                        dve.memset(h_last[:], 0.0).then_inc(first_state, 1)
                        dve.wait_ge(first_state, 1)

                        def body(it, s, seg, L):
                            at = ds(seg * SEG, L)
                            uu, cc = rows(u, L), rows(hc, L)
                            dve.wait_ge(b_spread, seg + 1)
                            for k in range(KD):
                                for half_no in range(2):
                                    n0 = half_no * HN
                                    last = dve.tensor_tensor(
                                        uu[:, k, n0:n0 + HN], gT[:, k, :, at].unsqueeze(1).to_broadcast([P, HN, NB, L]),
                                        spread(half_no, 0, L), ALU.mult)
                            last.then_inc(u_made, 1)
                            dve.wait_ge(dA_made[s], it + 1)
                            wait(dve, last_kept, seg)
                            d3 = flat_rows(dA[s], L)
                            u3 = flat_rows(u, L)
                            h3 = flat_rows(h, L)

                            def grid(buf):
                                return buf[:].rearrange("p (r b) -> p r b", r=R)

                            dve.tensor_tensor(grid(t1), grid(h_last), d3[:, :, :, 0], ALU.mult).then_inc(decayed, 1)
                            dve.wait_ge(decayed, seg + 1)
                            dve.wait_ge(u_made, seg + 1)
                            dve.tensor_tensor(grid(h0), grid(t1), u3[:, :, :, 0], ALU.add).then_inc(h0_made, 1)
                            dve.memset(d3[:, :, :, 0], 0.0).then_inc(dA_cut, 1)
                            dve.wait_ge(h0_made, seg + 1)
                            dve.tensor_tensor(sq[:], h0[:], h0[:], ALU.mult).then_inc(sq_made, 1)
                            dve.wait_ge(sq_summed, seg + 1)
                            dve.tensor_reduce(norm2[:], bank[:, 4, 0:W].rearrange("p (r b) -> p b r", r=R), AX.X,
                                              ALU.add).then_inc(norm2_made, 1)
                            dve.wait_ge(norm_made, seg + 1)
                            dve.tensor_scalar(norm[:], norm[:], 1e-8, None, ALU.add).then_inc(eps_in, 1)
                            dve.wait_ge(eps_in, seg + 1)
                            dve.reciprocal(scale[:], norm[:]).then_inc(inv_made, 1)
                            dve.wait_ge(inv_made, seg + 1)
                            dve.tensor_scalar(scale[:], scale[:], NORM_MAX, 1.0, ALU.mult, ALU.min).then_inc(scale_made, 1)
                            dve.wait_ge(scale_made, seg + 1)
                            dve.tensor_tensor(u3[:, :, :, 0], grid(h0), scale[:].unsqueeze(1).to_broadcast([P, R, NB]),
                                              ALU.mult).then_inc(h0_in, 1)
                            dve.wait_ge(h0_in, seg + 1)
                            dve.wait_ge(dA_cut, seg + 1)
                            dve.tensor_tensor_scan(h[:, 0:W * L], dA[s][:, 0:W * L], u[:, 0:W * L], 0.0, ALU.mult,
                                                   ALU.add).then_inc(scanned[s], 1)
                            dve.wait_ge(scanned[s], it + 1)
                            dve.tensor_copy(grid(h_last), h3[:, :, :, L - 1]).then_inc(last_kept, 1)
                            dve.wait_ge(c_spread, seg + 1)
                            for k in range(KD):
                                for half_no in range(2):
                                    n0 = half_no * HN
                                    last = dve.tensor_tensor(cc[:, k, n0:n0 + HN], rows(h, L)[:, k, n0:n0 + HN],
                                                             spread(half_no, 2, L), ALU.mult)
                            last.then_inc(hc_made, 1)
                            dve.wait_ge(hc_made, seg + 1)
                            settle(dve)
                            for k in range(KD):
                                last = dve.tensor_reduce(gT[:, k, :, at], cc[:, k].rearrange("p n b t -> p b t n"), AX.X,
                                                         ALU.add)
                            last.then_inc(y_made, 1)
                            dve.wait_ge(y_made, seg + 1)
                        segments(dve, body)
                scan_part.close()
                end_phase()

                turn_part = ExitStack()

                def sb(name, shape, dt=F32):
                    return turn_part.enter_context(nc.sbuf_tensor(name, shape, dt))

                ycp = sb("ycp", [P, KD, P])
                xs = sb("xs", [P, D])
                x2 = sb("x2", [P, D])
                y_copied, y_turned, xs_loaded, x2_made, x2_stored = (
                    sem("y_copied"), sem("y_turned"), sem("xs_loaded"), sem("x2_made"), sem("x2_stored"))
                with nc.Block() as block:
                    @block.sync
                    def _(sp):
                        def body(i):
                            wait(sp, x2_made, i)
                            sp.dma_start(xs[:], x_skip[ds(i * P, P), :]).then_inc(xs_loaded, 16)
                            sp.wait_ge(x2_made, i + 1)
                            sp.dma_start(x_mid[ds(i * P, P), :], x2[:]).then_inc(x2_stored, 16)
                        rounds(sp, TILES, body)
                        sp.wait_ge(x2_stored, 16 * TILES)

                    @block.scalar
                    def _(act):
                        def body(i):
                            wait(act, y_turned, i)
                            act.activation(ycp[:], xT[:, :, ds(i * P, P)], ACT.Copy).then_inc(y_copied, 1)
                        rounds(act, TILES, body)

                    @block.tensor
                    def _(pe):
                        def body(i):
                            pe.wait_ge(y_copied, i + 1)
                            wait(pe, x2_made, i)
                            for k in range(KD):
                                last = pe.transpose(bank[:, 0, k * P:(k + 1) * P], ycp[:, k, :], ident[:])
                            last.then_inc(y_turned, 1)
                        rounds(pe, TILES, body)

                    @block.vector
                    def _(dve):
                        def body(i):
                            dve.wait_ge(xs_loaded, 16 * (i + 1))
                            dve.wait_ge(y_turned, i + 1)
                            wait(dve, x2_stored, 16 * i)
                            dve.tensor_tensor(x2[:], xs[:], bank[:, 0, 0:D], ALU.add).then_inc(x2_made, 1)
                        rounds(dve, TILES, body)
                turn_part.close()
                end_phase()

        with ExitStack() as part:
            def sb(name, shape, dt=F32):
                return part.enter_context(nc.sbuf_tensor(name, shape, dt))

            weight = sb("weight", [P, TILES, TOPK])
            row_i = sb("row_i", [P, TILES, TOPK], I32)
            tile_expert = sb("tile_expert", [1, XT], I32)
            tile_no = sb("tile_no", [1, XT])
            tiles_to = sb("tiles_to", [P, E])

            choice_part = ExitStack()
            chosen = choice_part.enter_context(
                nc.sbuf_tensor("chosen", [P, TILES, TOPK, E], F32))
            route_part = ExitStack()

            def sb(name, shape, dt=F32):
                return route_part.enter_context(nc.sbuf_tensor(name, shape, dt))

            gate = sb("gate", [P, KD, E])
            x2 = [sb(f"x2{c}", [P, GT, D]) for c in range(4)]
            xn2 = [sb(f"xnb{s}", [P, GT, D]) for s in range(2)]
            xn2T = [sb(f"xnbT{s}", [P, GT, D]) for s in range(2)]
            stats = [sb(f"statsb{s}", [P, GT, 6]) for s in range(2)]
            meanvar = [sb(f"meanvarb{s}", [P, GT, 2]) for s in range(2)]
            rstd = [sb(f"rstdb{s}", [P, GT]) for s in range(2)]
            logit = [sb(f"logit{s}", [P, GT, E + 1]) for s in range(2)]
            best = [sb(f"best{s}", [P, GT, 8]) for s in range(2)]
            best_at = [sb(f"best_at{s}", [P, GT, 8], U32) for s in range(2)]
            all_logits = sb("all_logits", [P, TILES, E])
            all_best = sb("all_best", [P, TILES, TOPK])
            best_f = sb("best_f", [P, TILES, TOPK])
            shifted = sb("shifted", [P, TILES, E])
            ek = sb("ek", [P, TILES, TOPK])
            z_sum = sb("z_sum", [P, TILES])
            s_sum = sb("s_sum", [P, TILES])

            gate_loaded, pad_made = sem("gate_loaded"), sem("pad_made")
            (st_made, ag_made, ep_made, rs_made, xn2_made, xn2_turned, xn2T_made, logit_done,
             logit_copied, best_made, at_made) = [sem(n) for n in (
                 "st_made", "ag_made", "ep_made", "rs_made", "xn2_made", "xn2_turned", "xn2T_made",
                 "logit_done", "logit_copied", "best_made", "at_made")]
            x2_loaded, xn2_stored = sems("x2_loaded", 4), sems("xn2_stored")
            kept, r_step, shift_made, exp_made = sem("kept"), sem("r_step"), sem("shift_made"), sem("exp_made")

            with nc.Block() as block:
                @block.sync
                def _(sp):
                    sp.dma_start(gate[:], gate_t.rearrange("(k p) e -> p k e", p=P)).then_inc(gate_loaded, 16)

                    def store(g, s):
                        sp.wait_ge(xn2_made, g + 1)
                        sp.dma_start(group_rows(x_norm, g), xn2[s][:]).then_inc(xn2_stored[s], 16)

                    def body(it, c, g):
                        wait(sp, xn2_made, g - 3)
                        sp.dma_start(x2[c][:], group_rows(x_mid, g)).then_inc(x2_loaded[c], 16)
                        if not isinstance(g, int) or g > 1:
                            store(g - 2, c % 2)
                    steps(sp, GROUPS, body, 4)
                    for s in range(2):
                        store(GROUPS - 2 + s, s)
                        sp.wait_ge(xn2_stored[s], 8 * GROUPS)

                @block.gpsimd
                def _(pool):
                    def keep(g, s):
                        pool.wait_ge(at_made, g + 1)
                        settle(pool)
                        here = ds(g * GT, GT)
                        pool.tensor_copy(all_logits[:, here, :], logit[s][:, :, 0:E])
                        pool.tensor_copy(all_best[:, here, :], best[s][:, :, 0:TOPK])
                        pool.tensor_copy(best_f[:, here, :], best_at[s][:, :, 0:TOPK]).then_inc(kept, 1)

                    def pair(it):
                        for s in range(2):
                            g = it * 2 + s
                            pool.wait_ge(ag_made, g + 1)
                            wait(pool, xn2_made, g - 1)
                            settle(pool)
                            pool.tensor_scalar(rstd[s][:], meanvar[s][:, :, 1], EPS, None, ALU.add)\
                                .then_inc(ep_made, 1)
                            pool.wait_ge(ep_made, g + 1)
                            pool.tensor_tensor(rstd[s][:], rstd[s][:], minus_half[:].to_broadcast([P, GT]),
                                               ALU.pow).then_inc(rs_made, 1)
                            if not isinstance(g, int) or g > 2:
                                keep(g - 3, 1 - s)
                    pair(0)
                    pair(1)
                    with pool.Fori(2, GROUPS // 2) as it:
                        pair(it)
                    for g in range(GROUPS - 3, GROUPS):
                        keep(g, g % 2)

                @block.tensor
                def _(pe):
                    pe.wait_ge(gate_loaded, 16)

                    def logits(g, s):
                        pe.wait_ge(xn2T_made, g + 1)
                        wait(pe, logit_copied, g - 1)
                        for i in range(GT):
                            for k in range(KD):
                                last = pe.matmul(bank[:, 4 + s, i * E:(i + 1) * E],
                                                 xn2T[s][:, i, k * P:(k + 1) * P], gate[:, k, :],
                                                 start=(k == 0), stop=(k == KD - 1))
                        last.then_inc(logit_done, 1)

                    def pair(it):
                        for s in range(2):
                            g = it * 2 + s
                            pe.wait_ge(xn2_made, g + 1)
                            wait(pe, xn2T_made, g - 1)
                            for i in range(GT):
                                for k in range(KD):
                                    at = (i % 2) * D + k * P
                                    last = pe.transpose(bank[:, 2 * s + i // 2, at:at + P],
                                                        xn2[s][:, i, k * P:(k + 1) * P], ident[:])
                            last.then_inc(xn2_turned, 1)
                            if not isinstance(g, int) or g > 0:
                                logits(g - 1, 1 - s)
                    rounds(pe, GROUPS // 2, pair)
                    logits(GROUPS - 1, 1)

                @block.scalar
                def _(act):
                    act.preload_act_table_set("exp_and_others")

                    def pair(it):
                        for s in range(2):
                            g = it * 2 + s
                            act.wait_ge(xn2_turned, g + 1)
                            wait(act, logit_done, g - 1)
                            act.activation(xn2T[s][:], bank[:, 2 * s:2 * s + 2, :].rearrange("p b (i t) -> p (b i) t", t=D),
                                           ACT.Copy).then_inc(xn2T_made, 1)
                    rounds(act, GROUPS // 2, pair)
                    act.wait_ge(shift_made, 2)
                    act.activation(shifted[:], shifted[:], ACT.Exp).then_inc(exp_made, 1)
                    act.activation(ek[:], ek[:], ACT.Exp).then_inc(exp_made, 1)

                @block.vector
                def _(dve):
                    for s in range(2):
                        dve.memset(logit[s][:], -3.0e38).then_inc(pad_made, 1)
                    dve.wait_ge(pad_made, 2)

                    def measure(g, c):
                        s = c % 2
                        dve.wait_ge(x2_loaded[c], (g - c) * 4 + 16)
                        wait(dve, ag_made, g - 1)
                        settle(dve)
                        for i in range(GT):
                            dve.bn_stats(stats[s][:, i, :], x2[c][:, i, :]).then_inc(st_made, 1)
                        dve.wait_ge(st_made, GT * (g + 1))
                        wait(dve, rs_made, g - 1)
                        settle(dve)
                        for i in range(GT):
                            last = dve.bn_aggr(meanvar[s][:, i, :], stats[s][:, i, :])
                        last.then_inc(ag_made, 1)

                    def normalise(g, c):
                        s = c % 2
                        dve.wait_ge(rs_made, g + 1)
                        dve.wait_ge(ag_made, g + 1)
                        wait(dve, xn2_turned, g - 1)
                        if not isinstance(g, int) or g > 1:
                            dve.wait_ge(xn2_stored[s], (g - s) * 8)
                        for i in range(GT):
                            last = dve.tensor_scalar(xn2[s][:, i, :], x2[c][:, i, :], meanvar[s][:, i, 0:1],
                                                     rstd[s][:, i:i + 1], ALU.subtract, ALU.mult)
                        last.then_inc(xn2_made, 1)

                    def copy_logits(g, s):
                        dve.wait_ge(logit_done, g + 1)
                        wait(dve, at_made, g - 1)
                        wait(dve, kept, g - 1)
                        dve.tensor_copy(logit[s][:, :, 0:E],
                                        bank[:, 4 + s, 0:GT * E].rearrange("p (i e) -> p i e", e=E))\
                           .then_inc(logit_copied, 1)

                    def three_best(g, s):
                        dve.wait_ge(logit_copied, g + 1)
                        wait(dve, kept, g - 1)
                        settle(dve)
                        for i in range(GT):
                            dve.max(best[s][:, i, :], logit[s][:, i, :]).then_inc(best_made, 1)
                        dve.wait_ge(best_made, GT * (g + 1))
                        settle(dve)
                        for i in range(GT):
                            last = dve.max_index(best_at[s][:, i, :], best[s][:, i, :], logit[s][:, i, :])
                        last.then_inc(at_made, 1)

                    measure(0, 0)

                    def step(it, c, g):
                        s = c % 2
                        if not isinstance(g, int) or g + 1 < GROUPS:
                            measure(g + 1, (c + 1) % 4)
                        normalise(g, c)
                        if not isinstance(g, int) or g > 1:
                            copy_logits(g - 2, s)
                            three_best(g - 2, s)
                    steps(dve, GROUPS, step, 4)
                    copy_logits(GROUPS - 2, 0)
                    three_best(GROUPS - 2, 0)
                    copy_logits(GROUPS - 1, 1)
                    three_best(GROUPS - 1, 1)

                    n = [0]

                    def chain(ins):
                        ins.then_inc(r_step, 1)
                        n[0] += 1
                        dve.wait_ge(r_step, n[0])

                    dve.wait_ge(kept, GROUPS)
                    dve.tensor_tensor(shifted[:], all_logits[:], all_best[:, :, 0:1].to_broadcast([P, TILES, E]),
                                      ALU.subtract).then_inc(shift_made, 1)
                    dve.tensor_tensor(ek[:], all_best[:], all_best[:, :, 0:1].to_broadcast([P, TILES, TOPK]),
                                      ALU.subtract).then_inc(shift_made, 1)
                    chain(dve.tensor_tensor(
                        chosen[:], expert_no[:].unsqueeze(1).unsqueeze(2).to_broadcast([P, TILES, TOPK, E]),
                        best_f[:].unsqueeze(3).to_broadcast([P, TILES, TOPK, E]), ALU.is_equal))
                    dve.wait_ge(exp_made, 2)
                    chain(dve.tensor_reduce(z_sum[:], shifted[:], AX.X, ALU.add))
                    chain(dve.reciprocal(z_sum[:], z_sum[:]))
                    chain(dve.tensor_tensor(ek[:], ek[:], z_sum[:].unsqueeze(2).to_broadcast([P, TILES, TOPK]),
                                            ALU.mult))
                    chain(dve.tensor_reduce(s_sum[:], ek[:], AX.X, ALU.add))
                    chain(dve.tensor_scalar(s_sum[:], s_sum[:], 1e-20, None, ALU.add))
                    chain(dve.reciprocal(s_sum[:], s_sum[:]))
                    chain(dve.tensor_tensor(weight[:], ek[:], s_sum[:].unsqueeze(2).to_broadcast([P, TILES, TOPK]),
                                            ALU.mult))
            route_part.close()
            end_phase()

            rank_part = ExitStack()

            def sb(name, shape, dt=F32):
                return rank_part.enter_context(nc.sbuf_tensor(name, shape, dt))

            taken = sb("taken", [P, TILES, E])
            so_far = sb("so_far", [P, E, TILES])
            in_tile = sb("in_tile", [P, E, TILES])
            goes_on = sb("goes_on", [P, E, TILES])
            goes_on_made = sem("goes_on_made")
            row_f = sb("row_f", [P, TILES, E])
            one_row = sb("one_row", [P, TILES, E])
            picked = sb("picked", [P, TILES, TOPK])
            step_i = sb("step_i", [P, TILES], I32)
            step_f = sb("step_f", [P, TILES])
            over = sb("over", [P, E, TILES])
            n_tiles = sb("n_tiles", [P, E])
            base = sb("base", [P, E])
            tno_i = sb("tno_i", [1, XT], I32)
            unused_i = sb("unused_i", [P, XT], I32)
            unused = sb("unused", [P, XT])
            before = sb("before", [P, P])
            before_clear, before_made = sem("before_clear"), sem("before_made")
            r_pool, r_dve, r_pe, cleared = sem("r_pool"), sem("r_dve"), sem("r_pe"), sem("cleared")
            HT = TILES // 2
            with nc.Block() as block:
                @block.sync
                def _(sp):
                    sp.wait_ge(r_pool, 6)
                    sp.dma_start(row_choice.rearrange("(p j) o -> p (j o)", p=P), unused[:]).then_inc(cleared, 16)
                    sp.wait_ge(cleared, 16)

                @block.gpsimd
                def _(pool):
                    pool.memset(goes_on[:], 1.0).then_inc(goes_on_made, 1)
                    pool.memset(before[:], 1.0).then_inc(before_clear, 1)
                    pool.wait_ge(goes_on_made, 1)
                    pool.memset(goes_on[:, :, 0:1], 0.0).then_inc(goes_on_made, 1)
                    pool.wait_ge(before_clear, 1)
                    pool.affine_select(out=before[:], in_=before[:], compare_op=ALU.is_gt, fill=0.0,
                                       base=0, pattern=[[1, P]], channel_multiplier=-1).then_inc(before_made, 1)
                    pool.iota(step_i[:], pattern=[[P, TILES]], base=0, channel_multiplier=0).then_inc(r_pool, 1)
                    pool.iota(tno_i[:], pattern=[[1, XT]], base=0, channel_multiplier=0).then_inc(r_pool, 1)
                    pool.iota(unused_i[:], pattern=[[1, XT]], base=SLOTS * TOK, channel_multiplier=XT).then_inc(r_pool, 1)
                    pool.wait_ge(r_pool, 3)
                    pool.tensor_copy(step_f[:], step_i[:]).then_inc(r_pool, 1)
                    pool.tensor_copy(tile_no[:], tno_i[:]).then_inc(r_pool, 1)
                    pool.tensor_copy(unused[:], unused_i[:]).then_inc(r_pool, 1)

                @block.tensor
                def _(pe):
                    pe.wait_ge(before_made, 1)
                    pe.wait_ge(r_dve, 2)
                    for hf in range(2):
                        m = taken[:, hf * HT:(hf + 1) * HT, :].rearrange("p i e -> p (i e)")
                        pe.matmul(bank[:, hf, 0:HT * E], before[:], m, start=True, stop=True)
                        last = pe.matmul(bank[:, 2 + hf, 0:HT * E], ones[:], m, start=True, stop=True)
                    last.then_inc(r_pe, 1)

                @block.vector
                def _(dve):
                    n = [0]

                    def chain(ins):
                        ins.then_inc(r_dve, 1)
                        n[0] += 1
                        dve.wait_ge(r_dve, n[0])

                    chain(dve.tensor_tensor(taken[:], chosen[:, :, 0, :], chosen[:, :, 1, :], ALU.add))
                    chain(dve.tensor_tensor(taken[:], taken[:], chosen[:, :, 2, :], ALU.add))
                    dve.wait_ge(r_pe, 1)
                    for hf in range(2):
                        chain(dve.tensor_copy(in_tile[:, :, hf * HT:(hf + 1) * HT],
                                              bank[:, 2 + hf, 0:HT * E].rearrange("p (i e) -> p e i", e=E)))
                    dve.wait_ge(goes_on_made, 2)
                    chain(dve.tensor_tensor_scan(so_far[:].rearrange("p e i -> p (e i)"),
                                                 goes_on[:].rearrange("p e i -> p (e i)"),
                                                 in_tile[:].rearrange("p e i -> p (e i)"), 0.0, ALU.mult, ALU.add))
                    dve.wait_ge(r_pool, 5)
                    chain(dve.tensor_tensor(over[:], so_far[:, :, TILES - 1:TILES].to_broadcast([P, E, TILES]),
                                            step_f[:].unsqueeze(1).to_broadcast([P, E, TILES]), ALU.is_gt))
                    chain(dve.tensor_reduce(n_tiles[:], over[:], AX.X, ALU.add))
                    chain(dve.tensor_tensor_scan(tiles_to[:], ones[:, 0:E], n_tiles[:], 0.0, ALU.mult, ALU.add))
                    chain(dve.tensor_tensor(base[:], tiles_to[:], n_tiles[:], ALU.subtract))
                    chain(dve.tensor_scalar(base[:], base[:], float(P), None, ALU.mult))
                    for hf in range(2):
                        i0 = hf * HT
                        r = row_f[:, i0:i0 + HT, :]
                        chain(dve.tensor_tensor(r, so_far[:, :, i0:i0 + HT].rearrange("p e i -> p i e"),
                                                bank[:, 2 + hf, 0:HT * E].rearrange("p (i e) -> p i e", e=E),
                                                ALU.subtract))
                        chain(dve.tensor_tensor(r, r, bank[:, hf, 0:HT * E].rearrange("p (i e) -> p i e", e=E),
                                                ALU.add))
                    chain(dve.tensor_tensor(row_f[:], row_f[:], base[:].unsqueeze(1).to_broadcast([P, TILES, E]),
                                            ALU.add))
                    for k in range(TOPK):
                        chain(dve.tensor_tensor(one_row[:], row_f[:], chosen[:, :, k, :], ALU.mult))
                        chain(dve.tensor_reduce(picked[:, :, k], one_row[:], AX.X, ALU.add))
                    chain(dve.tensor_copy(row_i[:], picked[:]))
            rank_part.close()
            choice_part.close()
            end_phase()

            def sb(name, shape, dt=F32):
                return part.enter_context(nc.sbuf_tensor(name, shape, dt))

            b2 = sb("b2", [P, E * D])
            shared_weights = (sb("sw1", [P, KD, 2 * FS]), sb("sb1", [P, 2 * KS]), sb("sw2", [P, KS, D]),
                              sb("sb2", [P, D]))

            shared_part = ExitStack()

            def sb(name, shape, dt=F32):
                return shared_part.enter_context(nc.sbuf_tensor(name, shape, dt))

            sh = shared_expert(sb, shared_weights, 0, G1, x_mid)
            sw1, sb1, sw2, sb2 = shared_weights
            smul = sb("smul", [P, KS])
            exp_f = sb("exp_f", [1, XT])
            expert_step = sem("expert_step")
            s_loaded, s_scaled = sem("s_loaded"), sem("s_scaled")
            wmul = sb("wmul", [P, KD, E])
            to_row = [sb(f"to_row{c}", [P, TOPK], I32) for c in range(4)]
            choice = [sb(f"choice{c}", [P, TOPK]) for c in range(4)]
            choice_i = sb("choice_i", [P, TILES, TOPK], I32)
            choice_all = sb("choice_all", [P, TILES, TOPK])
            c_made, c_copied, c_sent = sem("c_made"), sem("c_copied"), sems("c_sent", 4)
            w_loaded, w_scaled = sem("w_loaded"), sem("w_scaled")
            LOADS = max(n for n in range(1, G1) if E * D % n == 0)
            W1P, W2P = E * 2 * F // LOADS, E * D // LOADS
            assert (G1 - 1) // 2 * 2 <= LOADS
            with nc.Block() as block:
                @block.sync
                def _(sp):
                    sh.load_xa(sp, 0, 0)
                    sp.dma_start(sw1[:], s_fc1_t.rearrange("(k p) f -> p k f", p=P)).then_inc(s_loaded, 16)
                    with nc.allow_non_contiguous_dma(reason="small constants, once"):
                        sp.dma_start(sb1[:], s_fc1_b.rearrange("(k p) -> p k", p=P)).then_inc(s_loaded, 16)
                        sp.dma_start(smul[:], s_mult.rearrange("(k p) -> p k", p=P)).then_inc(s_loaded, 16)
                    sp.dma_start(sw2[:], s_fc2_t.rearrange("(k p) f -> p k f", p=P)).then_inc(s_loaded, 16)
                    sp.dma_start(sb2[:], s_fc2_b.partition_broadcast(P)).then_inc(s_loaded, 16)

                    def body(j, s):
                        sh.move(sp, j, s)
                    pairwise(sp, G1, body)
                    sh.move_last(sp)

                @block.gpsimd
                def _(pool):
                    pool.iota(choice_i[:], pattern=[[SLOTS * P, TILES], [1, TOPK]], base=0, channel_multiplier=SLOTS)\
                        .then_inc(c_made, 1)
                    pool.wait_ge(c_made, 1)
                    pool.tensor_copy(choice_all[:], choice_i[:]).then_inc(c_made, 1)
                    pool.wait_ge(c_made, 2)

                    def copy_rows(it, c, t):
                        wait(pool, c_sent[c], 48 * it)
                        pool.tensor_copy(to_row[c][:], row_i[:, ds(t, 1), :].rearrange("p o k -> p (o k)"))
                        pool.tensor_copy(choice[c][:], choice_all[:, ds(t, 1), :].rearrange("p o k -> p (o k)"))\
                            .then_inc(c_copied, 1)

                    def step(it, c, t):
                        if not isinstance(t, int) or t + 1 < TILES:
                            copy_rows(it + (c + 1) // 4, (c + 1) % 4, t + 1)
                        pool.wait_ge(c_copied, t + 1)
                        settle(pool)
                        for k in range(TOPK):
                            pool.indirect_dma_start(
                                out=row_choice, out_offset=bass.IndirectOffsetOnAxis(ap=to_row[c][:, k:k + 1], axis=0),
                                in_=choice[c][:, k:k + 1], in_offset=None).then_inc(c_sent[c], 16)
                    copy_rows(0, 0, 0)
                    steps(pool, TILES, step, 4)
                    for c in range(4):
                        pool.wait_ge(c_sent[c], 48 * (TILES // 4))

                @block.tensor
                def _(pe):
                    def weights_ready():
                        pe.wait_ge(s_loaded, 80)
                        pe.wait_ge(s_scaled, 1)
                    sh.products(pe, weights_ready)

                @block.scalar
                def _(act):
                    act.preload_act_table_set("gelu_and_others")
                    w1_rows = fc1_t.rearrange("(k p) e f -> p k (e f)", p=P)
                    w2_rows = fc2_t.rearrange("(k p) e d -> p k (e d)", p=P)
                    b1_row, b2_row = fc1_b.rearrange("e f -> (e f)"), fc2_b.rearrange("e d -> (e d)")

                    def load_part(j):
                        at1, at2 = ds(j * W1P, W1P), ds(j * W2P, W2P)
                        act.dma_start(w1[:, :, at1], w1_rows[:, :, at1]).then_inc(w_loaded, 16)
                        act.dma_start(w2[:, :, at2], w2_rows[:, :, at2]).then_inc(w_loaded, 16)
                        act.dma_start(b1[:, at1], b1_row[at1].partition_broadcast(P)).then_inc(w_loaded, 16)
                        act.dma_start(b2[:, at2], b2_row[at2].partition_broadcast(P)).then_inc(w_loaded, 16)

                    sh.copy_xT(act, 0, 0)
                    act.wait_ge(s_loaded, 80)
                    act.dma_start(wmul[:], mult_t.rearrange("(k p) e -> p k e", p=P)).then_inc(w_loaded, 16)

                    def body(j, s):
                        if not isinstance(j, int) or j + 1 < G1:
                            sh.copy_xT(act, j + 1, 1 - s)
                        if not isinstance(j, int) or j < LOADS:
                            load_part(j)
                        sh.gelus(act, j, s)
                    pairwise(act, G1, body)
                    act.wait_ge(w_loaded, (4 * LOADS + 1) * 16)

                @block.vector
                def _(dve):
                    for e in range(E):
                        if e == 0:
                            past = dve.tensor_scalar(exp_f[:], tile_no[:], tiles_to[0:1, 0:1], None, ALU.is_ge)
                        else:
                            past = dve.scalar_tensor_tensor(exp_f[:], tile_no[:], tiles_to[0:1, e:e + 1], exp_f[:],
                                                            ALU.is_ge, ALU.add)
                        past.then_inc(expert_step, 1)
                        dve.wait_ge(expert_step, e + 1)
                    dve.tensor_scalar(exp_f[:], exp_f[:], float(E - 1), None, ALU.min).then_inc(expert_step, 1)
                    dve.wait_ge(expert_step, E + 1)
                    dve.tensor_copy(tile_expert[:], exp_f[:]).then_inc(expert_step, 1)
                    dve.wait_ge(s_loaded, 80)
                    dve.tensor_tensor(sw2[:], sw2[:], smul[:].unsqueeze(2).to_broadcast([P, KS, D]), ALU.mult)\
                       .then_inc(s_scaled, 1)

                    def body(j, s):
                        sh.glus(dve, j, s)
                        if not isinstance(j, int) or j > 0:
                            sh.add_out(dve, j - 1, 1 - s)
                    pairwise(dve, G1, body)
                    dve.wait_ge(w_loaded, (4 * LOADS + 1) * 16)
                    for k in range(KD):
                        rows_k = w2[:, k, :].rearrange("p (e d) -> p e d", e=E)
                        dve.tensor_tensor(rows_k, rows_k, wmul[:, k, :].unsqueeze(2).to_broadcast([P, E, D]),
                                          ALU.mult).then_inc(w_scaled, 1)
                    sh.add_out(dve, G1 - 1, (G1 - 1) % 2)
            shared_part.close()
            end_phase()

            exp_part = ExitStack()

            def sb(name, shape, dt=F32):
                return exp_part.enter_context(nc.sbuf_tensor(name, shape, dt))

            NB4 = 8
            TR = NB4 // 2
            row_ids = sb("row_ids", [XT // 2, 2, P])
            ids = sb("ids", [P, 2, XT // 2], I32)
            tokens = sb("tokens", [P, 2, XT // 2], I32)
            rt = [sb(f"rt{c}", [P, 1], I32) for c in range(NB4)]
            to_slot = [sb(f"to_slot{c}", [P, 1], I32) for c in range(NB4)]
            xg = [sb(f"xg{c}", [P, D]) for c in range(NB4)]
            xgT = [sb(f"xgT{s}", [P, KD, P]) for s in range(2)]
            hid = [sb(f"hid{s}", [P, 2 * F]) for s in range(2)]
            act_g = [sb(f"act_g{s}", [P, F]) for s in range(2)]
            glu = [sb(f"glu{s}", [P, F]) for s in range(2)]
            gluT = [sb(f"gluT{s}", [P, F // P, P]) for s in range(2)]
            ye = [sb(f"ye{c}", [P, D]) for c in range(NB4)]
            ids_loaded, ids_turned, ids_made = sem("ids_loaded"), sem("ids_turned"), sem("ids_made")
            rt_made, slot_made = sem("rt_made"), sem("slot_made")
            xg_loaded, ye_stored = sems("xg_loaded", NB4), sems("ye_stored", NB4)
            (xg_turned, xgT_made, h_done, hid_made, gelu_made, glu_made, glu_turned, gluT_made, y_done,
             ye_made) = [sem(n) for n in ("xg_turned", "xgT_made", "h_done", "hid_made", "gelu_made", "glu_made",
                                          "glu_turned", "gluT_made", "ye_done", "ye_made")]
            with nc.Block() as block:
                @block.sync
                def _(sp):
                    sp.dma_start(row_ids[:], row_choice.rearrange("(q s p) o -> q s (p o)", s=2, p=P)).then_inc(ids_loaded, 16)
                    sp.wait_ge(ids_loaded, 16)

                @block.gpsimd
                def _(pool):
                    pool.wait_ge(ids_made, 3)

                    def gather(it, c, j):
                        wait(pool, xg_loaded[c], 16 * it)
                        pool.tensor_copy(rt[c][:], tokens[:, c % 2, ds(it * TR + c // 2, 1)]).then_inc(rt_made, 1)
                        pool.wait_ge(rt_made, j + 1)
                        wait(pool, xg_turned, j - NB4 + 1)
                        settle(pool)
                        pool.indirect_dma_start(
                            out=xg[c][:], out_offset=None, in_=x_norm,
                            in_offset=bass.IndirectOffsetOnAxis(ap=rt[c][:, 0:1], axis=0)).then_inc(xg_loaded[c], 16)

                    def scatter(it, c, j):
                        wait(pool, ye_stored[c], 16 * it)
                        pool.tensor_copy(to_slot[c][:], ids[:, c % 2, ds(it * TR + c // 2, 1)]).then_inc(slot_made, 1)
                        pool.wait_ge(slot_made, j + 1)
                        pool.wait_ge(ye_made, j + 1)
                        settle(pool)
                        pool.indirect_dma_start(
                            out=choice_out, out_offset=bass.IndirectOffsetOnAxis(ap=to_slot[c][:, 0:1], axis=0),
                            in_=ye[c][:], in_offset=None).then_inc(ye_stored[c], 16)

                    AHEAD = NB4 - 2
                    for c in range(AHEAD):
                        gather(0, c, c)

                    def step(it, c, j):
                        if not isinstance(j, int) or j + AHEAD < XT:
                            gather(it + (c + AHEAD) // NB4, (c + AHEAD) % NB4, j + AHEAD)
                        if not isinstance(j, int) or j > 0:
                            scatter(it if c else it - 1, (c - 1) % NB4, j - 1)
                    steps(pool, XT, step, NB4)
                    scatter(XT // NB4 - 1, NB4 - 1, XT - 1)
                    for c in range(NB4):
                        pool.wait_ge(ye_stored[c], 16 * (XT // NB4))

                @block.tensor
                def _(pe):
                    pe.wait_ge(ids_loaded, 16)
                    for s in range(2):
                        last = pe.transpose(bank[:, s, 0:XT // 2], row_ids[:, s, :], ident[0:XT // 2, 0:XT // 2])
                    last.then_inc(ids_turned, 1)
                    pe.wait_ge(ids_made, 1)

                    def turn_x(c, it, j):
                        s = c % 2
                        pe.wait_ge(xg_loaded[c % NB4], 16 * (it + 1))
                        wait(pe, xgT_made, j - 1)
                        for k in range(KD):
                            last = pe.transpose(bank[:, s, k * P:(k + 1) * P], xg[c % NB4][:, k * P:(k + 1) * P], ident[:])
                        last.then_inc(xg_turned, 1)

                    def fc1(c, j):
                        s = c % 2
                        e_no = pe.value_load(tile_expert[0:1, ds(j, 1)], min_val=0, max_val=E - 1)
                        pe.wait_ge(xgT_made, j + 1)
                        wait(pe, hid_made, j - 1)
                        for k in range(KD):
                            last = pe.matmul(bank[:, 2 + s, :], xgT[s][:, k, :], w1[:, k, ds(e_no * (2 * F), 2 * F)],
                                             start=(k == 0), stop=(k == KD - 1))
                        last.then_inc(h_done, 1)

                    def turn_glu(c, j):
                        s = c % 2
                        pe.wait_ge(glu_made, j + 1)
                        wait(pe, gluT_made, j - 1)
                        for k in range(F // P):
                            last = pe.transpose(bank[:, 4 + s, k * P:(k + 1) * P], glu[s][:, k * P:(k + 1) * P], ident[:])
                        last.then_inc(glu_turned, 1)

                    def fc2(c, j):
                        s = c % 2
                        e_no = pe.value_load(tile_expert[0:1, ds(j, 1)], min_val=0, max_val=E - 1)
                        pe.wait_ge(gluT_made, j + 1)
                        wait(pe, ye_made, j - 1)
                        for k in range(F // P):
                            last = pe.matmul(bank[:, 6 + s, 0:D], gluT[s][:, k, :], w2[:, k, ds(e_no * D, D)],
                                             start=(k == 0), stop=(k == F // P - 1))
                        last.then_inc(y_done, 1)

                    turn_x(0, 0, 0)
                    turn_x(1, 0, 1)
                    fc1(0, 0)

                    def step(it, c, j):
                        if not isinstance(j, int) or j + 2 < XT:
                            turn_x(c + 2, it + (c + 2) // NB4, j + 2)
                        if not isinstance(j, int) or j + 1 < XT:
                            fc1(c + 1, j + 1)
                        turn_glu(c, j)
                        if not isinstance(j, int) or j > 0:
                            fc2(c + 1, j - 1)
                    steps(pe, XT, step, NB4)
                    fc2(1, XT - 1)

                @block.scalar
                def _(act):
                    act.preload_act_table_set("gelu_and_others")

                    def xT_copy(c, j):
                        s = c % 2
                        act.wait_ge(xg_turned, j + 1)
                        wait(act, h_done, j - 1)
                        act.activation(xgT[s][:], bank[:, s, 0:D].rearrange("p (k t) -> p k t", k=KD), ACT.Copy)\
                           .then_inc(xgT_made, 1)

                    def gelu(c, j):
                        s = c % 2
                        act.wait_ge(hid_made, j + 1)
                        wait(act, glu_made, j - 1)
                        act.activation(act_g[s][:], hid[s][:, F:2 * F], ACT.Gelu).then_inc(gelu_made, 1)

                    xT_copy(0, 0)
                    xT_copy(1, 1)
                    gelu(0, 0)

                    def step(it, c, j):
                        s = c % 2
                        if not isinstance(j, int) or j + 2 < XT:
                            xT_copy(c, j + 2)
                        act.wait_ge(glu_turned, j + 1)
                        wait(act, y_done, j - 1)
                        act.activation(gluT[s][:], bank[:, 4 + s, 0:F].rearrange("p (k t) -> p k t", t=P), ACT.Copy)\
                           .then_inc(gluT_made, 1)
                        if not isinstance(j, int) or j + 1 < XT:
                            gelu(c + 1, j + 1)
                    steps(act, XT, step, NB4)

                @block.vector
                def _(dve):
                    dve.wait_ge(ids_turned, 1)
                    dve.tensor_copy(ids[:], bank[:, 0:2, 0:XT // 2]).then_inc(ids_made, 1)
                    dve.wait_ge(ids_made, 1)
                    dve.tensor_scalar(tokens[:], ids[:], SLOTS_LOG, None, ALU.logical_shift_right).then_inc(ids_made, 1)
                    dve.wait_ge(ids_made, 2)
                    dve.tensor_scalar(tokens[:], tokens[:], TOK - 1, None, ALU.min).then_inc(ids_made, 1)

                    def add_bias(c, j):
                        s = c % 2
                        e_no = dve.value_load(tile_expert[0:1, ds(j, 1)], min_val=0, max_val=E - 1)
                        dve.wait_ge(h_done, j + 1)
                        wait(dve, glu_made, j - 1)
                        dve.tensor_tensor(hid[s][:], bank[:, 2 + s, :], b1[:, ds(e_no * (2 * F), 2 * F)],
                                          ALU.add).then_inc(hid_made, 1)

                    def gate_glu(c, j):
                        s = c % 2
                        dve.wait_ge(gelu_made, j + 1)
                        dve.wait_ge(hid_made, j + 1)
                        wait(dve, glu_turned, j - 1)
                        dve.tensor_tensor(glu[s][:], hid[s][:, 0:F], act_g[s][:], ALU.mult).then_inc(glu_made, 1)

                    def take_y(c, it, j):
                        e_no = dve.value_load(tile_expert[0:1, ds(j, 1)], min_val=0, max_val=E - 1)
                        dve.wait_ge(y_done, j + 1)
                        wait(dve, ye_stored[c % NB4], 16 * it)
                        dve.tensor_tensor(ye[c % NB4][:], bank[:, 6 + c % 2, 0:D], b2[:, ds(e_no * D, D)], ALU.add)\
                           .then_inc(ye_made, 1)

                    add_bias(0, 0)
                    gate_glu(0, 0)

                    def step(it, c, j):
                        if not isinstance(j, int) or j + 1 < XT:
                            add_bias(c + 1, j + 1)
                        if not isinstance(j, int) or j > 0:
                            take_y(c + NB4 - 1, it if c else it - 1, j - 1)
                        if not isinstance(j, int) or j + 1 < XT:
                            gate_glu(c + 1, j + 1)
                    steps(dve, XT, step, NB4)
                    take_y(NB4 - 1, XT // NB4 - 1, XT - 1)
            exp_part.close()
            end_phase()

            def sb(name, shape, dt=F32):
                return part.enter_context(nc.sbuf_tensor(name, shape, dt))

            G2 = GROUPS - G1
            assert G1 == 2 * (G2 - 1)
            order = [0, 1, 2]
            for j in range(2, G2 - 1):
                order += [2 * j - 1, G1 + j - 2, 2 * j]
            order += [G1 - 1, G1 + G2 - 3, G1 + G2 - 2, G1 + G2 - 1]
            assert sorted(order) == list(range(GROUPS))
            RING = 4
            Y3, TT = GT * TOPK * D, GT * D
            y3 = [arena_x[:, c * Y3:(c + 1) * Y3].rearrange("p (i d) -> p i d", i=GT) for c in range(RING)]
            total = [arena_dt[:, c * TT:(c + 1) * TT].rearrange("p (i d) -> p i d", i=GT) for c in range(RING)]
            y3_loaded, total_loaded, stored = sems("y3_loaded", RING), sems("total_loaded", RING), sems("stored", RING)
            summed = [sem(f"summed{k}") for k in range(TOPK)]

            def place(g):
                return order.index(g)

            def summed_up(eng, j):
                eng.wait_ge(summed[TOPK - 1], GT * (place(G1 + j) + 1))

            sh = shared_expert(sb, shared_weights, G1, G2, out_rows, summed_up)
            with nc.Block() as block:
                @block.sync
                def _(sp):
                    def load(q):
                        g, c = order[q], q % RING
                        wait(sp, summed[TOPK - 1], GT * (q - RING + 1))
                        for i in range(GT):
                            t = g * GT + i
                            choices = choice_out[t * P * SLOTS:(t + 1) * P * SLOTS, :]
                            sp.dma_start(y3[c][:, i, :],
                                         choices.rearrange("(p k) d -> p (k d)", k=SLOTS)[:, 0:TOPK * D])\
                              .then_inc(y3_loaded[c], 16)
                        if g < G1:
                            wait(sp, stored[g % RING], 16 * (g // RING))
                            sp.dma_start(total[g % RING], group_rows(x_mid, g)).then_inc(total_loaded[g % RING], 16)

                    def store(g):
                        sp.wait_ge(summed[TOPK - 1], GT * (place(g) + 1))
                        sp.dma_start(group_rows(out_rows, g), total[g % RING]).then_inc(stored[g % RING], 16)

                    for q in range(GROUPS):
                        if q >= RING and order[q - RING] < G1:
                            store(order[q - RING])
                        load(q)
                    for q in range(GROUPS - RING, GROUPS):
                        if order[q] < G1:
                            store(order[q])
                    for c in range(RING):
                        sp.wait_ge(stored[c], 16 * len(range(c, G1, RING)))

                @block.gpsimd
                def _(pool):
                    for j in range(2):
                        sh.load_xm(pool, j, j)
                    for j in range(2, G2):
                        sh.store(pool, j - 2, j % 2)
                        sh.load_xm(pool, j, j % 2)
                    sh.move_last(pool)

                @block.tensor
                def _(pe):
                    sh.products(pe, lambda: None)

                @block.scalar
                def _(act):
                    sh.load_xa(act, 0, 0)
                    sh.load_xa(act, 1, 1)
                    act.preload_act_table_set("gelu_and_others")
                    sh.copy_xT(act, 0, 0)

                    def body(j, s):
                        if not isinstance(j, int) or j + 2 < G2:
                            sh.load_xa(act, j + 2, s)
                        if not isinstance(j, int) or j + 1 < G2:
                            sh.copy_xT(act, j + 1, 1 - s)
                        sh.gelus(act, j, s)
                    pairwise(act, G2, body)

                @block.vector
                def _(dve):
                    def add_choices(places):
                        for u in places:
                            if u % GT == 0:
                                q = u // GT
                                g = order[q]
                                dve.wait_ge(y3_loaded[q % RING], 16 * GT * (q // RING + 1))
                                if g < G1:
                                    dve.wait_ge(total_loaded[g % RING], 16 * (g // RING + 1))
                                else:
                                    dve.wait_ge(sh.acc_made, 2 * (g - G1 + 1))
                        for k in range(TOPK):
                            if k:
                                dve.wait_ge(summed[k - 1], places[-1] + 1)
                            for u in places:
                                q, i = u // GT, u % GT
                                g = order[q]
                                onto = total[g % RING] if g < G1 else sh.xm[(g - G1) % 2][:]
                                dve.scalar_tensor_tensor(
                                    onto[:, i, :], y3[q % RING][:, i, k * D:(k + 1) * D],
                                    weight[:, g * GT + i, k:k + 1], onto[:, i, :], ALU.mult, ALU.add)\
                                   .then_inc(summed[k], 1)

                    def upto(done, end):
                        while done < end:
                            n = min(2 if end - done <= 2 else GT, end - done)
                            add_choices(range(done, done + n))
                            done += n
                        return done

                    done = 0
                    for j in range(G2):
                        end = GT if j == 0 else 3 * GT if j == 1 else 3 * GT * j if j < G2 - 1 else TILES - 2 * GT
                        for i in range(KS):
                            sh.glu_part(dve, j, j % 2, i)
                            if j > 0 and i < 2:
                                done = upto(done, done + 2)
                            if j > 1 and i == 2:
                                sh.add_out(dve, j - 2, j % 2)
                        done = upto(done, end)
                    for j in (G2 - 2, G2 - 1):
                        sh.add_out(dve, j, j % 2)
                        done = upto(done, done + GT)


def kernel(**inputs):
    import numpy as np
    import concourse.bacc as bacc
    from concourse import mybir as _mybir
    from concourse.bass_utils import run_bass_kernel_spmd

    a = {k: np.asarray(v) for k, v in inputs.items()}
    laid = {
        "x": a["L0_attn_x"],
        "W_dt_t": a["L0_attn_W_dt"].T,
        "b_dt": a["L0_attn_b_dt"],
        "W_bc_t": np.concatenate([a["L0_attn_W_B"], a["L0_attn_W_C"]], axis=0).T,
        "A_log": a["L0_attn_A_log"],
        "D_param": a["L0_attn_D_param"],
        "gate_t": a["L0_ffn_gate_w"].T,
        "fc1_t": a["L0_ffn_fc1_w"].transpose(2, 0, 1),
        "fc1_b": a["L0_ffn_fc1_b"],
        "mult_t": a["L0_ffn_geglu_mult"].T,
        "fc2_t": a["L0_ffn_fc2_w"].transpose(2, 0, 1),
        "fc2_b": a["L0_ffn_fc2_b"],
        "s_fc1_t": a["L0_ffn_s_fc1_w"].T,
        "s_fc1_b": a["L0_ffn_s_fc1_b"],
        "s_mult": a["L0_ffn_s_geglu_mult"],
        "s_fc2_t": a["L0_ffn_s_fc2_w"].T,
        "s_fc2_b": a["L0_ffn_s_fc2_b"],
    }
    nc = bacc.Bacc("TRN2", target_bir_lowering=False, num_devices=1)
    arrays, args = {}, {}
    for name, value in laid.items():
        value = np.ascontiguousarray(value)
        arrays["in_" + name] = value
        args[name] = nc.dram_tensor("in_" + name, value.shape, _mybir.dt.from_np(value.dtype), kind="ExternalInput").ap()
    shape = a["L0_attn_x"].shape
    args["out"] = nc.dram_tensor("out_0", shape, _mybir.dt.float32, kind="ExternalOutput").ap()
    model_kernel(nc, **args)
    r = run_bass_kernel_spmd(nc, [arrays], core_ids=[0])
    return r.results[0]["out_0"]
```
